# Optimizing a Trainium2 kernel written in Bass

```python
import numpy as np
import jax
import jax.numpy as jnp

def _softmax(x, axis=-1):
    return jax.nn.softmax(x, axis=axis)

def _gelu(x):
    return jax.nn.gelu(x, approximate=True)

def _silu(x):
    return jax.nn.silu(x)

def _sigmoid(x):
    return jax.nn.sigmoid(x)

def _layernorm(x, axis=-1, eps=1e-05):
    m = jnp.mean(x, axis=axis, keepdims=True)
    v = jnp.var(x, axis=axis, keepdims=True)
    return (x - m) / jnp.sqrt(v + eps)

def _scatter_add(tgt, idx, src, axis=0):
    return tgt.at[idx].add(src)

def _segment_sum(src, seg, n):
    return jax.ops.segment_sum(src, seg, n)
kernel_name = 'mk_gps_d1_gnn_r32_c95ee0'

def setup_inputs(seed: int=0):
    np.random.seed(seed)
    _w = jnp.asarray

    def _rec_inputs():
        import jax
        import jax.numpy as jnp
        _gk = jax.random.key(seed)
        x = -8.776e-05 + 1 * jax.random.normal(jax.random.fold_in(_gk, 1), (625, 256), jnp.float32)
        src = jax.random.randint(jax.random.fold_in(_gk, 2), (20000,), 0, 625, jnp.int32)
        dst = jax.random.randint(jax.random.fold_in(_gk, 3), (20000,), 0, 625, jnp.int32)
        _o = jnp.argsort(dst, stable=True)
        src = src[_o]
        dst = dst[_o]
        return (x, src, dst)
    x, src, dst = _rec_inputs()

    def _L0_gnn_setup():
        import jax, jax.numpy as jnp
        import numpy as np
        N = 625
        E = 10000
        IN = 256
        H = 4
        C = 64
        D = H * C
        LN_EPS = 1e-05
        key = jax.random.key(seed)
        ks = jax.random.split(key, 8)
        w = lambda k, sh: jax.random.normal(k, sh, jnp.float32) * 0.05
        return {'x': jax.random.normal(ks[0], (N, IN), jnp.float32), 'edge_index': jax.random.randint(ks[1], (2, E), 0, N, dtype=jnp.int32), 'Wq': w(ks[2], (IN, D)), 'bq': jnp.zeros((D,), jnp.float32), 'Wk': w(ks[3], (IN, D)), 'bk': jnp.zeros((D,), jnp.float32), 'Wv': w(ks[4], (IN, D)), 'bv': jnp.zeros((D,), jnp.float32), 'Wskip': w(ks[5], (IN, D)), 'bskip': jnp.zeros((D,), jnp.float32), 'gamma': jnp.ones((D,), jnp.float32), 'beta_ln': jnp.zeros((D,), jnp.float32)}
    _L0_gnn_all = _L0_gnn_setup()
    _L0_gnn_in = {k: v for k, v in _L0_gnn_all.items() if k in ('Wq', 'bq', 'Wk', 'bk', 'Wv', 'bv', 'Wskip', 'bskip', 'gamma', 'beta_ln')}
    del _L0_gnn_all

    def _L0_mix_setup():
        import jax, jax.numpy as jnp
        import numpy as np
        HEADS, DIM_HEAD = (8, 64)
        EPS = 1e-05

        def instance_norm(t):
            mu = jnp.mean(t, axis=-1, keepdims=True)
            var = jnp.mean((t - mu) ** 2, axis=-1, keepdims=True)
            return (t - mu) * jax.lax.rsqrt(var + EPS)
        key = jax.random.key(seed)
        k1, k2, k3, k4 = jax.random.split(key, 4)
        B, N, D = (8, 256, 256)
        inner = HEADS * DIM_HEAD
        x = jax.random.normal(k1, (B, N, D), jnp.float32)
        w_qkv = jax.random.normal(k2, (3 * inner, D), jnp.float32) / np.sqrt(D).astype(np.float32)
        w_out = jax.random.normal(k3, (D, inner), jnp.float32) / np.sqrt(inner).astype(np.float32)
        b_out = 0.01 * jax.random.normal(k4, (D,), jnp.float32)
        return {'x': x, 'w_qkv': w_qkv, 'w_out': w_out, 'b_out': b_out}
    _L0_mix_all = _L0_mix_setup()
    _L0_mix_in = {k: v for k, v in _L0_mix_all.items() if k in ('w_qkv', 'w_out', 'b_out')}
    del _L0_mix_all

    def _L0_ffn_setup():
        import jax, jax.numpy as jnp
        import numpy as np
        B, T, C = (64, 384, 256)
        NH, NKV = (4, 2)
        HD = C // NH
        NREP = NH // NKV
        NE, TOPK = (8, 2)
        HID = int(8 / 3 * C)
        EPS_RMS = 1e-06

        def _rope_tables(t_len):
            inv_freq = 1.0 / 10000.0 ** (np.arange(0, HD, 2, dtype=np.float32) / HD)
            t = np.arange(t_len, dtype=np.float32)
            freqs = np.outer(t, inv_freq)
            emb = np.concatenate([freqs, freqs], axis=-1)
            return (jnp.asarray(np.cos(emb)), jnp.asarray(np.sin(emb)))

        def _rotate_half(x):
            h = x.shape[-1] // 2
            return jnp.concatenate([-x[..., h:], x[..., :h]], axis=-1)

        def _rmsnorm(v, w):
            return v * jax.lax.rsqrt(jnp.mean(v * v, axis=-1, keepdims=True) + EPS_RMS) * w
        key = jax.random.key(seed)
        ks = jax.random.split(key, 10)
        s = lambda k, shape: jax.random.normal(k, shape, jnp.float32) * 0.02
        return {'x': jax.random.normal(ks[0], (B, T, C), jnp.float32), 'ln1_w': jnp.ones((C,), jnp.float32), 'ln2_w': jnp.ones((C,), jnp.float32), 'wq': s(ks[1], (NH * HD, C)), 'wk': s(ks[2], (NKV * HD, C)), 'wv': s(ks[3], (NKV * HD, C)), 'wo': s(ks[4], (C, C)), 'router_w': s(ks[5], (NE, C)), 'w1': s(ks[6], (NE, HID, C)), 'w2': s(ks[7], (NE, C, HID)), 'w3': s(ks[8], (NE, HID, C))}
    _L0_ffn_all = _L0_ffn_setup()
    _L0_ffn_in = {k: v for k, v in _L0_ffn_all.items() if k in ('ln1_w', 'ln2_w', 'wq', 'wk', 'wv', 'wo', 'router_w', 'w1', 'w2', 'w3')}
    del _L0_ffn_all
    return {'x': x, 'src': src, 'dst': dst, 'L0_gnn_Wq': _L0_gnn_in['Wq'], 'L0_gnn_bq': _L0_gnn_in['bq'], 'L0_gnn_Wk': _L0_gnn_in['Wk'], 'L0_gnn_bk': _L0_gnn_in['bk'], 'L0_gnn_Wv': _L0_gnn_in['Wv'], 'L0_gnn_bv': _L0_gnn_in['bv'], 'L0_gnn_Wskip': _L0_gnn_in['Wskip'], 'L0_gnn_bskip': _L0_gnn_in['bskip'], 'L0_gnn_gamma': _L0_gnn_in['gamma'], 'L0_gnn_beta_ln': _L0_gnn_in['beta_ln'], 'L0_mix_w_qkv': _L0_mix_in['w_qkv'], 'L0_mix_w_out': _L0_mix_in['w_out'], 'L0_mix_b_out': _L0_mix_in['b_out'], 'L0_ffn_ln1_w': _L0_ffn_in['ln1_w'], 'L0_ffn_ln2_w': _L0_ffn_in['ln2_w'], 'L0_ffn_wq': _L0_ffn_in['wq'], 'L0_ffn_wk': _L0_ffn_in['wk'], 'L0_ffn_wv': _L0_ffn_in['wv'], 'L0_ffn_wo': _L0_ffn_in['wo'], 'L0_ffn_router_w': _L0_ffn_in['router_w'], 'L0_ffn_w1': _L0_ffn_in['w1'], 'L0_ffn_w2': _L0_ffn_in['w2'], 'L0_ffn_w3': _L0_ffn_in['w3']}

def reference(x, src, dst, L0_gnn_Wq, L0_gnn_bq, L0_gnn_Wk, L0_gnn_bk, L0_gnn_Wv, L0_gnn_bv, L0_gnn_Wskip, L0_gnn_bskip, L0_gnn_gamma, L0_gnn_beta_ln, L0_mix_w_qkv, L0_mix_w_out, L0_mix_b_out, L0_ffn_ln1_w, L0_ffn_ln2_w, L0_ffn_wq, L0_ffn_wk, L0_ffn_wv, L0_ffn_wo, L0_ffn_router_w, L0_ffn_w1, L0_ffn_w2, L0_ffn_w3):
    import jax
    import jax.numpy as jnp

    def _L0_gnn_ref(x, edge_index, Wq, bq, Wk, bk, Wv, bv, Wskip, bskip, gamma, beta_ln):
        import jax, jax.numpy as jnp
        import numpy as np
        N = 625
        E = 10000
        IN = 256
        H = 4
        C = 64
        D = H * C
        LN_EPS = 1e-05
        src = edge_index[0]
        dst = edge_index[1]
        q = (x @ Wq + bq).reshape(N, H, C)
        k = (x @ Wk + bk).reshape(N, H, C)
        v = (x @ Wv + bv).reshape(N, H, C)
        scale = 1.0 / jnp.sqrt(jnp.float32(C))
        alpha = jnp.einsum('ehc,ehc->eh', q[dst], k[src]) * scale
        m = jax.ops.segment_max(alpha, dst, num_segments=N)
        m = jnp.where(jnp.isfinite(m), m, 0.0)
        a = jnp.exp(alpha - m[dst])
        denom = jax.ops.segment_sum(a, dst, num_segments=N)
        a = a / (denom[dst] + 1e-16)
        msg = a[:, :, None] * v[src]
        agg = jax.ops.segment_sum(msg, dst, num_segments=N)
        out = agg.reshape(N, D) + (x @ Wskip + bskip)
        out = jax.nn.gelu(out, approximate=False)
        mu = jnp.mean(out, axis=-1, keepdims=True)
        var = jnp.var(out, axis=-1, keepdims=True)
        out = (out - mu) * jax.lax.rsqrt(var + LN_EPS) * gamma + beta_ln
        return out

    def _L0_mix_ref(x, w_qkv, w_out, b_out):
        import jax, jax.numpy as jnp
        import numpy as np
        HEADS, DIM_HEAD = (8, 64)
        EPS = 1e-05

        def instance_norm(t):
            mu = jnp.mean(t, axis=-1, keepdims=True)
            var = jnp.mean((t - mu) ** 2, axis=-1, keepdims=True)
            return (t - mu) * jax.lax.rsqrt(var + EPS)
        B, N, _ = x.shape
        H, Dh = (HEADS, DIM_HEAD)
        qkv = jnp.einsum('bnd,ed->bne', x, w_qkv)
        q, k, v = jnp.split(qkv, 3, axis=-1)

        def to_heads(t):
            return t.reshape(B, N, H, Dh).transpose(0, 2, 1, 3)
        q, k, v = (to_heads(q), to_heads(k), to_heads(v))
        k = instance_norm(k)
        v = instance_norm(v)
        dots = jnp.einsum('bhnd,bhne->bhde', k, v)
        out = jnp.einsum('bhnd,bhde->bhne', q, dots) / N
        out = out.transpose(0, 2, 1, 3).reshape(B, N, H * Dh)
        return jnp.einsum('bne,de->bnd', out, w_out) + b_out

    def _L0_ffn_ref(x, ln1_w, ln2_w, wq, wk, wv, wo, router_w, w1, w2, w3):
        import jax, jax.numpy as jnp
        import numpy as np
        B, T, C = (64, 384, 256)
        NH, NKV = (4, 2)
        HD = C // NH
        NREP = NH // NKV
        NE, TOPK = (8, 2)
        HID = int(8 / 3 * C)
        EPS_RMS = 1e-06

        def _rope_tables(t_len):
            inv_freq = 1.0 / 10000.0 ** (np.arange(0, HD, 2, dtype=np.float32) / HD)
            t = np.arange(t_len, dtype=np.float32)
            freqs = np.outer(t, inv_freq)
            emb = np.concatenate([freqs, freqs], axis=-1)
            return (jnp.asarray(np.cos(emb)), jnp.asarray(np.sin(emb)))

        def _rotate_half(x):
            h = x.shape[-1] // 2
            return jnp.concatenate([-x[..., h:], x[..., :h]], axis=-1)

        def _rmsnorm(v, w):
            return v * jax.lax.rsqrt(jnp.mean(v * v, axis=-1, keepdims=True) + EPS_RMS) * w
        Bx, Tx, Cx = x.shape
        h = _rmsnorm(x, ln1_w)
        q = (h @ wq.T).reshape(Bx, Tx, NH, HD).transpose(0, 2, 1, 3)
        k = (h @ wk.T).reshape(Bx, Tx, NKV, HD).transpose(0, 2, 1, 3)
        v = (h @ wv.T).reshape(Bx, Tx, NKV, HD).transpose(0, 2, 1, 3)
        cos, sin = _rope_tables(Tx)
        cos, sin = (cos[None, None], sin[None, None])
        q = q * cos + _rotate_half(q) * sin
        k = k * cos + _rotate_half(k) * sin
        k = jnp.repeat(k, NREP, axis=1)
        v = jnp.repeat(v, NREP, axis=1)
        scores = jnp.einsum('bhtd,bhsd->bhts', q, k) / jnp.sqrt(jnp.float32(HD))
        causal = jnp.tril(jnp.ones((Tx, Tx), dtype=bool))
        scores = jnp.where(causal[None, None], scores, jnp.float32(-1e+30))
        att = jax.nn.softmax(scores, axis=-1)
        y = jnp.einsum('bhts,bhsd->bhtd', att, v).transpose(0, 2, 1, 3).reshape(Bx, Tx, Cx)
        x = x + y @ wo.T
        flat = _rmsnorm(x, ln2_w).reshape(-1, Cx)
        probs = jax.nn.softmax(flat @ router_w.T, axis=-1)
        tp, ti = jax.lax.top_k(probs, TOPK)
        tp = tp / (jnp.sum(tp, axis=-1, keepdims=True) + 1e-09)
        weights = jnp.sum(tp[..., None] * jax.nn.one_hot(ti, NE, dtype=flat.dtype), axis=1)
        out = jnp.zeros_like(flat)
        for e in range(NE):
            hh = jax.nn.silu(flat @ w1[e].T) * (flat @ w3[e].T)
            out = out + weights[:, e:e + 1] * (hh @ w2[e].T)
        return x + out.reshape(Bx, Tx, Cx)
    edge_index = jnp.stack([src, dst])
    xn = _layernorm(x, axis=-1)
    x = x + _L0_gnn_ref(xn, edge_index, L0_gnn_Wq, L0_gnn_bq, L0_gnn_Wk, L0_gnn_bk, L0_gnn_Wv, L0_gnn_bv, L0_gnn_Wskip, L0_gnn_bskip, L0_gnn_gamma, L0_gnn_beta_ln) + _L0_mix_ref(xn[None], L0_mix_w_qkv, L0_mix_w_out, L0_mix_b_out)[0]
    x = x + _L0_ffn_ref(_layernorm(x, axis=-1)[None], L0_ffn_ln1_w, L0_ffn_ln2_w, L0_ffn_wq, L0_ffn_wk, L0_ffn_wv, L0_ffn_wo, L0_ffn_router_w, L0_ffn_w1, L0_ffn_w2, L0_ffn_w3)[0]
    return x

_drawn_inputs = setup_inputs


def setup_inputs(seed=0):
    import zlib

    import numpy as np

    out = dict(_drawn_inputs(seed))
    spreads = {'L0_gnn_bq': (0.0, 0.669),
     'L0_gnn_bk': (0.0, 0.8),
     'L0_gnn_bv': (0.0, 0.1),
     'L0_gnn_bskip': (0.0, 0.1),
     'L0_gnn_gamma': (1.0, 0.2),
     'L0_gnn_beta_ln': (0.0, 0.1),
     'L0_ffn_ln1_w': (1.0, 0.6),
     'L0_ffn_ln2_w': (1.0, 0.6)}
    factors = {'L0_mix_b_out': 8.0,
     'L0_ffn_wq': 8.0,
     'L0_ffn_wk': 8.0,
     'L0_ffn_wv': 7.956,
     'L0_ffn_wo': 7.466,
     'L0_ffn_router_w': 7.517,
     'L0_ffn_w1': 6.689,
     'L0_ffn_w2': 6.638,
     'L0_ffn_w3': 6.624}
    for name, (base, spread) in spreads.items():
        noise = np.random.default_rng([zlib.crc32(name.encode()), seed]).standard_normal(out[name].shape)
        drawn = base * np.exp(spread * noise) if base else spread * noise
        out[name] = jnp.asarray(drawn.astype(out[name].dtype))
    for name, factor in factors.items():
        out[name] = (out[name] * factor).astype(out[name].dtype)
    return out
```

```python
import numpy as np
import concourse.bass as bass
from concourse import mybir
from contextlib import ExitStack

fp32 = mybir.dt.float32
bf16 = mybir.dt.bfloat16
fp16 = mybir.dt.float16
i32 = mybir.dt.int32
u32 = mybir.dt.uint32
ALU = mybir.AluOpType
ACT = mybir.ActivationFunctionType
AX = mybir.AxisListType

N, D = 625, 256
NT, TP = 5, 125
KC = D // 128
H, C = 4, 64
EDGES = 20000
ET = EDGES // TP
EG = 4
NG = ET // EG
MH = 8
MI = MH * C
NE, HID = 8, 682
HH = HID // 2
HC = 3
HCW = (128, 128, HH - 256)
MAXB = 17
NB = MAXB + 1
EPS = 1e-5
EPS_RMS = 1e-6
BIG = 1e30


def build(nc, x, edge_groups, edge_src, edge_dst, w_gnn, b_gnn_qk, b_gnn_vs, w_mix_kv, w_mix_q,
          w_mix_out, rows, w_ffn_qkv, w_ffn_o, ln1_col, w_router, w13, w2, c_f32, c_bf16, c_iota,
          c_rope, c_row, out):
    xg = nc.dram_tensor("xg_scratch", (NB * 128, D), fp32, kind="Internal").ap()
    yg = nc.dram_tensor("yg_scratch", (MAXB * 128, D), fp32, kind="Internal").ap()
    ctx = ExitStack()
    with ctx:
        def sb(name, shape, dt=fp32):
            return ctx.enter_context(nc.sbuf_tensor(name, shape, dt))

        def sem(name):
            return ctx.enter_context(nc.semaphore(name))

        W13 = sb("W13", [128, NE, KC, 2 * HID])
        W2 = sb("W2", [128, NE, 2 * HC, D])
        w2_flat = W2[:, :, :, :].rearrange("p e k d -> p (e k d)")
        kvc = w2_flat[:, 0:5120].rearrange("p (i n) -> p i n", i=NT)
        wgnn = w2_flat[:, 5120:7168].rearrange("p (k n) -> p k n", k=KC)
        wkv = w2_flat[:, 7168:9216].rearrange("p (k n) -> p k n", k=KC)
        wmq = w2_flat[:, 9216:10240].rearrange("p (e n) -> p e n", e=4)
        wmo = w2_flat[:, 10240:11264].rearrange("p (e n) -> p e n", e=4)
        M1 = w2_flat[:, 11264:12288].rearrange("p (e n) -> p e n", e=4)
        NLATE = 5
        late_flat = W13[:, NE - NLATE:NE, :, :].rearrange("p e k n -> p (e k n)")
        VS = late_flat[0:TP, 0:2560].rearrange("p (i n) -> p i n", i=NT)
        gqkT = late_flat[:, 2560:5060].rearrange("p (m n) -> p m n", m=4)
        edge_mask = late_flat[:, 5060:6624].bitcast(bf16)[0:TP, 0:3125].rearrange("p (i n) -> p i n", i=NT)
        X = late_flat[0:TP, 6624:7904].rearrange("p (i n) -> p i n", i=NT)

        cnt = late_flat[0:TP, 7904:11029].rearrange("p (i n) -> p i n", i=NT)
        edgesg = late_flat[0:NG, 7904:8404].bitcast(i32)
        dbd = late_flat[:, 11029:11541].rearrange("p (e n) -> p e n", e=4)
        bvs = late_flat[0:TP, 11541:12053]
        M2 = late_flat[:, 12053:12565].rearrange("p (k n) -> p k n", k=KC)
        zrow = late_flat[:, 12565:12821]
        rowv = late_flat[0:TP, 12821:13589].rearrange("p (k n) -> p k n", k=3)
        gamma, beta, bout = (rowv[:, k, :] for k in range(3))

        CM = sb("CM", [128, 4352])
        AT = CM[0:TP, 0:1250].rearrange("p (u j n) -> p u j n", u=2, j=NT)
        rope = CM[0:TP, 1250:1890].rearrange("p (k i c) -> p k i c", k=2, i=NT)
        yat = CM[0:TP, 1890:2402].rearrange("p (u n) -> p u n", u=2)
        yT = CM[:, 2402:2902].rearrange("p (u k n) -> p u k n", u=2, k=KC)
        wqkv = CM[:, 2902:3926].rearrange("p (k n) -> p k n", k=KC)
        zero16 = CM[:, 3926:4182].bitcast(fp16)
        xblk = CM[:, 0:512].rearrange("p (u n) -> p u n", u=2)
        xTb = CM[:, 512:1024].rearrange("p (u k n) -> p u k n", u=2, k=KC)
        gb = CM[:, 1024:1024 + 4 * HH].rearrange("p (u j n) -> p u j n", u=2, j=2)
        hTb = CM[:, 2390:2390 + 768].rearrange("p (j k n) -> p j k n", j=2, k=HC)
        yb = CM[:, 3158:3158 + 512].rearrange("p (u n) -> p u n", u=2)
        sl = CM[:, 3670:3670 + 2 * HH].rearrange("p (j n) -> p j n", j=2)

        RING = sb("RING", [128, 3140])
        ring16 = RING[:, 0:EG * 384].bitcast(fp16)
        oh_src = ring16[0:TP, 0:EG * 640].rearrange("p (s n) -> p s n", s=EG)
        oh_dst = ring16[0:TP, EG * 640:EG * 768].rearrange("p (s n) -> p s n", s=EG)
        QKT = RING[:, 0:1875].rearrange("p (m n) -> p m n", m=3)
        Vc = RING[0:TP, 1875:1875 + 640].rearrange("p (i n) -> p i n", i=NT)
        qkr = RING[0:TP, 2515:2515 + 384]
        Y1 = RING[0:TP, 0:1280].rearrange("p (i n) -> p i n", i=NT)
        Y2 = RING[0:TP, 1280:2560].rearrange("p (i n) -> p i n", i=NT)

        ER = sb("ER", [128, 1888])
        E = ER[0:TP, 0:1875].rearrange("p (s n) -> p s n", s=3)
        sq = ER[0:TP, 0:1024]
        dstf = ER[0:TP, 0:160]
        srcf = ER[0:TP, 160:320]
        dstrel = ER[0:TP, 320:1120].rearrange("p (b t) -> p b t", b=NT)
        dsti = ER[0:TP, 1120:1280].bitcast(i32)
        srci = ER[0:TP, 1280:1440].bitcast(i32)
        iota16 = ER[0:TP, 1440:1756].bitcast(fp16)[:, 0:N]

        xnT = sb("xnT", [128, KC, N])
        xn = sb("xn", [TP, NT, D])
        x1 = sb("x1", [TP, NT, D])
        hrow = sb("hrow", [TP, NT, D])
        wo = sb("wo", [128, KC, D])
        wr = sb("wr", [128, KC, NE])
        ln1c = sb("ln1c", [128, KC])
        bqk = sb("bqk", [128, 4])
        ln2r = sb("ln2r", [TP, D])
        ln2 = ln2r[:, :]
        cf = sb("cf", [128, 128 + 160])
        ident = cf[:, 0:128]
        iota8 = cf[0:TP, 128:136]
        thr = cf[0:TP, 136:141]
        cbf = sb("cbf", [128, 4 * 128], bf16)
        tri = cbf[0:TP, 0:TP]
        ones = cbf[0:TP, 128:128 + TP]
        identb = cbf[0:TP, 256:256 + TP]
        causal = cbf[0:TP, 384:384 + TP]
        powm = sb("powm", [TP, 80])
        st = sb("st", [TP, NT, 6])
        mv = sb("mv", [TP, NT, 2])
        v_eps = sb("v_eps", [TP, NT])
        rstd = sb("rstd", [TP, NT])
        wmean = sb("wmean", [128, 32])
        ss = sb("ss", [TP, NT, 16])
        ssp = sb("ssp", [TP, NT, 8])
        rkv = sb("rkv", [TP, NT, 8])
        gmm = sb("gmm", [NG, 2])
        crow = sb("crow", [1, 512])
        rr = sb("rr", [1, 920])
        rangei = sb("rangei", [1, 2, NT], i32)
        mn = sb("mn", [TP, 20])
        den = sb("den", [TP, 20])
        rd = sb("rd", [TP, 4])
        mn2 = sb("mn2", [TP, 20])
        den2 = sb("den2", [TP, 20])
        rt = sb("rt", [TP, 864])
        rti = sb("rti", [TP, 64], u32)
        blki = sb("blki", [1, 32], i32)
        ps = ctx.enter_context(nc.psum_tensor("ps", [128, 8, 512], fp32))

        def flat(b, n=1024):
            return ps[:, b:b + (n + 511) // 512, :].rearrange("p b n -> p (b n)")[:, 0:n]

        ld_x, ld_const, ld_edges, ld_gnn, ld_mix, ld_ffn, ld_rows = (
            sem(n) for n in ("ld_x", "ld_const", "ld_edges", "ld_gnn", "ld_mix", "ld_ffn", "ld_rows"))
        ld_w, ld_late, xg_zeroed = sem("ld_w"), sem("ld_late"), sem("xg_zeroed")
        link_dve, link_pool = sem("link_dve"), sem("link_pool")
        consts_set = sem("consts_set")
        var1, rstd1, xn_done, xnT_ps, xnT_done = (
            sem(n) for n in ("var1", "rstd1", "xn_done", "xnT_ps", "xnT_done"))
        bq_scaled, qk_ps, qk_done, vs_ps, vs_done = (
            sem(n) for n in ("bq_scaled", "qk_ps", "qk_done", "vs_ps", "vs_done"))
        gmm_done, gmm_ps, range_done = sem("gmm_done"), sem("gmm_ps"), sem("range_done")
        oh_built, oh_used, cnt_ps, cnt_done, mask_done = (
            sem(n) for n in ("oh_built", "oh_used", "cnt_ps", "cnt_done", "mask_done"))
        wkv_centred, kv_ps, kv_copied, sq_done, sq_used, ssp_done, rkv_done, kv_normed = (
            sem(n) for n in ("wkv_centred", "kv_ps", "kv_copied", "sq_done", "sq_used", "ssp_done",
                             "rkv_done", "kv_normed"))
        dots_ps, dbd_done, M1_ps, M1_done, M2_ps, M2_done = (
            sem(n) for n in ("dots_ps", "dbd_done", "M1_ps", "M1_done", "M2_ps", "M2_done"))
        xb_done, S_ps, S_used, exp_done, A_done, AT_ps, AT_done, AV_done, O_used, gelu_done = (
            sem(n) for n in ("xb_done", "S_ps", "S_used", "exp_done", "A_done", "AT_ps", "AT_done",
                             "AV_done", "O_used", "gelu_done"))
        agg_done, varg, rstdg, var2, r2, ms2, hr = (
            sem(n) for n in ("agg_done", "varg", "rstdg", "var2", "r2", "ms2", "hr"))
        h_done, hT_ps, hT_done, qkv_ps, qkr_done, vc_done, qkT_ps, qkT_done, qkr_used = (
            sem(n) for n in ("h_done", "hT_ps", "hT_done", "qkv_ps", "qkr_done", "vc_done", "qkT_ps",
                             "qkT_done", "qkr_used"))
        qkv_used = sem("qkv_used")
        S2_ps, max2_done, exp2_done, ET_ps, ET_done, AV2_done, y_done, O2_used = (
            sem(n) for n in ("S2_ps", "max2_done", "exp2_done", "ET_ps", "ET_done", "AV2_done",
                             "y_done", "O2_used"))
        yT_ps, yT_done, wo_ps, x2_done = (sem(n) for n in ("yT_ps", "yT_done", "wo_ps", "x2_done"))
        ms3, r3, flat_done, flatT_ps, flatT_done, logit_ps = (
            sem(n) for n in ("ms3", "r3", "flat_done", "flatT_ps", "flatT_done", "logit_ps"))
        rmax_done, rexp_done, sel_done, rank_ps, blk_done, slot_done, scattered = (
            sem(n) for n in ("rmax_done", "rexp_done", "sel_done", "rank_ps", "blk_done", "slot_done",
                             "scattered"))
        xblk_ld = [sem("xblk_ld0"), sem("xblk_ld1")]
        y_stored, last_y_stored, y_free = sem("y_stored"), sem("last_y_stored"), sem("y_free")
        mxT_ps, mxT_done, ab_ps, silu_done, g_done, gT_ps, gT_copied, y_ps, y_copied = (
            sem(n) for n in ("mxT_ps", "mxT_done", "ab_ps", "silu_done", "g_done", "gT_ps",
                             "gT_copied", "y_ps", "y_copied"))
        y_gathered, out_done, out_stored = sem("y_gathered"), sem("out_done"), sem("out_stored")

        block = ctx.enter_context(nc.Block())

        HALVES = ((0, 313), (313, 625))

        @block.sync
        def _(sp):
            sp.dma_start(X, x.rearrange("(i p) c -> p i c", p=TP)).then_inc(ld_x, 16)
            sp.dma_start(cf[:, :], c_f32).then_inc(ld_const, 16)
            sp.dma_start(edgesg, edge_groups).then_inc(ld_edges, 16)
            sp.dma_start(crow[:, :], c_row).then_inc(ld_edges, 16)
            sp.dma_start(dsti, edge_dst).then_inc(ld_edges, 16)
            sp.dma_start(srci, edge_src).then_inc(ld_edges, 16)
            sp.dma_start(iota16, c_iota.partition_broadcast(TP)).then_inc(ld_edges, 16)
            sp.dma_start(wgnn, w_gnn).then_inc(ld_gnn, 16)
            sp.dma_start(bqk[:, :], b_gnn_qk).then_inc(ld_gnn, 16)
            sp.dma_start(bvs, b_gnn_vs.partition_broadcast(TP)).then_inc(ld_gnn, 16)
            sp.dma_start(wkv, w_mix_kv).then_inc(ld_mix, 16)
            sp.dma_start(wmq, w_mix_q).then_inc(ld_mix, 16)
            sp.dma_start(wmo, w_mix_out).then_inc(ld_mix, 16)
            sp.dma_start(rowv, rows[0:3, :].partition_broadcast(TP)).then_inc(ld_rows, 16)
            sp.dma_start(ln2, rows[3, :].partition_broadcast(TP)).then_inc(ld_rows, 16)
            sp.dma_start(cbf[:, :], c_bf16).then_inc(ld_const, 16)
            sp.dma_start(rope, c_rope).then_inc(ld_const, 16)
            sp.dma_start(wqkv, w_ffn_qkv).then_inc(ld_ffn, 16)
            sp.dma_start(wo[:, :, :], w_ffn_o).then_inc(ld_ffn, 16)
            sp.dma_start(wr[:, :, :], w_router).then_inc(ld_ffn, 16)
            sp.dma_start(ln1c[:, :], ln1_col).then_inc(ld_ffn, 16)
            for e in range(NE - NLATE):
                sp.dma_start(W13[:, e, :, :], w13[:, e, :, :]).then_inc(ld_w, 16)
            sp.wait_ge(consts_set, 3)
            sp.dma_start(xg.rearrange("(p j) c -> p j c", p=128),
                         zrow.unsqueeze(1).to_broadcast([128, NB, D])).then_inc(xg_zeroed, 16)
            sp.dma_start(yg.rearrange("(p j) c -> p j c", p=128),
                         zrow.unsqueeze(1).to_broadcast([128, MAXB, D])).then_inc(xg_zeroed, 16)
            sp.wait_ge(M2_done, 1)
            for e in range(NE):
                for j in range(2):
                    sp.dma_start(W2[:, e, HC * j:HC * j + 2, :],
                                 w2[e, HH * j:HH * j + 256, :].rearrange("(k p) d -> p k d", p=128)
                                 ).then_inc(ld_late, 16)
                    sp.dma_start(W2[0:HCW[2], e, HC * j + 2, :],
                                 w2[e, HH * j + 256:HH * (j + 1), :]).then_inc(ld_late, 16)
            sp.wait_ge(var2, 1)
            for e in range(NE - NLATE, NE):
                sp.dma_start(W13[:, e, :, :], w13[:, e, :, :]).then_inc(ld_late, 16)
            sp.wait_ge(scattered, 16 * 2 * NT)
            sp.wait_ge(blk_done, 1)
            iters = sp.value_load(blki[0:1, NB:NB + 1], min_val=1, max_val=(MAXB - 1) // 2)
            sp.dma_start(xblk[:, 0, :], xg[0:128, :]).then_inc(xblk_ld[0], 16)
            sp.dma_start(xblk[:, 1, :], xg[128:256, :]).then_inc(xblk_ld[1], 16)
            with sp.Fori(0, iters) as m:
                for u, s in ((0, 2 * m + 1), (1, 2 * m + 2)):
                    sp.wait_ge(mxT_ps, s)
                    sp.dma_start(xblk[:, u, :], xg[bass.ds(s * 128 + 128, 128), :]).then_inc(xblk_ld[u], 16)
            for i in range(NT):
                sp.wait_ge(out_done, i + 1)
                sp.dma_start(out.rearrange("(i p) c -> p i c", p=TP)[:, i, :], x1[:, i, :]).then_inc(out_stored, 16)
            sp.wait_ge(out_stored, 16 * NT)

        @block.gpsimd
        def _(pool):
            steps = [0]

            def link(ins):
                steps[0] += 1
                ins.then_inc(link_pool, 1)
                pool.wait_ge(link_pool, steps[0])

            nc.gpsimd.memset(powm[:, :], -0.5).then_inc(consts_set, 1)
            nc.gpsimd.memset(zero16, 0.0).then_inc(consts_set, 1)
            nc.gpsimd.memset(zrow, 0.0).then_inc(consts_set, 1)
            nc.gpsimd.memset(dbd, 0.0).then_inc(consts_set, 1)
            pool.wait_ge(consts_set, 4)
            pool.wait_ge(var1, 1)
            nc.gpsimd.tensor_tensor(rstd[:, :], v_eps[:, :], powm[:, 0:NT], ALU.pow).then_inc(rstd1, 1)
            pool.wait_ge(ld_gnn, 48)
            nc.gpsimd.tensor_scalar(bqk[:, 0:2], bqk[:, 0:2], -1.0 / 8.0, 0.0, ALU.mult, ALU.add).then_inc(bq_scaled, 1)
            pool.wait_ge(ld_rows, 32)
            pool.wait_ge(ld_x, 16)
            link(nc.gpsimd.tensor_tensor(beta, beta, bout, ALU.add))
            for i in range(NT):
                nc.gpsimd.tensor_tensor(x1[:, i, :], X[:, i, :], beta, ALU.add).then_inc(xb_done, 1)
            pool.wait_ge(ssp_done, 1)
            nc.gpsimd.tensor_tensor(rkv[:, :, :].rearrange("p i h -> p (i h)"),
                                    ssp[:, :, :].rearrange("p i h -> p (i h)"), powm[:, 0:40], ALU.pow).then_inc(rkv_done, 1)
            pool.wait_ge(varg, 1)
            nc.gpsimd.tensor_tensor(rstd[:, :], v_eps[:, :], powm[:, 0:NT], ALU.pow).then_inc(rstdg, 1)
            pool.wait_ge(var2, 1)
            nc.gpsimd.tensor_tensor(rstd[:, :], v_eps[:, :], powm[:, 0:NT], ALU.pow).then_inc(r2, 1)
            pool.wait_ge(ms2, 1)
            nc.gpsimd.tensor_tensor(rt[:, 0:NT], rt[:, 5:10], powm[:, 0:NT], ALU.pow).then_inc(hr, 1)
            pool.wait_ge(ms3, 1)
            nc.gpsimd.tensor_tensor(rstd[:, :], v_eps[:, :], powm[:, 0:NT], ALU.pow).then_inc(r3, 1)
            pool.wait_ge(slot_done, 1)
            pool.wait_ge(xg_zeroed, 32)
            for k in range(2):
                for i in range(NT):
                    nc.gpsimd.indirect_dma_start(
                        xg, bass.IndirectOffsetOnAxis(rti[:, 40 + 5 * k + i:41 + 5 * k + i], 0),
                        hrow[:, i, :], None).then_inc(scattered, 16)
            pool.wait_ge(blk_done, 1)
            iters = pool.value_load(blki[0:1, NB:NB + 1], min_val=1, max_val=(MAXB - 1) // 2)
            with pool.Fori(0, iters) as m:
                for u, s in ((0, 2 * m), (1, 2 * m + 1)):
                    pool.wait_ge(y_copied, s + 2)
                    pool.dma_start(yg[bass.ds(s * 128, 128), :], yb[:, u, :]).then_inc(y_stored, 16)
                    pool.wait_ge(y_stored, 16 * s + 16)
                    pool.sem_inc(y_free, 1)
            pool.wait_ge(y_copied, 2 * iters + 2)
            pool.dma_start(yg[bass.ds(iters * 256, 128), :], yb[:, 0, :]).then_inc(last_y_stored, 16)
            pool.wait_ge(last_y_stored, 16)
            for i in range(NT):
                for k, Y in ((0, Y1), (1, Y2)):
                    nc.gpsimd.indirect_dma_start(
                        Y[:, i, :], None, yg,
                        bass.IndirectOffsetOnAxis(rti[:, 40 + 5 * k + i:41 + 5 * k + i], 0)).then_inc(y_gathered, 16)

        @block.scalar
        def _(act):
            for i in range(NT):
                act.wait_ge(xnT_ps, i + 1)
                nc.scalar.copy(xnT[:, :, i * TP:(i + 1) * TP],
                               ps[:, i % 2, 0:256].rearrange("p (k n) -> p k n", k=KC)[:, :, 0:TP]).then_inc(xnT_done, 1)
            act.wait_ge(bq_scaled, 1)
            for j in range(8):
                m, (a, b) = j // 2, HALVES[j % 2]
                act.wait_ge(qk_ps, j + 1)
                nc.scalar.activation(gqkT[:, m, a:b], ps[:, 2 + j % 4, 0:b - a], ACT.Identity,
                                     bias=bqk[:, m:m + 1], scale=-0.125 if m < 2 else 1.0).then_inc(qk_done, 1)
            for b in range(NT):
                act.wait_ge(cnt_ps, b + 1)
                if b == 0:
                    act.wait_ge(range_done, 1)
                nc.scalar.copy(cnt[:, b, 0:512], ps[0:TP, b, :]).then_inc(cnt_done, 1)
            nc.scalar.copy(cnt[:, 0:4, 512:N], ps[0:TP, 5, 0:4 * 113].rearrange("p (b n) -> p b n", b=4)).then_inc(cnt_done, 1)
            nc.scalar.copy(cnt[:, 4, 512:N], ps[0:TP, 6, 0:113]).then_inc(cnt_done, 1)
            for i in range(NT):
                kv = flat(2 * (i % 2))[0:TP, :]
                act.wait_ge(kv_ps, i + 1)
                nc.scalar.copy(kvc[0:TP, i, :], kv).then_inc(kv_copied, 1)
                if i:
                    act.wait_ge(sq_used, i)
                nc.scalar.activation(sq, kv, ACT.Square).then_inc(sq_done, 1)
            act.wait_ge(M1_ps, 1)
            nc.scalar.copy(M1, flat(5).rearrange("p (e n) -> p e n", e=4)).then_inc(M1_done, 1)
            act.wait_ge(M2_ps, 1)
            nc.scalar.copy(M2[:, :, :].rearrange("p k n -> p (k n)"), ps[:, 7, :]).then_inc(M2_done, 1)

            def gnn_AT(n):
                act.wait_ge(AT_ps, n + 1)
                if n >= 2:
                    act.wait_ge(AV_done, n - 1)
                nc.scalar.copy(AT[:, n % 2, :, :],
                               flat(4)[0:TP, 0:640].rearrange("p (j n) -> p j n", j=NT)[:, :, 0:TP]).then_inc(AT_done, 1)

            for n in range(20):
                act.wait_ge(S_used, n + 1)
                nc.scalar.activation(E[:, n % 3, :], E[:, n % 3, :], ACT.Exp,
                                     bias=mn[:, n:n + 1], scale=-1.0).then_inc(exp_done, 1)
                if n >= 2:
                    gnn_AT(n - 2)
            gnn_AT(18)
            gnn_AT(19)
            act.wait_ge(agg_done, NT)
            nc.scalar.activation(VS[:, :, D:512], VS[:, :, D:512], ACT.Gelu).then_inc(gelu_done, 1)
            act.wait_ge(ld_ffn, 64)
            for i in range(NT):
                act.wait_ge(hT_ps, i + 1)
                for k in range(KC):
                    ins = nc.scalar.activation(xnT[:, k, i * TP:(i + 1) * TP],
                                               ps[:, i % 2, 128 * k:128 * k + TP], ACT.Copy, scale=ln1c[:, k:k + 1])
                ins.then_inc(hT_done, 1)

            def qkT_copy(i):
                act.wait_ge(qkT_ps, i + 1)
                t = ps[:, 4 + i % 2, 0:384].rearrange("p (m n) -> p m n", m=3)[:, :, 0:TP]
                nc.scalar.mul(QKT[:, 0:2, i * TP:(i + 1) * TP], t[:, 0:2, :], 0.125)
                nc.scalar.copy(QKT[:, 2, i * TP:(i + 1) * TP], t[:, 2, :]).then_inc(qkT_done, 1)

            for i in range(NT):
                act.wait_ge(qkv_used, i + 1)
                nc.scalar.copy(Vc[:, i, :], ps[0:TP, 2 + i % 2, 384:512]).then_inc(vc_done, 1)
                if i:
                    qkT_copy(i - 1)
            qkT_copy(NT - 1)

            def ffn_ET(n):
                i = n // 4
                act.wait_ge(ET_ps, n + 1)
                if n >= 2:
                    act.wait_ge(AV2_done, n - 1)
                nc.scalar.copy(AT[:, n % 2, 0:i + 1, :],
                               flat(4)[0:TP, 0:640].rearrange("p (j n) -> p j n", j=NT)[:, 0:i + 1, 0:TP]).then_inc(ET_done, 1)

            def ffn_yT(i):
                act.wait_ge(yT_ps, i + 1)
                nc.scalar.copy(yT[:, i % 2, :, :],
                               ps[:, 7, 0:256].rearrange("p (k n) -> p k n", k=KC)[:, :, 0:TP]).then_inc(yT_done, 1)

            for n in range(20):
                i = n // 4
                act.wait_ge(max2_done, n + 1)
                if n >= 3:
                    act.wait_ge(ET_ps, n - 2)
                w = TP * (i + 1)
                nc.scalar.activation(E[:, n % 3, 0:w], flat(2 * (n % 2))[0:TP, 0:w], ACT.Exp,
                                     bias=mn2[:, n:n + 1], scale=1.0,
                                     accum_out=den2[:, n:n + 1]).then_inc(exp2_done, 1)
                if n >= 2:
                    ffn_ET(n - 2)
                if n % 4 == 3 and 7 <= n < 19:
                    ffn_yT(i - 1)
            ffn_ET(18)
            ffn_yT(3)
            ffn_ET(19)
            ffn_yT(NT - 1)
            for i in range(NT):
                act.wait_ge(flatT_ps, i + 1)
                nc.scalar.copy(xnT[:, :, i * TP:(i + 1) * TP],
                               ps[:, i % 2, 0:256].rearrange("p (k n) -> p k n", k=KC)[:, :, 0:TP]).then_inc(flatT_done, 1)
            act.wait_ge(rmax_done, 1)
            nc.scalar.activation(rt[:, 64:104], rt[:, 64:104], ACT.Exp).then_inc(rexp_done, 1)

            def xT_copy(s, u):
                act.wait_ge(mxT_ps, s + 1)
                nc.scalar.copy(xTb[:, u, :, :], ps[:, 7, 0:256].rearrange("p (k n) -> p k n", k=KC)).then_inc(mxT_done, 1)

            def silu(s, j):
                act.wait_ge(ab_ps, 2 * s + j + 1)
                if not isinstance(s, int):
                    act.wait_ge(g_done, 2 * s + j - 1)
                nc.scalar.activation(sl[:, j, :], ps[:, 2 * j, 0:HH], ACT.Silu).then_inc(silu_done, 1)

            def hT_copy(s, j):
                act.wait_ge(gT_ps, 2 * s + j + 1)
                nc.scalar.copy(hTb[:, j, :, :], ps[:, 4 + j, 0:384].rearrange("p (k n) -> p k n", k=HC)).then_inc(gT_copied, 1)

            act.wait_ge(blk_done, 1)
            iters = act.value_load(blki[0:1, NB:NB + 1], min_val=1, max_val=(MAXB - 1) // 2)
            xT_copy(0, 0)
            silu(0, 0)
            xT_copy(1, 1)
            silu(0, 1)
            with act.Fori(0, iters) as m:
                for u, s in ((1, 2 * m + 1), (0, 2 * m + 2)):
                    silu(s, 0)
                    xT_copy(s + 1, 1 - u)
                    hT_copy(s - 1, 0)
                    hT_copy(s - 1, 1)
                    silu(s, 1)
            for j in range(2):
                hT_copy(2 * iters, j)

        @block.tensor
        def _(pe):
            def two_transposes(bank, rows, src_parts=TP):
                for k in range(KC):
                    ins = nc.tensor.transpose(ps[:, bank, 128 * k:128 * k + src_parts],
                                              rows[:, 128 * k:128 * (k + 1)], ident[0:src_parts, 0:src_parts])
                return ins

            pe.wait_ge(ld_const, 48)
            for i in range(NT):
                pe.wait_ge(xn_done, i + 1)
                if i >= 2:
                    pe.wait_ge(xnT_done, i - 1)
                two_transposes(i % 2, xn[:, i, :]).then_inc(xnT_ps, 1)
            pe.wait_ge(ld_gnn, 48)
            pe.wait_ge(xnT_done, NT)
            for j in range(8):
                m, (a, b) = j // 2, HALVES[j % 2]
                if j >= 4:
                    pe.wait_ge(qk_done, j - 3)
                for k in range(KC):
                    ins = nc.tensor.matmul(ps[:, 2 + j % 4, 0:b - a], wgnn[:, k, 128 * m:128 * (m + 1)],
                                           xnT[:, k, a:b], start=(k == 0), stop=(k == KC - 1))
                ins.then_inc(qk_ps, 1)
            for i in range(NT):
                if i >= 2:
                    pe.wait_ge(vs_done, i - 1)
                for k in range(KC):
                    ins = nc.tensor.matmul(ps[0:TP, 6 + i % 2, :], xnT[:, k, i * TP:(i + 1) * TP],
                                           wgnn[:, k, 512:1024], start=(k == 0), stop=(k == KC - 1))
                ins.then_inc(vs_ps, 1)
            pe.wait_ge(gmm_done, 1)
            for k in range(2):
                ins = nc.tensor.matmul(ps[0:1, 0, 40 * k:40 * k + 40], gmm[:, k:k + 1], ident[0:NG, 0:NG],
                                       start=True, stop=True)
            ins.then_inc(gmm_ps, 1)
            pe.wait_ge(range_done, 1)
            pe.wait_ge(qk_done, 8)
            pe.wait_ge(vs_done, NT)
            pe.wait_ge(consts_set, 4)
            seq = pe.alloc_register("pe_tiles")
            pe.reg_mov(seq, 0)
            for b in range(NT):
                big = ps[:, b, :]
                small = ps[:, 5, b * 113:b * 113 + 113] if b < 4 else ps[:, 6, 0:113]

                def zeros(start):
                    nc.tensor.matmul(big, zero16[:, 0:128], zero16, start=start, stop=not start)
                    return nc.tensor.matmul(small, zero16[:, 0:128], zero16[:, 0:113], start=start, stop=not start)

                first = pe.value_load(rangei[0:1, 0, b:b + 1], min_val=0, max_val=NG - 1)
                last = pe.value_load(rangei[0:1, 1, b:b + 1], min_val=1, max_val=NG)
                zeros(True)
                with pe.Fori(first, last):
                    done = pe.snap(seq, min_val=0, max_val=NT * ET)
                    for k in range(EG):
                        pe.wait_ge(oh_built, done + (k + 1))
                        nc.tensor.matmul(big, oh_dst[:, k, :], oh_src[:, k, 0:512], start=False, stop=False)
                        nc.tensor.matmul(small, oh_dst[:, k, :], oh_src[:, k, 512:N], start=False,
                                         stop=False).then_inc(oh_used, 1)
                    pe.reg_add(seq, seq, EG)
                zeros(False).then_inc(cnt_ps, 1)
            pe.wait_ge(ld_mix, 48)
            pe.wait_ge(wkv_centred, 1)
            pe.wait_ge(cnt_done, NT + 2)
            for i in range(NT):
                if i >= 2:
                    pe.wait_ge(sq_done, i - 1)
                for j in range(2):
                    for k in range(KC):
                        ins = nc.tensor.matmul(ps[0:TP, 2 * (i % 2) + j, :], xnT[:, k, i * TP:(i + 1) * TP],
                                               wkv[:, k, 512 * j:512 * (j + 1)], start=(k == 0), stop=(k == KC - 1))
                ins.then_inc(kv_ps, 1)
            pe.wait_ge(kv_normed, NT)
            for p in range(4):
                for i in range(NT):
                    ins = nc.tensor.matmul(ps[:, 4, 128 * p:128 * (p + 1)],
                                           kvc[0:TP, i, 512 + 128 * p:512 + 128 * (p + 1)],
                                           kvc[0:TP, i, 128 * p:128 * (p + 1)], start=(i == 0), stop=(i == NT - 1))
            ins.then_inc(dots_ps, 1)
            pe.wait_ge(dbd_done, 1)
            for p in range(4):
                ins = nc.tensor.matmul(ps[:, 5 + p // 2, 256 * (p % 2):256 * (p % 2) + 256], dbd[:, p, :],
                                       wmo[:, p, :], start=True, stop=True)
            ins.then_inc(M1_ps, 1)
            pe.wait_ge(M1_done, 1)
            for m in range(KC):
                for p in range(4):
                    ins = nc.tensor.matmul(ps[:, 7, 256 * m:256 * (m + 1)], wmq[:, p, 128 * m:128 * (m + 1)],
                                           M1[:, p, :], start=(p == 0), stop=(p == 3))
            ins.then_inc(M2_ps, 1)
            pe.wait_ge(M2_done, 1)

            def gnn_AV(n):
                i, h = n // 4, n % 4
                pe.wait_ge(AT_done, n + 1)
                for j in range(NT):
                    ins = nc.tensor.matmul(ps[0:TP, 6 + i % 2, C * h:C * (h + 1)], AT[:, n % 2, j, :],
                                           VS[:, j, C * h:C * (h + 1)], start=(j == 0), stop=(j == NT - 1))
                ins.then_inc(AV_done, 1)

            def gnn_T(n):
                pe.wait_ge(A_done, n + 1)
                if n >= 1:
                    pe.wait_ge(AT_done, n)
                for j in range(NT):
                    ins = nc.tensor.transpose(flat(4)[0:TP, 128 * j:128 * j + TP], E[:, n % 3, TP * j:TP * (j + 1)],
                                              ident[0:TP, 0:TP])
                ins.then_inc(AT_ps, 1)

            for n in range(20):
                i, h = n // 4, n % 4
                if n >= 2:
                    pe.wait_ge(S_used, n - 1)
                r = 64 * (h % 2)
                for a, b in ((0, 512), (512, N)):
                    ins = nc.tensor.matmul(flat(2 * (n % 2))[0:TP, a:b], gqkT[r:r + 64, h // 2, i * TP:(i + 1) * TP],
                                           gqkT[r:r + 64, 2 + h // 2, a:b], start=True, stop=True)
                ins.then_inc(S_ps, 1)
                if n >= 2:
                    gnn_T(n - 2)
                if h == 0:
                    if i >= 2:
                        pe.wait_ge(O_used, i - 1)
                    for k in range(KC):
                        nc.tensor.matmul(ps[0:TP, 6 + i % 2, 256:512], xnT[:, k, i * TP:(i + 1) * TP], M2[:, k, :],
                                         start=(k == 0), stop=(k == KC - 1))
                if n >= 3:
                    gnn_AV(n - 3)
            gnn_T(18)
            gnn_AV(17)
            gnn_T(19)
            gnn_AV(18)
            gnn_AV(19)
            pe.wait_ge(ld_ffn, 64)
            pe.wait_ge(S_used, 20)
            for i in range(NT):
                pe.wait_ge(h_done, i + 1)
                if i >= 2:
                    pe.wait_ge(hT_done, i - 1)
                two_transposes(i % 2, hrow[:, i, :]).then_inc(hT_ps, 1)

            def qkT(i):
                pe.wait_ge(qkr_done, i + 1)
                if i >= 2:
                    pe.wait_ge(qkT_done, i - 1)
                for m in range(3):
                    ins = nc.tensor.transpose(ps[:, 4 + i % 2, 128 * m:128 * m + TP], qkr[:, 128 * m:128 * (m + 1)],
                                              ident[0:TP, 0:TP])
                ins.then_inc(qkT_ps, 1)

            for i in range(NT):
                pe.wait_ge(hT_done, i + 1)
                if i >= 2:
                    pe.wait_ge(qkv_used, i - 1)
                    pe.wait_ge(vc_done, i - 1)
                for k in range(KC):
                    ins = nc.tensor.matmul(ps[0:TP, 2 + i % 2, :], xnT[:, k, i * TP:(i + 1) * TP], wqkv[:, k, :],
                                           start=(k == 0), stop=(k == KC - 1))
                ins.then_inc(qkv_ps, 1)
                if i:
                    qkT(i - 1)
            qkT(NT - 1)
            pe.wait_ge(qkT_done, NT)
            pe.wait_ge(vc_done, NT)
            pe.wait_ge(qkv_used, NT)

            def ffn_T(n):
                pe.wait_ge(exp2_done, n + 1)
                if n >= 1:
                    pe.wait_ge(ET_done, n)
                for j in range(n // 4 + 1):
                    ins = nc.tensor.transpose(flat(4)[0:TP, 128 * j:128 * j + TP], E[:, n % 3, TP * j:TP * (j + 1)],
                                              ident[0:TP, 0:TP])
                ins.then_inc(ET_ps, 1)

            def ffn_AV(n):
                i, h = n // 4, n % 4
                pe.wait_ge(ET_done, n + 1)
                if h == 0 and i:
                    pe.wait_ge(O2_used, i)
                for j in range(i + 1):
                    ins = nc.tensor.matmul(ps[0:TP, 6, C * h:C * (h + 1)], AT[:, n % 2, j, :],
                                           Vc[:, j, C * (h // 2):C * (h // 2) + C], start=(j == 0), stop=(j == i))
                ins.then_inc(AV2_done, 1)

            def ffn_yT(i):
                pe.wait_ge(y_done, i + 1)
                if i:
                    pe.wait_ge(x2_done, i)
                two_transposes(7, yat[:, i % 2, :]).then_inc(yT_ps, 1)

            def ffn_wo(i):
                pe.wait_ge(yT_done, i + 1)
                if i:
                    pe.wait_ge(x2_done, i)
                for k in range(KC):
                    ins = nc.tensor.matmul(ps[0:TP, 7, 256:512], yT[:, i % 2, k, :], wo[:, k, :],
                                           start=(k == 0), stop=(k == KC - 1))
                ins.then_inc(wo_ps, 1)

            for n in range(20):
                i, h = n // 4, n % 4
                if n >= 2:
                    pe.wait_ge(exp2_done, n - 1)
                w = TP * (i + 1)
                r = 64 * (h // 2)
                S = flat(2 * (n % 2))[0:TP, :]
                q = QKT[r:r + 64, h % 2, i * TP:(i + 1) * TP]
                edges = [0, w - TP, w] if w > 512 else [0, w]
                for a, b in zip(edges, edges[1:]):
                    b1 = min(b, 512)
                    last = b == w
                    if a < b1:
                        nc.tensor.matmul(S[:, a:b1], q, QKT[r:r + 64, 2, a:b1], start=True,
                                         stop=not (last and b1 <= 512), skip_group_check=True)
                    if b > 512:
                        nc.tensor.matmul(S[:, 512:b], q, QKT[r:r + 64, 2, 512:b], start=True, stop=False,
                                         skip_group_check=True)
                for a, b in ((w - TP, min(w, 512)), (512, w)):
                    if a < b:
                        ins = nc.tensor.matmul(S[:, a:b], identb, causal[:, a - (w - TP):b - (w - TP)], start=False,
                                               stop=True, skip_group_check=True)
                ins.then_inc(S2_ps, 1)
                if n >= 2:
                    ffn_T(n - 2)
                if n >= 3:
                    ffn_AV(n - 3)
                if n >= 8 and h == 0:
                    ffn_yT(i - 2)
                if n >= 8 and h == 2:
                    ffn_wo(i - 2)
            ffn_T(18)
            ffn_AV(17)
            ffn_T(19)
            ffn_yT(3)
            ffn_AV(18)
            ffn_AV(19)
            ffn_wo(3)
            ffn_yT(4)
            ffn_wo(4)
            for i in range(NT):
                pe.wait_ge(flat_done, i + 1)
                if i >= 2:
                    pe.wait_ge(flatT_done, i - 1)
                two_transposes(i % 2, hrow[:, i, :]).then_inc(flatT_ps, 1)
            for i in range(NT):
                pe.wait_ge(flatT_done, i + 1)
                for k in range(KC):
                    ins = nc.tensor.matmul(ps[0:TP, 2, NE * i:NE * (i + 1)], xnT[:, k, i * TP:(i + 1) * TP], wr[:, k, :],
                                           start=(k == 0), stop=(k == KC - 1))
            ins.then_inc(logit_ps, 1)
            pe.wait_ge(sel_done, 1)
            sel = rt[:, 840:860].bitcast(bf16).rearrange("p (i e) -> p i e", i=NT)
            for i in range(NT):
                for j in range(i + 1):
                    nc.tensor.matmul(ps[0:TP, 3, NE * i:NE * (i + 1)], tri if j == i else ones, sel[:, j, :],
                                     start=(j == 0), stop=(j == i))
            for j in range(NT):
                ins = nc.tensor.matmul(ps[0:TP, 3, 64:64 + NE], ones, sel[:, j, :], start=(j == 0), stop=(j == NT - 1))
            ins.then_inc(rank_ps, 1)

            def up_gate(s, u, j, e):
                if not isinstance(s, int):
                    pe.wait_ge(g_done, 2 * s + j - 1)
                for g in range(2):
                    for k in range(KC):
                        w = W13[:, bass.ds(e, 1), k, HID * g + HH * j:HID * g + HH * (j + 1)].rearrange("p a n -> p (a n)")
                        ins = nc.tensor.matmul(ps[:, 2 * j + g, 0:HH], xTb[:, u, k, :], w,
                                               start=(k == 0), stop=(k == KC - 1))
                ins.then_inc(ab_ps, 1)

            def gT(s, u):
                for j in range(2):
                    pe.wait_ge(g_done, 2 * s + j + 1)
                    for c in range(HC):
                        ins = nc.tensor.transpose(ps[0:HCW[c], 4 + j, 128 * c:128 * (c + 1)],
                                                  gb[:, u, j, 128 * c:128 * c + HCW[c]], ident)
                    ins.then_inc(gT_ps, 1)

            def down(s, e):
                pe.wait_ge(y_copied, s + 1)
                for j in range(2):
                    pe.wait_ge(gT_copied, 2 * s + j + 1)
                    for c in range(HC):
                        w = W2[0:HCW[c], bass.ds(e, 1), HC * j + c, :].rearrange("p a n -> p (a n)")
                        ins = nc.tensor.matmul(ps[:, 6, 0:D], hTb[0:HCW[c], j, c, :], w,
                                               start=(j == 0 and c == 0), stop=(j == 1 and c == HC - 1))
                ins.then_inc(y_ps, 1)

            def expert(s):
                return pe.value_load(blki[0:1, bass.ds(s, 1)], min_val=0, max_val=NE - 1)

            pe.wait_ge(blk_done, 1)
            pe.wait_ge(y_done, NT)
            pe.wait_ge(ET_done, 20)
            pe.wait_ge(x2_done, NT)
            pe.wait_ge(ld_w, 16 * (NE - NLATE))
            pe.wait_ge(ld_late, 16 * (4 * NE + NLATE))
            nc.tensor.matmul(ps[:, 4, :], zero16[:, 0:128], zero16, start=True, stop=True)
            nc.tensor.matmul(ps[:, 5, :], zero16[:, 0:128], zero16, start=True, stop=True)
            iters = pe.value_load(blki[0:1, NB:NB + 1], min_val=1, max_val=(MAXB - 1) // 2)
            pe.wait_ge(xblk_ld[0], 16)
            two_transposes(7, xblk[:, 0, :], 128).then_inc(mxT_ps, 1)
            e0 = expert(0)
            pe.wait_ge(mxT_done, 1)
            up_gate(0, 0, 0, e0)
            pe.wait_ge(xblk_ld[1], 16)
            two_transposes(7, xblk[:, 1, :], 128).then_inc(mxT_ps, 1)
            up_gate(0, 0, 1, e0)
            with pe.Fori(0, iters) as m:
                for u, s in ((1, 2 * m + 1), (0, 2 * m + 2)):
                    e = expert(s)
                    pe.wait_ge(mxT_done, s + 1)
                    up_gate(s, u, 0, e)
                    pe.wait_ge(xblk_ld[1 - u], 16 * m + 32)
                    two_transposes(7, xblk[:, 1 - u, :], 128).then_inc(mxT_ps, 1)
                    gT(s - 1, 1 - u)
                    up_gate(s, u, 1, e)
                    e_last = expert(s - 1)
                    down(s - 1, e_last)
            gT(2 * iters, 0)
            down(2 * iters, expert(2 * iters))

        @block.vector
        def _(dve):
            steps = [0]

            def link(ins):
                steps[0] += 1
                ins.then_inc(link_dve, 1)
                dve.wait_ge(link_dve, steps[0])

            def stats(src):
                for i in range(NT):
                    ins = nc.vector.bn_stats(st[:, i, :], src[:, i, :])
                link(ins)
                for i in range(NT):
                    ins = nc.vector.bn_aggr(mv[:, i, :], st[:, i, :])
                link(ins)
                return nc.vector.tensor_scalar(v_eps[:, :], mv[:, :, 1], EPS, None, ALU.add)

            dve.wait_ge(ld_x, 16)
            stats(X).then_inc(var1, 1)
            dve.wait_ge(ld_edges, 80)
            nc.vector.tensor_reduce(gmm[:, 0:1], edgesg, AX.X, ALU.min)
            nc.vector.tensor_reduce(gmm[:, 1:2], edgesg, AX.X, ALU.max).then_inc(gmm_done, 1)
            dve.wait_ge(rstd1, 1)
            for i in range(NT):
                nc.vector.tensor_scalar(xn[:, i, :], X[:, i, :], mv[:, i, 0:1], rstd[:, i:i + 1],
                                        ALU.subtract, ALU.mult).then_inc(xn_done, 1)
            nc.vector.tensor_copy(srcf, srci)
            link(nc.vector.tensor_copy(dstf, dsti))
            for b in range(NT):
                ins = nc.vector.tensor_scalar(dstrel[:, b, :], dstf, float(TP * b), None, ALU.subtract)
            link(ins)
            for i in range(NT):
                dve.wait_ge(vs_ps, i + 1)
                nc.vector.tensor_tensor(VS[:, i, :], ps[0:TP, 6 + i % 2, :], bvs, ALU.add).then_inc(vs_done, 1)
            dve.wait_ge(gmm_ps, 1)
            g = rr[:, 0:80].rearrange("p (k g) -> p k g", k=2)
            link(nc.vector.tensor_copy(rr[:, 0:80], ps[0:1, 0, 0:80]))
            r1 = rr[:, 80:280].rearrange("p (b g) -> p b g", b=NT)
            r2_ = rr[:, 280:480].rearrange("p (b g) -> p b g", b=NT)
            lo = crow[:, 0:200].rearrange("p (b g) -> p b g", b=NT)
            hi = crow[:, 200:400].rearrange("p (b g) -> p b g", b=NT)
            up = crow[:, 400:440].unsqueeze(1).to_broadcast([1, NT, NG])
            down_ = crow[:, 440:480].unsqueeze(1).to_broadcast([1, NT, NG])
            nc.vector.tensor_tensor(r1, hi, g[:, 0:1, :].to_broadcast([1, NT, NG]), ALU.is_ge)
            link(nc.vector.tensor_tensor(r2_, lo, g[:, 1:2, :].to_broadcast([1, NT, NG]), ALU.is_le))
            link(nc.vector.tensor_tensor(r1, r1, r2_, ALU.mult))
            r3_ = rr[:, 480:680].rearrange("p (b g) -> p b g", b=NT)
            nc.vector.tensor_tensor(r2_, r1, down_, ALU.mult)
            link(nc.vector.tensor_tensor(r3_, r1, up, ALU.mult))
            nc.vector.tensor_reduce(rr[:, 700:705], r2_, AX.X, ALU.max)
            link(nc.vector.tensor_reduce(rr[:, 705:710], r3_, AX.X, ALU.max))
            link(nc.vector.tensor_scalar(rr[:, 710:715], rr[:, 700:705], -1.0, float(NG), ALU.mult, ALU.add))
            link(nc.vector.tensor_scalar(rr[:, 710:715], rr[:, 710:715], float(NG - 1), None, ALU.min))
            link(nc.vector.tensor_scalar(rr[:, 715:720], rr[:, 710:715], 1.0, None, ALU.add))
            link(nc.vector.tensor_tensor(rr[:, 715:720], rr[:, 715:720], rr[:, 705:710], ALU.max))
            nc.vector.tensor_copy(rangei[:, :, :].rearrange("p k b -> p (k b)"), rr[:, 710:720]).then_inc(range_done, 1)
            dve.wait_ge(range_done, 1)
            seq = dve.alloc_register("dve_tiles")
            dve.reg_mov(seq, 0)
            dve.sem_inc(oh_used, EG)
            for b in range(NT):
                first = dve.value_load(rangei[0:1, 0, b:b + 1], min_val=0, max_val=NG - 1)
                last = dve.value_load(rangei[0:1, 1, b:b + 1], min_val=1, max_val=NG)
                with dve.Fori(first, last) as gi:
                    done = dve.snap(seq, min_val=0, max_val=NT * ET)
                    for k in range(EG):
                        dve.wait_ge(oh_used, done + (k + 1))
                        nc.vector.tensor_scalar(oh_src[:, k, 0:N], iota16, srcf[:, bass.ds(EG * gi + k, 1)], None,
                                                ALU.is_equal)
                        nc.vector.tensor_scalar(oh_dst[:, k, :], iota16[:, 0:128],
                                                dstrel[:, b, bass.ds(EG * gi + k, 1)], None,
                                                ALU.is_equal).then_inc(oh_built, 1)
                    dve.reg_add(seq, seq, EG)
            dve.wait_ge(ld_mix, 48)
            link(nc.vector.tensor_reduce(wmean[:, :], wkv.rearrange("p k (h c) -> p (k h) c", c=C), AX.X, ALU.add))
            link(nc.vector.tensor_scalar(wmean[:, :], wmean[:, :], 1.0 / C, None, ALU.mult))
            wk3 = wkv.rearrange("p k (h c) -> p (k h) c", c=C)
            nc.vector.tensor_tensor(wk3, wk3, wmean[:, :].unsqueeze(2).to_broadcast([128, 32, C]),
                                    ALU.subtract).then_inc(wkv_centred, 1)
            dve.wait_ge(cnt_done, NT + 2)
            for i in range(NT):
                nc.vector.tensor_scalar(edge_mask[:, i, :], cnt[:, i, :], 0.0, BIG, ALU.is_equal, ALU.mult)
            for i in range(NT):
                dve.wait_ge(sq_done, i + 1)
                nc.vector.tensor_reduce(ss[:, i, :], sq.rearrange("p (h c) -> p h c", c=C), AX.X, ALU.add).then_inc(sq_used, 1)
            dve.wait_ge(sq_used, NT)
            link(nc.vector.tensor_scalar(ss[:, :, :], ss[:, :, :], 1.0 / C, EPS, ALU.mult, ALU.add))
            nc.vector.tensor_tensor(ssp[:, :, :], ss[:, :, 0:8], ss[:, :, 8:16], ALU.mult).then_inc(ssp_done, 1)
            dve.wait_ge(rkv_done, 1)
            dve.wait_ge(kv_copied, NT)
            for i in range(NT):
                kk = kvc[0:TP, i, 0:512].rearrange("p (h c) -> p h c", c=C)
                nc.vector.tensor_tensor(kk, kk, rkv[:, i, :].unsqueeze(2).to_broadcast([TP, MH, C]),
                                        ALU.mult).then_inc(kv_normed, 1)
            dve.wait_ge(dots_ps, 1)
            dve.wait_ge(consts_set, 4)
            for r in (0, 64):
                ins = nc.vector.tensor_scalar(dbd[r:r + 64, :, r:r + 64],
                                              ps[r:r + 64, 4, :].rearrange("p (e n) -> p e n", e=4)[:, :, r:r + 64],
                                              1.0 / N, None, ALU.mult)
            ins.then_inc(dbd_done, 1)

            def gnn_weigh(n):
                dve.wait_ge(exp_done, n + 1)
                nc.vector.tensor_tensor_reduce(out=E[:, n % 3, :], in0=E[:, n % 3, :], in1=cnt[:, n // 4, :], scale=1.0,
                                               scalar=0.0, op0=ALU.mult, op1=ALU.add,
                                               accum_out=den[:, n:n + 1]).then_inc(A_done, 1)

            def gnn_out(i):
                dve.wait_ge(A_done, 4 * i + 4)
                link(nc.vector.tensor_scalar(rd[:, :], den[:, 4 * i:4 * i + 4], 1e-16, None, ALU.add))
                link(nc.vector.reciprocal(rd[:, :], rd[:, :]))
                dve.wait_ge(AV_done, 4 * i + 4)
                o = ps[0:TP, 6 + i % 2, :]
                link(nc.vector.tensor_tensor(hrow[:, i, :].rearrange("p (h c) -> p h c", c=C),
                                             o[:, 0:256].rearrange("p (h c) -> p h c", c=C),
                                             rd[:, :].unsqueeze(2).to_broadcast([TP, H, C]), ALU.mult))
                nc.vector.tensor_tensor(VS[:, i, D:512], VS[:, i, D:512], hrow[:, i, :], ALU.add).then_inc(agg_done, 1)
                dve.wait_ge(xb_done, NT)
                nc.vector.tensor_tensor(x1[:, i, :], o[:, 256:512], x1[:, i, :], ALU.add).then_inc(O_used, 1)

            for n in range(20):
                i = n // 4
                dve.wait_ge(S_ps, n + 1)
                if n >= 3:
                    dve.wait_ge(AT_ps, n - 2)
                nc.vector.tensor_tensor_reduce(out=E[:, n % 3, :], in0=flat(2 * (n % 2))[0:TP, 0:N],
                                               in1=edge_mask[:, i, :], scale=1.0, scalar=3e38, op0=ALU.add, op1=ALU.min,
                                               accum_out=mn[:, n:n + 1]).then_inc(S_used, 1)
                if n:
                    gnn_weigh(n - 1)
                if n % 4 == 3 and n > 4:
                    gnn_out(i - 1)
            gnn_weigh(19)
            gnn_out(NT - 1)
            dve.wait_ge(gelu_done, 1)
            dve.wait_ge(O_used, NT)
            stats(VS[:, :, D:512]).then_inc(varg, 1)
            dve.wait_ge(rstdg, 1)
            for i in range(NT):
                ins = nc.vector.scalar_tensor_tensor(out=hrow[:, i, :], in0=VS[:, i, D:512], scalar=mv[:, i, 0:1],
                                                     in1=gamma, op0=ALU.subtract, op1=ALU.mult)
            link(ins)
            for i in range(NT):
                ins = nc.vector.scalar_tensor_tensor(out=x1[:, i, :], in0=hrow[:, i, :], scalar=rstd[:, i:i + 1],
                                                     in1=x1[:, i, :], op0=ALU.mult, op1=ALU.add)
            link(ins)
            stats(x1).then_inc(var2, 1)
            dve.wait_ge(r2, 1)
            link(nc.vector.tensor_tensor(rt[:, 10:15], rstd[:, :], rstd[:, :], ALU.mult))
            link(nc.vector.tensor_tensor(rt[:, 15:20], rt[:, 10:15], mv[:, :, 1], ALU.mult))
            nc.vector.tensor_scalar(rt[:, 5:10], rt[:, 15:20], EPS_RMS, None, ALU.add).then_inc(ms2, 1)
            for i in range(NT):
                nc.vector.tensor_scalar(xn[:, i, :], x1[:, i, :], mv[:, i, 0:1], rstd[:, i:i + 1], ALU.subtract, ALU.mult)
            dve.wait_ge(hr, 1)
            link(nc.vector.tensor_tensor(rt[:, 20:25], rt[:, 0:5], rstd[:, :], ALU.mult))
            for i in range(NT):
                nc.vector.tensor_scalar(hrow[:, i, :], x1[:, i, :], mv[:, i, 0:1], rt[:, 20 + i:21 + i],
                                        ALU.subtract, ALU.mult).then_inc(h_done, 1)
            rot = rt[:, 64:64 + 768].rearrange("p (k n) -> p k n", k=2)
            for i in range(NT):
                dve.wait_ge(qkv_ps, i + 1)
                qk = ps[0:TP, 2 + i % 2, 0:384].rearrange("p (h s c) -> p h s c", h=6, s=2)
                ra = rot[:, 0, :].rearrange("p (h s c) -> p h s c", h=6, s=2)
                rb = rot[:, 1, :].rearrange("p (h s c) -> p h s c", h=6, s=2)
                cos = rope[:, 0, i, :].unsqueeze(1).to_broadcast([TP, 6, C])
                sin = rope[:, 1, i, :].rearrange("p (s c) -> p s c", s=2)
                nc.vector.tensor_tensor(rot[:, 0, :].rearrange("p (h c) -> p h c", h=6),
                                        ps[0:TP, 2 + i % 2, 0:384].rearrange("p (h c) -> p h c", h=6), cos, ALU.mult)
                for a in range(2):
                    ins = nc.vector.tensor_tensor(rb[:, :, a, :], qk[:, :, 1 - a, :],
                                                  sin[:, a:a + 1, :].to_broadcast([TP, 6, 32]), ALU.mult)
                ins.then_inc(qkv_used, 1)
                dve.wait_ge(qkv_used, i + 1)
                if i:
                    dve.wait_ge(qkT_ps, i)
                nc.vector.tensor_tensor(qkr, rot[:, 0, :], rot[:, 1, :], ALU.add).then_inc(qkr_done, 1)
                dve.wait_ge(qkr_done, i + 1)

            def ffn_y(i):
                dve.wait_ge(exp2_done, 4 * i + 4)
                link(nc.vector.reciprocal(rd[:, :], den2[:, 4 * i:4 * i + 4]))
                dve.wait_ge(AV2_done, 4 * i + 4)
                nc.vector.tensor_tensor(yat[:, i % 2, :].rearrange("p (h c) -> p h c", c=C),
                                        ps[0:TP, 6, 0:256].rearrange("p (h c) -> p h c", c=C),
                                        rd[:, :].unsqueeze(2).to_broadcast([TP, H, C]), ALU.mult).then_inc(y_done, 1)
                dve.wait_ge(y_done, i + 1)
                dve.sem_inc(O2_used, 1)

            def ffn_x2(i):
                dve.wait_ge(wo_ps, i + 1)
                nc.vector.tensor_tensor(xn[:, i, :], ps[0:TP, 7, 256:512], xn[:, i, :], ALU.add).then_inc(x2_done, 1)

            for n in range(20):
                i = n // 4
                dve.wait_ge(S2_ps, n + 1)
                nc.vector.tensor_reduce(mn2[:, n:n + 1], flat(2 * (n % 2))[0:TP, 0:TP * (i + 1)], AX.X, ALU.max,
                                        negate=True).then_inc(max2_done, 1)
                if n % 4 == 3 and n > 4:
                    ffn_y(i - 1)
                if n % 4 == 3 and n >= 11:
                    ffn_x2(i - 2)
            ffn_y(4)
            ffn_x2(3)
            ffn_x2(4)
            dve.wait_ge(x2_done, NT)
            for i in range(NT):
                ins = nc.vector.tensor_tensor_reduce(out=hrow[:, i, :], in0=xn[:, i, :], in1=xn[:, i, :], scale=1.0 / D,
                                                     scalar=0.0, op0=ALU.mult, op1=ALU.add, accum_out=rt[:, 30 + i:31 + i])
            link(ins)
            nc.vector.tensor_scalar(v_eps[:, :], rt[:, 30:35], EPS_RMS, None, ALU.add).then_inc(ms3, 1)
            dve.wait_ge(r3, 1)
            for i in range(NT):
                nc.vector.scalar_tensor_tensor(out=hrow[:, i, :], in0=xn[:, i, :], scalar=rstd[:, i:i + 1], in1=ln2,
                                               op0=ALU.mult, op1=ALU.mult).then_inc(flat_done, 1)
            dve.wait_ge(logit_ps, 1)
            dve.wait_ge(qkT_ps, NT)

            def t3(a, n=NE):
                return rt[:, a:a + NT * n].rearrange("p (i e) -> p i e", i=NT)

            def bc(a):
                return rt[:, a:a + NT].unsqueeze(2).to_broadcast([TP, NT, NE])

            lg = ps[0:TP, 2, 0:40].rearrange("p (i e) -> p i e", i=NT)
            link(nc.vector.tensor_reduce(rt[:, 35:40], lg, AX.X, ALU.max))
            nc.vector.tensor_tensor(t3(64), lg, bc(35), ALU.subtract).then_inc(rmax_done, 1)
            dve.wait_ge(rexp_done, 1)
            link(nc.vector.tensor_reduce(rt[:, 40:45], t3(64), AX.X, ALU.add))
            link(nc.vector.reciprocal(rt[:, 40:45], rt[:, 40:45]))
            link(nc.vector.tensor_tensor(t3(64), t3(64), bc(40), ALU.mult))
            for i in range(NT):
                ins = nc.vector.max(out=rt[:, 104 + 8 * i:112 + 8 * i], in_=rt[:, 64 + 8 * i:72 + 8 * i])
            link(ins)
            for i in range(NT):
                ins = nc.vector.max_index(out=rti[:, 8 * i:8 * i + 8], in_max=rt[:, 104 + 8 * i:112 + 8 * i],
                                          in_values=rt[:, 64 + 8 * i:72 + 8 * i])
            link(ins)
            link(nc.vector.tensor_copy(rt[:, 144:184], rti[:, 0:40]))
            top, idx = t3(104), t3(144)
            io = iota8.unsqueeze(1).to_broadcast([TP, NT, NE])
            nc.vector.tensor_tensor(t3(184), io, idx[:, :, 0:1].to_broadcast([TP, NT, NE]), ALU.is_equal)
            link(nc.vector.tensor_tensor(t3(224), io, idx[:, :, 1:2].to_broadcast([TP, NT, NE]), ALU.is_equal))
            nc.vector.tensor_tensor(rt[:, 840:860].bitcast(bf16).rearrange("p (i e) -> p i e", i=NT), t3(184), t3(224),
                                    ALU.add).then_inc(sel_done, 1)
            link(nc.vector.tensor_tensor(rt[:, 45:50], top[:, :, 0], top[:, :, 1], ALU.add))
            link(nc.vector.tensor_scalar(rt[:, 45:50], rt[:, 45:50], 1e-9, None, ALU.add))
            link(nc.vector.reciprocal(rt[:, 45:50], rt[:, 45:50]))
            nc.vector.tensor_tensor(rt[:, 50:55], top[:, :, 0], rt[:, 45:50], ALU.mult)
            nc.vector.tensor_tensor(rt[:, 55:60], top[:, :, 1], rt[:, 45:50], ALU.mult)
            dve.wait_ge(rank_ps, 1)
            tot = ps[0:TP, 3, 64:72]
            link(nc.vector.tensor_tensor(rt[:, 264:304].rearrange("p (e k) -> p e k", e=NE),
                                         tot.unsqueeze(2).to_broadcast([TP, NE, 5]),
                                         thr.unsqueeze(1).to_broadcast([TP, NE, 5]), ALU.is_gt))
            link(nc.vector.tensor_reduce(rt[:, 304:312], rt[:, 264:304].rearrange("p (e k) -> p e k", e=NE), AX.X, ALU.add))
            link(nc.vector.tensor_tensor_scan(rt[:, 312:320], cf[0:TP, 160:168], rt[:, 304:312], 0.0,
                                              ALU.mult, ALU.add))
            link(nc.vector.tensor_tensor(rt[:, 320:328], rt[:, 312:320], rt[:, 304:312], ALU.subtract))
            link(nc.vector.tensor_scalar(rt[:, 320:328], rt[:, 320:328], 128.0, None, ALU.mult))
            link(nc.vector.tensor_tensor(t3(328), ps[0:TP, 3, 0:40].rearrange("p (i e) -> p i e", i=NT),
                                         rt[:, 320:328].unsqueeze(1).to_broadcast([TP, NT, NE]), ALU.add))
            nc.vector.tensor_tensor(t3(184), t3(184), t3(328), ALU.mult)
            link(nc.vector.tensor_tensor(t3(224), t3(224), t3(328), ALU.mult))
            nc.vector.tensor_reduce(rt[:, 370:375], t3(184), AX.X, ALU.add)
            link(nc.vector.tensor_reduce(rt[:, 375:380], t3(224), AX.X, ALU.add))
            nc.vector.tensor_copy(rti[:, 40:50], rt[:, 370:380]).then_inc(slot_done, 1)
            e_of = rr[:, 720:720 + NB * NE].rearrange("p (g e) -> p g e", g=NB)
            link(nc.vector.tensor_tensor(e_of, rt[0:1, 312:320].unsqueeze(1).to_broadcast([1, NB, NE]),
                                         crow[:, 480:480 + NB].unsqueeze(2).to_broadcast([1, NB, NE]), ALU.is_le))
            link(nc.vector.tensor_reduce(rr[:, 880:880 + NB], e_of, AX.X, ALU.add))
            link(nc.vector.tensor_scalar(rr[:, 880:880 + NB], rr[:, 880:880 + NB], float(NE - 1), None, ALU.min))
            link(nc.vector.tensor_tensor(rr[:, 910:918], rt[0:1, 319:320].to_broadcast([1, 8]), crow[:, 500:508], ALU.is_gt))
            link(nc.vector.tensor_reduce(rr[:, 880 + NB:881 + NB], rr[:, 910:918], AX.X, ALU.add))
            nc.vector.tensor_copy(blki[:, 0:NB + 1], rr[:, 880:881 + NB]).then_inc(blk_done, 1)
            dve.wait_ge(blk_done, 1)

            def gate(s, u, j):
                dve.wait_ge(silu_done, 2 * s + j + 1)
                nc.vector.tensor_tensor(gb[:, u, j, :], ps[:, 2 * j + 1, 0:HH], sl[:, j, :], ALU.mult).then_inc(g_done, 1)

            iters = dve.value_load(blki[0:1, NB:NB + 1], min_val=1, max_val=(MAXB - 1) // 2)
            dve.sem_inc(y_copied, 1)
            dve.sem_inc(y_free, 2)

            def y_copy(s, u):
                dve.wait_ge(y_ps, s + 1)
                dve.wait_ge(y_free, s + 1)
                nc.vector.tensor_copy(yb[:, u, :], ps[:, 6, 0:D]).then_inc(y_copied, 1)

            gate(0, 0, 0)
            gate(0, 0, 1)
            with dve.Fori(0, iters) as m:
                for u, s in ((1, 2 * m + 1), (0, 2 * m + 2)):
                    gate(s, u, 0)
                    gate(s, u, 1)
                    y_copy(s - 1, 1 - u)
            y_copy(2 * iters, 0)
            for i in range(NT):
                ins = nc.vector.tensor_tensor(x1[:, i, :], x1[:, i, :], xn[:, i, :], ALU.add)
            link(ins)
            for i in range(NT):
                dve.wait_ge(y_gathered, 16 * 2 * NT)
                link(nc.vector.scalar_tensor_tensor(out=x1[:, i, :], in0=Y1[:, i, :], scalar=rt[:, 50 + i:51 + i],
                                                    in1=x1[:, i, :], op0=ALU.mult, op1=ALU.add))
                nc.vector.scalar_tensor_tensor(out=x1[:, i, :], in0=Y2[:, i, :], scalar=rt[:, 55 + i:56 + i],
                                               in1=x1[:, i, :], op0=ALU.mult, op1=ALU.add).then_inc(out_done, 1)


def laid_out(a):
    def cols(w):
        n, k = w.shape
        return w.T.reshape(k // 128, 128, n).transpose(1, 0, 2)

    def krows(w):
        k, n = w.shape
        return w.reshape(k // 128, 128, n).transpose(1, 0, 2)

    g = "L0_gnn_"
    f = "L0_ffn_"
    src, dst = a["src"], a["dst"]
    wq = a[f + "wq"].reshape(H, C, D)[[0, 2, 1, 3]].reshape(D, D)
    mix = a["L0_mix_w_qkv"]
    w13 = np.concatenate([a[f + "w1"], a[f + "w3"]], axis=1)
    ident = np.eye(128, dtype=np.float32)
    c_f32 = np.zeros((128, 288), np.float32)
    c_f32[:, 0:128] = ident
    c_f32[:, 128:136] = np.arange(8)
    c_f32[:, 136:141] = np.arange(5) * 128
    c_f32[:, 160:168] = 1.0
    bf = mybir.dt.np(bf16)
    r = np.arange(128)
    c_bf = np.zeros((128, 512), np.float32)
    c_bf[:, 0:128] = r[:, None] < r[None, :]
    c_bf[:, 128:256] = 1.0
    c_bf[:, 256:384] = ident
    c_bf[:, 384:512] = np.where(r[None, :] > r[:, None], -BIG, 0.0)
    inv_freq = 1.0 / 10000.0 ** (np.arange(0, C, 2, dtype=np.float32) / C)
    freqs = np.outer(np.arange(N, dtype=np.float32), inv_freq)
    cos, sin = np.cos(freqs), np.sin(freqs)
    c_rope = np.stack([np.concatenate([cos, cos], 1), np.concatenate([-sin, sin], 1)])
    c_row = np.zeros((1, 512), np.float32)
    b = np.arange(NT)
    c_row[0, 0:200] = np.repeat(TP * b, NG)
    c_row[0, 200:400] = np.repeat(TP * b + TP - 1, NG)
    c_row[0, 400:440] = np.arange(NG) + 1
    c_row[0, 440:480] = NG - np.arange(NG)
    c_row[0, 480:480 + NB] = np.arange(NB)
    c_row[0, 500:508] = 2 * np.arange(8) + 1
    return dict(
        x_in=a["x"],
        edge_groups=dst.reshape(NG, EG * TP),
        edge_src=src.reshape(ET, TP).T,
        edge_dst=dst.reshape(ET, TP).T,
        w_gnn=krows(np.concatenate([a[g + "Wq"], a[g + "Wk"], a[g + "Wv"], a[g + "Wskip"]], axis=1)),
        b_gnn_qk=np.concatenate([a[g + "bq"], a[g + "bk"]]).reshape(4, 128).T,
        b_gnn_vs=np.concatenate([a[g + "bv"], a[g + "bskip"]]),
        w_mix_kv=cols(mix[MI:3 * MI]),
        w_mix_q=mix[0:MI].reshape(4, 128, D).transpose(1, 0, 2),
        w_mix_out=cols(a["L0_mix_w_out"]),
        rows=np.stack([a[g + "gamma"], a[g + "beta_ln"], a["L0_mix_b_out"], a[f + "ln2_w"]]),
        w_ffn_qkv=cols(np.concatenate([wq, a[f + "wk"], a[f + "wv"]])),
        w_ffn_o=cols(a[f + "wo"]),
        ln1_col=a[f + "ln1_w"].reshape(KC, 128).T,
        w_router=cols(a[f + "router_w"]),
        w13=w13.transpose(0, 2, 1).reshape(NE, KC, 128, 2 * HID).transpose(2, 0, 1, 3),
        w2=a[f + "w2"].transpose(0, 2, 1),
        c_f32=c_f32,
        c_bf16=c_bf.astype(bf),
        c_iota=np.arange(N).astype(np.float16),
        c_rope=c_rope.reshape(2, NT, TP, C).transpose(2, 0, 1, 3).astype(np.float32),
        c_row=c_row,
    )


def kernel(**inputs):
    import concourse.bacc as _bacc
    from concourse.bass_utils import run_bass_kernel_spmd as _run

    nc = _bacc.Bacc("TRN2", target_bir_lowering=False, num_devices=1)
    arrays = {k: np.ascontiguousarray(v) for k, v in laid_out({k: np.asarray(v) for k, v in inputs.items()}).items()}
    args = [nc.dram_tensor(k, v.shape, mybir.dt.from_np(v.dtype), kind="ExternalInput").ap() for k, v in arrays.items()]
    args.append(nc.dram_tensor("out", (N, D), fp32, kind="ExternalOutput").ap())
    build(nc, *args)
    r = _run(nc, [arrays], core_ids=[0])
    return r.results[0]["out"]
```

```python
import numpy as np
import concourse.bass as bass
from concourse import mybir
from contextlib import ExitStack

fp32 = mybir.dt.float32
bf16 = mybir.dt.bfloat16
fp16 = mybir.dt.float16
i32 = mybir.dt.int32
u32 = mybir.dt.uint32
ALU = mybir.AluOpType
ACT = mybir.ActivationFunctionType
AX = mybir.AxisListType

N, D = 625, 256
NT, TP = 5, 125
KC = D // 128
H, C = 4, 64
EDGES = 20000
ET = EDGES // TP
EG = 8
NG = ET // EG
SLOTS = 2
MH = 8
MI = MH * C
NE, HID = 8, 682
HH = HID // 2
HC = 3
HCW = (128, 128, HH - 256)
MAXB = 17
NB = MAXB + 1
CAP = 640
RW = D + 2
XROWS = NE * CAP + 128
EPS = 1e-5
EPS_RMS = 1e-6
BIG = 1e30


def build(nc, x, edge_groups, edge_src, edge_dst, w_gnn, b_gnn_qk, b_gnn_vs, w_mix_kv, w_mix_q,
          w_mix_out, rows, w_ffn_qkv, w_ffn_o, ln1_col, w_router, w13, w2, c_f32, c_bf16, c_iota,
          c_rope, c_row, c_pad, out):
    xg = nc.dram_tensor("xg_scratch", (XROWS, RW), fp32, kind="Internal").ap()
    acc = nc.dram_tensor("acc_scratch", (N + 128, D), fp32, kind="Internal").ap()
    ctx = ExitStack()
    with ctx:
        def sb(name, shape, dt=fp32):
            return ctx.enter_context(nc.sbuf_tensor(name, shape, dt))

        def sem(name):
            return ctx.enter_context(nc.semaphore(name))

        W13 = sb("W13", [128, NE, KC, 2 * HID])
        W2 = sb("W2", [128, NE, 2 * HC, D])
        w2_flat = W2[:, :, :, :].rearrange("p e k d -> p (e k d)")
        kvc = w2_flat[:, 0:5120].rearrange("p (i n) -> p i n", i=NT)
        wgnn = w2_flat[:, 5120:7168].rearrange("p (k n) -> p k n", k=KC)
        wkv = w2_flat[:, 7168:9216].rearrange("p (k n) -> p k n", k=KC)
        wmq = w2_flat[:, 9216:10240].rearrange("p (e n) -> p e n", e=4)
        wmo = w2_flat[:, 10240:11264].rearrange("p (e n) -> p e n", e=4)
        M1 = w2_flat[:, 11264:12288].rearrange("p (e n) -> p e n", e=4)
        NLATE = 5
        late_flat = W13[:, NE - NLATE:NE, :, :].rearrange("p e k n -> p (e k n)")
        VS = late_flat[0:TP, 0:2560].rearrange("p (i n) -> p i n", i=NT)
        gqkT = late_flat[:, 2560:5060].rearrange("p (m n) -> p m n", m=4)
        edge_mask = late_flat[:, 5060:6624].bitcast(bf16)[0:TP, 0:3125].rearrange("p (i n) -> p i n", i=NT)
        X = late_flat[0:TP, 6624:7904].rearrange("p (i n) -> p i n", i=NT)

        cnt = late_flat[0:TP, 7904:11029].rearrange("p (i n) -> p i n", i=NT)
        edgesg = late_flat[0:NG, 7904:7904 + EG * TP].bitcast(i32)
        dbd = late_flat[:, 11029:11541].rearrange("p (e n) -> p e n", e=4)
        bvs = late_flat[0:TP, 11541:12053]
        M2 = late_flat[:, 12053:12565].rearrange("p (k n) -> p k n", k=KC)
        pad = late_flat[:, 12565:12565 + RW]
        rowv = late_flat[0:TP, 12823:13591].rearrange("p (k n) -> p k n", k=3)
        gamma, beta, bout = (rowv[:, k, :] for k in range(3))

        CM = sb("CM", [128, 4352])
        AT = CM[0:TP, 0:1250].rearrange("p (u j n) -> p u j n", u=2, j=NT)
        rope = CM[0:TP, 1250:1890].rearrange("p (k i c) -> p k i c", k=2, i=NT)
        yat = CM[0:TP, 1890:2402].rearrange("p (u n) -> p u n", u=2)
        yT = CM[:, 2402:2902].rearrange("p (u k n) -> p u k n", u=2, k=KC)
        wqkv = CM[:, 2902:3926].rearrange("p (k n) -> p k n", k=KC)
        zero16 = CM[:, 3926:4182].bitcast(fp16)
        xblk = CM[:, 0:2 * RW].rearrange("p (u n) -> p u n", u=2)
        xTb = CM[:, 516:1028].rearrange("p (u k n) -> p u k n", u=2, k=KC)
        gb = CM[:, 1028:1028 + 4 * HH].rearrange("p (u j n) -> p u j n", u=2, j=2)
        hTb = CM[:, 2392:2392 + 768].rearrange("p (j k n) -> p j k n", j=2, k=HC)
        sl = CM[:, 3160:3160 + 2 * HH].rearrange("p (j n) -> p j n", j=2)

        NEARLY = 3
        ring = W13[:, 0:NEARLY, :, :].rearrange("p e k n -> p (e k n)")[0:TP, 0:SLOTS * EG * 384].bitcast(fp16)
        ring = ring.rearrange("p (s k n) -> p s k n", s=SLOTS, k=EG)

        QKV_MEM = sb("QKV_MEM", [128, 3140])
        QKT = QKV_MEM[:, 0:1875].rearrange("p (m n) -> p m n", m=3)
        Vc = QKV_MEM[0:TP, 1875:1875 + 640].rearrange("p (i n) -> p i n", i=NT)
        qkr = QKV_MEM[0:TP, 2515:2515 + 384]
        yb = QKV_MEM[:, 0:512].rearrange("p (u n) -> p u n", u=2)

        ER = sb("ER", [128, 1888])
        E = ER[0:TP, 0:1875].rearrange("p (s n) -> p s n", s=3)
        dstf = ER[0:TP, 0:160]
        srcf = ER[0:TP, 160:320]
        dstrel = ER[0:TP, 320:1120].rearrange("p (b t) -> p b t", b=NT)
        dsti = ER[0:TP, 1120:1280].bitcast(i32)
        srci = ER[0:TP, 1280:1440].bitcast(i32)
        iota16 = ER[0:TP, 1440:1756].bitcast(fp16)[:, 0:N]

        xnT = sb("xnT", [128, KC, N])
        xn = sb("xn", [TP, NT, D])
        x1 = sb("x1", [TP, NT, D])
        hrow = sb("hrow", [TP, NT, D])
        rowbuf = hrow[:, :, :].rearrange("p i n -> p (i n)")[:, 0:4 * RW].rearrange("p (u k n) -> p u k n", u=2, k=2)
        wo = sb("wo", [128, KC, D])
        wr = sb("wr", [128, KC, NE])
        ln1c = sb("ln1c", [128, KC])
        bqk = sb("bqk", [128, 4])
        ln2r = sb("ln2r", [TP, D])
        ln2 = ln2r[:, :]
        cf = sb("cf", [128, 128 + 160])
        ident = cf[:, 0:128]
        iota8 = cf[0:TP, 128:136]
        thr = cf[0:TP, 136:141]
        ids = cf[0:TP, 141:146]
        region = cf[0:TP, 146:154]
        cbf = sb("cbf", [128, 4 * 128], bf16)
        tri = cbf[0:TP, 0:TP]
        ones = cbf[0:TP, 128:128 + TP]
        identb = cbf[0:TP, 256:256 + TP]
        causal = cbf[0:TP, 384:384 + TP]
        powm = sb("powm", [TP, 80])
        st = sb("st", [TP, NT, 6])
        mv = sb("mv", [TP, NT, 2])
        v_eps = sb("v_eps", [TP, 2 * NT])
        rstd = sb("rstd", [TP, 2 * NT])
        wmean = sb("wmean", [128, 32])
        ss = sb("ss", [TP, NT, 16])
        ssp = sb("ssp", [TP, NT, 8])
        rkv = sb("rkv", [TP, NT, 8])
        gmm = sb("gmm", [NG, 2])
        crow = sb("crow", [1, 512])
        rr = sb("rr", [1, 920])
        rangei = sb("rangei", [1, 2, NT], i32)
        mn = sb("mn", [TP, 20])
        den = sb("den", [TP, 20])
        rd = sb("rd", [TP, 4])
        mn2 = sb("mn2", [TP, 20])
        den2 = sb("den2", [TP, 20])
        rt = sb("rt", [TP, 864])
        rti = sb("rti", [TP, 64], u32)
        blki = sb("blki", [1, 2 * NB + 4], i32)
        slot_w = sb("slot_w", [128, 2])
        slot_id = sb("slot_id", [128, 2], i32)
        ps = ctx.enter_context(nc.psum_tensor("ps", [128, 8, 512], fp32))

        def flat(b, n=1024):
            return ps[:, b:b + (n + 511) // 512, :].rearrange("p b n -> p (b n)")[:, 0:n]

        ld_x, ld_ident, ld_groups, ld_const, ld_edges, ld_gnn, ld_mix, ld_ffn, ld_rows = (
            sem(n) for n in ("ld_x", "ld_ident", "ld_groups", "ld_const", "ld_edges", "ld_gnn", "ld_mix", "ld_ffn", "ld_rows"))
        ld_w, ld_late, xg_emptied = sem("ld_w"), sem("ld_late"), sem("xg_emptied")
        ld_pad, acc_emptied, acc_stored = sem("ld_pad"), sem("acc_emptied"), sem("acc_stored")
        link_dve, link_pool = sem("link_dve"), sem("link_pool")
        consts_set = sem("consts_set")
        var1, rstd1, xn_done, xnT_ps, xnT_done = (
            sem(n) for n in ("var1", "rstd1", "xn_done", "xnT_ps", "xnT_done"))
        bq_scaled, qk_ps, qk_done, vs_ps, vs_copied, vs_done = (
            sem(n) for n in ("bq_scaled", "qk_ps", "qk_done", "vs_ps", "vs_copied", "vs_done"))
        gmm_done, gmm_ps, range_done = sem("gmm_done"), sem("gmm_ps"), sem("range_done")
        oh_built, oh_used, cnt_ps, cnt_done, mask_done = (
            sem(n) for n in ("oh_built", "oh_used", "cnt_ps", "cnt_done", "mask_done"))
        wmean_done, wkv_centred, kv_ps, kv_copied, sq_done, kv_normed, mix_ps, mix_used = (
            sem(n) for n in ("wmean_done", "wkv_centred", "kv_ps", "kv_copied", "sq_done", "kv_normed", "mix_ps",
                             "mix_used"))
        dots_ps, dbd_done, M1_ps, M1_done, M2_ps, M2_done = (
            sem(n) for n in ("dots_ps", "dbd_done", "M1_ps", "M1_done", "M2_ps", "M2_done"))
        xb_done, S_ps, S_used, exp_done, A_done, AT_ps, AT_done, AV_done, O_used, gelu_done = (
            sem(n) for n in ("xb_done", "S_ps", "S_used", "exp_done", "A_done", "AT_ps", "AT_done",
                             "AV_done", "O_used", "gelu_done"))
        agg_done, varg, rstdg, var2, r2 = (sem(n) for n in ("agg_done", "varg", "rstdg", "var2", "r2"))
        h_done, hT_ps, hT_done, qkv_ps, qkr_done, vc_done, qkT_ps, qkT_done, qkr_used = (
            sem(n) for n in ("h_done", "hT_ps", "hT_done", "qkv_ps", "qkr_done", "vc_done", "qkT_ps",
                             "qkT_done", "qkr_used"))
        qkv_used = sem("qkv_used")
        S2_ps, max2_done, exp2_done, ET_ps, ET_done, AV2_done, y_done, O2_used = (
            sem(n) for n in ("S2_ps", "max2_done", "exp2_done", "ET_ps", "ET_done", "AV2_done",
                             "y_done", "O2_used"))
        yT_ps, yT_done, wo_ps, x2_done = (sem(n) for n in ("yT_ps", "yT_done", "wo_ps", "x2_done"))
        ms3, r3, flat_done, flatT_ps, flatT_done, logit_ps = (
            sem(n) for n in ("ms3", "r3", "flat_done", "flatT_ps", "flatT_done", "logit_ps"))
        rmax_done, rexp_done, sel_done, rank_ps, rank_used, blk_done, slot_done = (
            sem(n) for n in ("rmax_done", "rexp_done", "sel_done", "rank_ps", "rank_used", "blk_done",
                             "slot_done"))
        scattered = [sem("scattered0"), sem("scattered1")]
        xblk_ld = [sem("xblk_ld0"), sem("xblk_ld1")]
        y_added, last_y_added, y_free = sem("y_added"), sem("last_y_added"), sem("y_free")
        y_seen = sem("y_seen")
        mxT_ps, mxT_done, ab_ps, silu_done, g_done, gT_ps, gT_copied, y_ps, y_copied = (
            sem(n) for n in ("mxT_ps", "mxT_done", "ab_ps", "silu_done", "g_done", "gT_ps",
                             "gT_copied", "y_ps", "y_copied"))
        res_done, meta_done, out_stored = sem("res_done"), sem("meta_done"), sem("out_stored")

        block = ctx.enter_context(nc.Block())

        MIX_OUT = (9, 11, 13, 15, 17)

        FT_BANK = (5, 5, 7, 0, 2)
        LG_BANK = (5, 5, 1, 1, 3)

        def R(i, a, n):
            return rt[:, 64 * (i + 1) + a:64 * (i + 1) + a + n]

        def sel_of(i):
            return rt[:, 840 + 4 * i:844 + 4 * i].bitcast(bf16)

        HALVES = ((0, 313), (313, 625))

        @block.sync
        def _(sp):
            sp.dma_start(X, x.rearrange("(i p) c -> p i c", p=TP)).then_inc(ld_x, 16)
            sp.dma_start(cf[:, :], c_f32).then_inc(ld_ident, 16)
            sp.dma_start(edgesg, edge_groups).then_inc(ld_groups, 16)
            sp.dma_start(crow[:, :], c_row).then_inc(ld_groups, 16)
            sp.dma_start(dsti, edge_dst).then_inc(ld_edges, 16)
            sp.dma_start(srci, edge_src).then_inc(ld_edges, 16)
            sp.dma_start(iota16, c_iota.partition_broadcast(TP)).then_inc(ld_edges, 16)
            sp.dma_start(wgnn, w_gnn).then_inc(ld_gnn, 16)
            sp.dma_start(bqk[:, :], b_gnn_qk).then_inc(ld_gnn, 16)
            sp.dma_start(bvs, b_gnn_vs.partition_broadcast(TP)).then_inc(ld_gnn, 16)
            sp.dma_start(wkv, w_mix_kv).then_inc(ld_mix, 16)
            sp.dma_start(wmq, w_mix_q).then_inc(ld_mix, 16)
            sp.dma_start(wmo, w_mix_out).then_inc(ld_mix, 16)
            sp.dma_start(rowv, rows[0:3, :].partition_broadcast(TP)).then_inc(ld_rows, 16)
            sp.dma_start(ln2, rows[3, :].partition_broadcast(TP)).then_inc(ld_rows, 16)
            sp.dma_start(cbf[:, :], c_bf16).then_inc(ld_const, 16)
            sp.dma_start(rope, c_rope).then_inc(ld_const, 16)
            sp.dma_start(wqkv, w_ffn_qkv).then_inc(ld_ffn, 16)
            sp.dma_start(wo[:, :, :], w_ffn_o).then_inc(ld_ffn, 16)
            sp.dma_start(wr[:, :, :], w_router).then_inc(ld_ffn, 16)
            sp.dma_start(ln1c[:, :], ln1_col).then_inc(ld_ffn, 16)
            for e in range(NEARLY, NE - NLATE):
                sp.dma_start(W13[:, e, :, :], w13[:, e, :, :]).then_inc(ld_w, 16)
            sp.dma_start(pad, c_pad).then_inc(ld_pad, 16)
            sp.wait_ge(ld_pad, 16)
            sp.dma_start(xg.rearrange("(j p) c -> p j c", p=128),
                         pad.unsqueeze(1).to_broadcast([128, XROWS // 128, RW])).then_inc(xg_emptied, 16)
            sp.dma_start(acc[N:N + 128, :], pad[:, 0:D]).then_inc(acc_emptied, 16)
            sp.wait_ge(cnt_ps, NT)
            for e in range(NEARLY):
                sp.dma_start(W13[:, e, :, :], w13[:, e, :, :]).then_inc(ld_w, 16)
            sp.wait_ge(M2_done, 1)
            for e in range(NE):
                for j in range(2):
                    sp.dma_start(W2[:, e, HC * j:HC * j + 2, :],
                                 w2[e, HH * j:HH * j + 256, :].rearrange("(k p) d -> p k d", p=128)
                                 ).then_inc(ld_late, 16)
                    sp.dma_start(W2[0:HCW[2], e, HC * j + 2, :],
                                 w2[e, HH * j + 256:HH * (j + 1), :]).then_inc(ld_late, 16)
            sp.wait_ge(xg_emptied, 16)
            sp.wait_ge(acc_emptied, 16)
            sp.wait_ge(var2, 1)
            for e in range(NE - NLATE, NE):
                sp.dma_start(W13[:, e, :, :], w13[:, e, :, :]).then_inc(ld_late, 16)
            for i in range(NT):
                sp.wait_ge(res_done, i + 1)
                sp.dma_start(acc[i * TP:(i + 1) * TP, :], x1[:, i, :]).then_inc(acc_stored, 16)
            def rows_of(s):
                return sp.value_load(blki[0:1, bass.ds(s + NB, 1)], min_val=0, max_val=NE * CAP)

            sp.wait_ge(blk_done, 1)
            iters = sp.value_load(blki[0:1, 2 * NB:2 * NB + 1], min_val=1, max_val=(MAXB - 1) // 2)
            first, second = rows_of(0), rows_of(1)
            sp.wait_ge(scattered[0], 32 * 3)
            sp.wait_ge(scattered[1], 32 * 2)
            sp.dma_start(xblk[:, 0, :], xg[bass.ds(first, 128), :]).then_inc(xblk_ld[0], 16)
            sp.dma_start(xblk[:, 1, :], xg[bass.ds(second, 128), :]).then_inc(xblk_ld[1], 16)
            with sp.Fori(0, iters) as m:
                for u, s in ((0, 2 * m + 1), (1, 2 * m + 2)):
                    row = rows_of(s + 1)
                    sp.wait_ge(mxT_ps, s)
                    sp.wait_ge(meta_done, s)
                    sp.dma_start(xblk[:, u, :], xg[bass.ds(row, 128), :]).then_inc(xblk_ld[u], 16)
            sp.wait_ge(last_y_added, 16)
            sp.dma_start(out, acc[0:N, :]).then_inc(out_stored, 16)
            sp.wait_ge(out_stored, 16)

        @block.gpsimd
        def _(pool):
            steps = [0]

            def link(ins):
                steps[0] += 1
                ins.then_inc(link_pool, 1)
                pool.wait_ge(link_pool, steps[0])

            nc.gpsimd.memset(powm[:, :], -0.5).then_inc(consts_set, 1)
            nc.gpsimd.memset(zero16, 0.0).then_inc(consts_set, 1)
            nc.gpsimd.memset(dbd, 0.0).then_inc(consts_set, 1)
            pool.wait_ge(consts_set, 3)
            pool.wait_ge(var1, 1)
            nc.gpsimd.tensor_tensor(rstd[:, 0:NT], v_eps[:, 0:NT], powm[:, 0:NT], ALU.pow).then_inc(rstd1, 1)
            pool.wait_ge(ld_gnn, 48)
            nc.gpsimd.tensor_scalar(bqk[:, 0:2], bqk[:, 0:2], -1.0 / 8.0, 0.0, ALU.mult, ALU.add).then_inc(bq_scaled, 1)
            pool.wait_ge(wmean_done, 1)
            wk3 = wkv.rearrange("p k (h c) -> p (k h) c", c=C)
            nc.gpsimd.tensor_tensor(wk3, wk3, wmean[:, :].unsqueeze(2).to_broadcast([128, 32, C]),
                                    ALU.subtract).then_inc(wkv_centred, 1)
            for i in range(NT):
                pool.wait_ge(vs_copied, i + 1)
                nc.gpsimd.tensor_tensor(VS[:, i, :], VS[:, i, :], bvs, ALU.add).then_inc(vs_done, 1)
            pool.wait_ge(ld_rows, 32)
            pool.wait_ge(ld_x, 16)
            link(nc.gpsimd.tensor_tensor(beta, beta, bout, ALU.add))
            for i in range(NT):
                nc.gpsimd.tensor_tensor(x1[:, i, :], X[:, i, :], beta, ALU.add).then_inc(xb_done, 1)

            def mask(i):
                pool.wait_ge(cnt_done, 2 * i + 2)
                nc.gpsimd.tensor_scalar(edge_mask[:, i, :], cnt[:, i, :], 0.0, BIG, ALU.is_equal,
                                        ALU.mult).then_inc(mask_done, 1)

            for i in range(NT - 1):
                mask(i)
            pool.wait_ge(sq_done, NT)
            link(nc.gpsimd.tensor_scalar(ss[:, :, :], ss[:, :, :], 1.0 / C, EPS, ALU.mult, ALU.add))
            link(nc.gpsimd.tensor_tensor(ssp[:, :, :], ss[:, :, 0:8], ss[:, :, 8:16], ALU.mult))
            link(nc.gpsimd.tensor_tensor(rkv[:, :, :].rearrange("p i h -> p (i h)"),
                                         ssp[:, :, :].rearrange("p i h -> p (i h)"), powm[:, 0:40], ALU.pow))
            for i in range(NT):
                kk = kvc[0:TP, i, 0:512].rearrange("p (h c) -> p h c", c=C)
                nc.gpsimd.tensor_tensor(kk, kk, rkv[:, i, :].unsqueeze(2).to_broadcast([TP, MH, C]),
                                        ALU.mult).then_inc(kv_normed, 1)
            mask(NT - 1)
            pool.wait_ge(varg, 1)
            nc.gpsimd.tensor_tensor(rstd[:, 0:NT], v_eps[:, 0:NT], powm[:, 0:NT], ALU.pow).then_inc(rstdg, 1)
            pool.wait_ge(var2, 1)
            nc.gpsimd.tensor_tensor(rstd[:, :], v_eps[:, :], powm[:, 0:2 * NT], ALU.pow).then_inc(r2, 1)

            def scatter(i):
                pool.wait_ge(slot_done, i + 1)
                pool.wait_ge(xg_emptied, 16)
                for k in range(2):
                    nc.gpsimd.indirect_dma_start(
                        xg, bass.IndirectOffsetOnAxis(rti[:, 40 + 2 * i + k:41 + 2 * i + k], 0),
                        rowbuf[:, i % 2, k, :], None).then_inc(scattered[i % 2], 16)

            for i in range(NT):
                pool.wait_ge(ms3, i + 1)
                nc.gpsimd.tensor_tensor(rstd[:, i:i + 1], v_eps[:, i:i + 1], powm[:, i:i + 1], ALU.pow).then_inc(r3, 1)
                if i:
                    scatter(i - 1)
                if i < NT - 1:
                    nc.gpsimd.tensor_tensor(x1[:, i, :], x1[:, i, :], xn[:, i, :], ALU.add).then_inc(res_done, 1)
            scatter(NT - 1)
            nc.gpsimd.tensor_tensor(x1[:, NT - 1, :], x1[:, NT - 1, :], xn[:, NT - 1, :], ALU.add).then_inc(res_done, 1)
            pool.wait_ge(blk_done, 1)
            iters = pool.value_load(blki[0:1, 2 * NB:2 * NB + 1], min_val=1, max_val=(MAXB - 1) // 2)

            pool.wait_ge(acc_stored, 16 * NT)
            pool.wait_ge(acc_emptied, 16)

            def add_rows(u):
                pool.sem_inc(y_seen, 1)
                return nc.gpsimd.indirect_dma_start(
                    acc, bass.IndirectOffsetOnAxis(slot_id[:, u:u + 1], 0), yb[:, u, :], None,
                    compute_op=ALU.add)

            with pool.Fori(0, iters) as m:
                for u, s in ((0, 2 * m), (1, 2 * m + 1)):
                    pool.wait_ge(y_copied, s + 2)
                    add_rows(u).then_inc(y_added, 16)
                    pool.wait_ge(y_added, 16 * s + 16)
                    pool.sem_inc(y_free, 1)
            pool.wait_ge(y_copied, 2 * iters + 2)
            add_rows(0).then_inc(last_y_added, 16)

        @block.scalar
        def _(act):
            for i in range(NT):
                act.wait_ge(xnT_ps, i + 1)
                nc.scalar.copy(xnT[:, :, i * TP:(i + 1) * TP],
                               ps[:, i % 2, 0:256].rearrange("p (k n) -> p k n", k=KC)[:, :, 0:TP]).then_inc(xnT_done, 1)
            act.wait_ge(bq_scaled, 1)
            for j in range(8):
                m, (a, b) = j // 2, HALVES[j % 2]
                act.wait_ge(qk_ps, j + 1)
                nc.scalar.activation(gqkT[:, m, a:b], ps[:, 2 + j % 4, 0:b - a], ACT.Identity,
                                     bias=bqk[:, m:m + 1], scale=-0.125 if m < 2 else 1.0).then_inc(qk_done, 1)

            def cnt_copy(b):
                act.wait_ge(cnt_ps, b + 1)
                if b == 0:
                    act.wait_ge(range_done, 1)
                nc.scalar.copy(cnt[:, b, 0:512], ps[0:TP, 0, :]).then_inc(cnt_done, 1)
                nc.scalar.copy(cnt[:, b, 512:N], ps[0:TP, 1, 0:N - 512]).then_inc(cnt_done, 1)

            def kv_copy(i):
                kv = flat(2 + 2 * (i % 2))[0:TP, :]
                act.wait_ge(kv_ps, i + 1)
                nc.scalar.copy(kvc[0:TP, i, :], kv).then_inc(kv_copied, 1)
                act.wait_ge(kv_copied, i + 1)
                for g in range(2 * MH):
                    ins = nc.scalar.activation(kv[:, C * g:C * (g + 1)], kv[:, C * g:C * (g + 1)], ACT.Square,
                                               accum_out=ss[:, i, g:g + 1])
                ins.then_inc(sq_done, 1)

            cnt_copy(0)
            for i in range(NT):
                act.wait_ge(vs_ps, i + 1)
                nc.scalar.copy(VS[:, i, :], ps[0:TP, 6 + i % 2, :]).then_inc(vs_copied, 1)
            cnt_copy(1)
            kv_copy(0)
            kv_copy(1)
            cnt_copy(2)
            kv_copy(2)
            kv_copy(3)
            cnt_copy(3)
            kv_copy(4)
            cnt_copy(4)

            def gnn_AT(n):
                act.wait_ge(AT_ps, n + 1)
                if n >= 2:
                    act.wait_ge(AV_done, n - 1)
                nc.scalar.copy(AT[:, n % 2, :, :],
                               flat(4)[0:TP, 0:640].rearrange("p (j n) -> p j n", j=NT)[:, :, 0:TP]).then_inc(AT_done, 1)

            for n in range(20):
                act.wait_ge(S_used, n + 1)
                nc.scalar.activation(E[:, n % 3, :], E[:, n % 3, :], ACT.Exp,
                                     bias=mn[:, n:n + 1], scale=-1.0).then_inc(exp_done, 1)
                if n >= 2:
                    gnn_AT(n - 2)
                if n in (4, 5):
                    act.wait_ge(M1_ps, n - 3)
                    nc.scalar.copy(M1[:, 2 * (n - 4):2 * (n - 3), :],
                                   ps[:, 7, :].rearrange("p (e n) -> p e n", e=2)).then_inc(M1_done, 1)
                if n == 7:
                    act.wait_ge(M2_ps, 1)
                    nc.scalar.copy(M2.rearrange("p k n -> p (k n)"), ps[:, 7, :]).then_inc(M2_done, 1)
            gnn_AT(18)
            gnn_AT(19)
            act.wait_ge(agg_done, NT)
            nc.scalar.activation(VS[:, :, D:512], VS[:, :, D:512], ACT.Gelu).then_inc(gelu_done, 1)
            act.wait_ge(ld_ffn, 64)
            for i in range(NT):
                act.wait_ge(hT_ps, i + 1)
                for k in range(KC):
                    ins = nc.scalar.activation(xnT[:, k, i * TP:(i + 1) * TP],
                                               ps[:, i % 2, 128 * k:128 * k + TP], ACT.Copy, scale=ln1c[:, k:k + 1])
                ins.then_inc(hT_done, 1)

            def qkT_copy(i):
                act.wait_ge(qkT_ps, i + 1)
                t = ps[:, 4 + i % 2, 0:384].rearrange("p (m n) -> p m n", m=3)[:, :, 0:TP]
                nc.scalar.mul(QKT[:, 0:2, i * TP:(i + 1) * TP], t[:, 0:2, :], 0.125)
                nc.scalar.copy(QKT[:, 2, i * TP:(i + 1) * TP], t[:, 2, :]).then_inc(qkT_done, 1)

            for i in range(NT):
                act.wait_ge(qkv_used, i + 1)
                nc.scalar.copy(Vc[:, i, :], ps[0:TP, 2 + i % 2, 384:512]).then_inc(vc_done, 1)
                if i:
                    qkT_copy(i - 1)
            qkT_copy(NT - 1)

            def ffn_ET(n):
                i = n // 4
                act.wait_ge(ET_ps, n + 1)
                if n >= 2:
                    act.wait_ge(AV2_done, n - 1)
                nc.scalar.copy(AT[:, n % 2, 0:i + 1, :],
                               flat(4)[0:TP, 0:640].rearrange("p (j n) -> p j n", j=NT)[:, 0:i + 1, 0:TP]).then_inc(ET_done, 1)

            def ffn_yT(i):
                act.wait_ge(yT_ps, i + 1)
                nc.scalar.copy(yT[:, i % 2, :, :],
                               ps[:, 7, 0:256].rearrange("p (k n) -> p k n", k=KC)[:, :, 0:TP]).then_inc(yT_done, 1)

            def flatT_copy(i):
                act.wait_ge(flatT_ps, i + 1)
                nc.scalar.copy(xnT[:, :, i * TP:(i + 1) * TP],
                               ps[:, FT_BANK[i], 0:256].rearrange("p (k n) -> p k n", k=KC)[:, :, 0:TP]).then_inc(flatT_done, 1)

            def router_exp(i):
                act.wait_ge(rmax_done, i + 1)
                nc.scalar.activation(R(i, 16, 8), R(i, 8, 8), ACT.Exp, bias=R(i, 52, 1),
                                     accum_out=R(i, 53, 1)).then_inc(rexp_done, 1)

            for n in range(20):
                i = n // 4
                act.wait_ge(max2_done, n + 1)
                if n >= 3:
                    act.wait_ge(ET_ps, n - 2)
                w = TP * (i + 1)
                nc.scalar.activation(E[:, n % 3, 0:w], flat(2 * (n % 2))[0:TP, 0:w], ACT.Exp,
                                     bias=mn2[:, n:n + 1], scale=1.0,
                                     accum_out=den2[:, n:n + 1]).then_inc(exp2_done, 1)
                if n >= 2:
                    ffn_ET(n - 2)
                if n % 4 == 3 and n >= 7:
                    ffn_yT(i - 1)
                if n % 4 == 2 and n >= 10:
                    flatT_copy(i - 2)
                if n % 4 == 0 and n >= 12:
                    router_exp(i - 3)
            ffn_ET(18)
            ffn_ET(19)
            router_exp(2)
            flatT_copy(3)
            ffn_yT(4)
            router_exp(3)
            flatT_copy(4)
            router_exp(4)

            def xT_copy(s, u):
                act.wait_ge(mxT_ps, s + 1)
                nc.scalar.copy(xTb[:, u, :, :], ps[:, 7, 0:256].rearrange("p (k n) -> p k n", k=KC)).then_inc(mxT_done, 1)

            def silu(s, j):
                act.wait_ge(ab_ps, 2 * s + j + 1)
                if not isinstance(s, int):
                    act.wait_ge(g_done, 2 * s + j - 1)
                nc.scalar.activation(sl[:, j, :], ps[:, 2 * j, 0:HH], ACT.Silu).then_inc(silu_done, 1)

            def hT_copy(s, j):
                act.wait_ge(gT_ps, 2 * s + j + 1)
                nc.scalar.copy(hTb[:, j, :, :], ps[:, 4 + j, 0:384].rearrange("p (k n) -> p k n", k=HC)).then_inc(gT_copied, 1)

            act.wait_ge(blk_done, 1)
            iters = act.value_load(blki[0:1, 2 * NB:2 * NB + 1], min_val=1, max_val=(MAXB - 1) // 2)
            xT_copy(0, 0)
            silu(0, 0)
            xT_copy(1, 1)
            silu(0, 1)
            with act.Fori(0, iters) as m:
                for u, s in ((1, 2 * m + 1), (0, 2 * m + 2)):
                    silu(s, 0)
                    xT_copy(s + 1, 1 - u)
                    hT_copy(s - 1, 0)
                    hT_copy(s - 1, 1)
                    silu(s, 1)
            for j in range(2):
                hT_copy(2 * iters, j)

        @block.tensor
        def _(pe):
            def two_transposes(bank, rows, src_parts=TP):
                for k in range(KC):
                    ins = nc.tensor.transpose(ps[:, bank, 128 * k:128 * k + src_parts],
                                              rows[:, 128 * k:128 * (k + 1)], ident[0:src_parts, 0:src_parts])
                return ins

            pe.wait_ge(ld_ident, 16)
            for i in range(NT):
                pe.wait_ge(xn_done, i + 1)
                if i >= 2:
                    pe.wait_ge(xnT_done, i - 1)
                two_transposes(i % 2, xn[:, i, :]).then_inc(xnT_ps, 1)
            pe.wait_ge(gmm_done, 1)
            for k in range(2):
                ins = nc.tensor.matmul(ps[0:1, 7, NG * k:NG * (k + 1)], gmm[:, k:k + 1], ident[0:NG, 0:NG],
                                       start=True, stop=True)
            ins.then_inc(gmm_ps, 1)
            pe.wait_ge(ld_gnn, 48)
            pe.wait_ge(xnT_done, NT)
            for j in range(8):
                m, (a, b) = j // 2, HALVES[j % 2]
                if j >= 4:
                    pe.wait_ge(qk_done, j - 3)
                for k in range(KC):
                    ins = nc.tensor.matmul(ps[:, 2 + j % 4, 0:b - a], wgnn[:, k, 128 * m:128 * (m + 1)],
                                           xnT[:, k, a:b], start=(k == 0), stop=(k == KC - 1))
                ins.then_inc(qk_ps, 1)
            seq = pe.alloc_register("pe_groups")
            slot = pe.alloc_register("pe_slot")
            pe.reg_mov(seq, 0)
            pe.reg_mov(slot, 0)
            big, small = ps[:, 0, :], ps[:, 1, 0:N - 512]

            def zeros(start):
                nc.tensor.matmul(big, zero16[:, 0:128], zero16, start=start, stop=not start)
                return nc.tensor.matmul(small, zero16[:, 0:128], zero16[:, 0:N - 512], start=start, stop=not start)

            def count(b):
                first = pe.value_load(rangei[0:1, 0, b:b + 1], min_val=0, max_val=NG - 1)
                last = pe.value_load(rangei[0:1, 1, b:b + 1], min_val=1, max_val=NG)
                if b:
                    pe.wait_ge(cnt_done, 2 * b)
                zeros(True)
                with pe.Fori(first, last):
                    done = pe.snap(seq, min_val=0, max_val=NT * NG)
                    r = ring[:, bass.ds(pe.snap(slot, min_val=0, max_val=SLOTS - 1), 1), :, :].rearrange("p a k n -> p (a k) n")
                    pe.wait_ge(oh_built, done + 1)
                    for k in range(EG):
                        nc.tensor.matmul(big, r[:, k, 640:768], r[:, k, 0:512], start=False, stop=False)
                        ins = nc.tensor.matmul(small, r[:, k, 640:768], r[:, k, 512:N], start=False, stop=False)
                    ins.then_inc(oh_used, 1)
                    pe.reg_add(seq, seq, 1)
                    pe.reg_add(slot, slot, 1)
                    pe.reg_mod(slot, slot, SLOTS)
                zeros(False).then_inc(cnt_ps, 1)

            def mix_kv(i):
                if i >= 2:
                    pe.wait_ge(sq_done, i - 1)
                for j in range(2):
                    for k in range(KC):
                        ins = nc.tensor.matmul(ps[0:TP, 2 + 2 * (i % 2) + j, :], xnT[:, k, i * TP:(i + 1) * TP],
                                               wkv[:, k, 512 * j:512 * (j + 1)], start=(k == 0), stop=(k == KC - 1))
                ins.then_inc(kv_ps, 1)

            pe.wait_ge(range_done, 1)
            pe.wait_ge(consts_set, 3)
            count(0)
            for i in range(NT):
                if i >= 2:
                    pe.wait_ge(vs_copied, i - 1)
                for k in range(KC):
                    ins = nc.tensor.matmul(ps[0:TP, 6 + i % 2, :], xnT[:, k, i * TP:(i + 1) * TP],
                                           wgnn[:, k, 512:1024], start=(k == 0), stop=(k == KC - 1))
                ins.then_inc(vs_ps, 1)
            count(1)
            pe.wait_ge(ld_mix, 48)
            pe.wait_ge(wkv_centred, 1)
            pe.wait_ge(qk_done, 8)
            mix_kv(0)
            mix_kv(1)
            count(2)
            mix_kv(2)
            mix_kv(3)
            count(3)
            mix_kv(4)
            count(4)
            pe.wait_ge(cnt_done, 2 * NT)
            pe.wait_ge(sq_done, NT)
            pe.wait_ge(vs_done, NT)

            def mix_dots():
                pe.wait_ge(kv_normed, NT)
                for p in range(4):
                    for i in range(NT):
                        ins = nc.tensor.matmul(ps[:, 7, 128 * p:128 * (p + 1)],
                                               kvc[0:TP, i, 512 + 128 * p:512 + 128 * (p + 1)],
                                               kvc[0:TP, i, 128 * p:128 * (p + 1)], start=(i == 0), stop=(i == NT - 1))
                ins.then_inc(dots_ps, 1)

            def mix_M1(half):
                if half:
                    pe.wait_ge(M1_done, 1)
                else:
                    pe.wait_ge(dbd_done, 1)
                for p in (2 * half, 2 * half + 1):
                    ins = nc.tensor.matmul(ps[:, 7, 256 * (p % 2):256 * (p % 2) + 256], dbd[:, p, :],
                                           wmo[:, p, :], start=True, stop=True)
                ins.then_inc(M1_ps, 1)

            def mix_M2():
                pe.wait_ge(M1_done, 2)
                for m in range(KC):
                    for p in range(4):
                        ins = nc.tensor.matmul(ps[:, 7, 256 * m:256 * (m + 1)], wmq[:, p, 128 * m:128 * (m + 1)],
                                               M1[:, p, :], start=(p == 0), stop=(p == 3))
                ins.then_inc(M2_ps, 1)

            def mix_out(i):
                if i:
                    pe.wait_ge(mix_used, i)
                else:
                    pe.wait_ge(M2_done, 1)
                for k in range(KC):
                    ins = nc.tensor.matmul(ps[0:TP, 7, 0:256], xnT[:, k, i * TP:(i + 1) * TP], M2[:, k, :],
                                           start=(k == 0), stop=(k == KC - 1))
                ins.then_inc(mix_ps, 1)

            def gnn_AV(n):
                i, h = n // 4, n % 4
                pe.wait_ge(AT_done, n + 1)
                if h == 0 and i:
                    pe.wait_ge(O_used, i)
                for j in range(NT):
                    ins = nc.tensor.matmul(ps[0:TP, 6, C * h:C * (h + 1)], AT[:, n % 2, j, :],
                                           VS[:, j, C * h:C * (h + 1)], start=(j == 0), stop=(j == NT - 1))
                ins.then_inc(AV_done, 1)

            def gnn_T(n):
                pe.wait_ge(A_done, n + 1)
                if n >= 1:
                    pe.wait_ge(AT_done, n)
                for j in range(NT):
                    ins = nc.tensor.transpose(flat(4)[0:TP, 128 * j:128 * j + TP], E[:, n % 3, TP * j:TP * (j + 1)],
                                              ident[0:TP, 0:TP])
                ins.then_inc(AT_ps, 1)

            for n in range(20):
                i, h = n // 4, n % 4
                if n >= 2:
                    pe.wait_ge(S_used, n - 1)
                r = 64 * (h % 2)
                for a, b in ((0, 512), (512, N)):
                    ins = nc.tensor.matmul(flat(2 * (n % 2))[0:TP, a:b], gqkT[r:r + 64, h // 2, i * TP:(i + 1) * TP],
                                           gqkT[r:r + 64, 2 + h // 2, a:b], start=True, stop=True)
                ins.then_inc(S_ps, 1)
                if n >= 2:
                    gnn_T(n - 2)
                if n == 2:
                    mix_dots()
                if n in (4, 5):
                    mix_M1(n - 4)
                if n == 7:
                    mix_M2()
                if n in MIX_OUT:
                    mix_out(MIX_OUT.index(n))
                if n >= 3:
                    gnn_AV(n - 3)
            gnn_T(18)
            gnn_AV(17)
            gnn_T(19)
            gnn_AV(18)
            gnn_AV(19)
            pe.wait_ge(ld_ffn, 64)
            pe.wait_ge(ld_const, 32)
            pe.wait_ge(S_used, 20)
            pe.wait_ge(mix_used, NT)
            for i in range(NT):
                pe.wait_ge(h_done, i + 1)
                if i >= 2:
                    pe.wait_ge(hT_done, i - 1)
                two_transposes(i % 2, hrow[:, i, :]).then_inc(hT_ps, 1)

            def qkT(i):
                pe.wait_ge(qkr_done, i + 1)
                if i >= 2:
                    pe.wait_ge(qkT_done, i - 1)
                for m in range(3):
                    ins = nc.tensor.transpose(ps[:, 4 + i % 2, 128 * m:128 * m + TP], qkr[:, 128 * m:128 * (m + 1)],
                                              ident[0:TP, 0:TP])
                ins.then_inc(qkT_ps, 1)

            for i in range(NT):
                pe.wait_ge(hT_done, i + 1)
                if i >= 2:
                    pe.wait_ge(qkv_used, i - 1)
                    pe.wait_ge(vc_done, i - 1)
                for k in range(KC):
                    ins = nc.tensor.matmul(ps[0:TP, 2 + i % 2, :], xnT[:, k, i * TP:(i + 1) * TP], wqkv[:, k, :],
                                           start=(k == 0), stop=(k == KC - 1))
                ins.then_inc(qkv_ps, 1)
                if i:
                    qkT(i - 1)
            qkT(NT - 1)
            pe.wait_ge(qkT_done, NT)
            pe.wait_ge(vc_done, NT)
            pe.wait_ge(qkv_used, NT)

            def ffn_T(n):
                pe.wait_ge(exp2_done, n + 1)
                if n >= 1:
                    pe.wait_ge(ET_done, n)
                if n == 16:
                    pe.wait_ge(rank_used, 2)
                for j in range(n // 4 + 1):
                    ins = nc.tensor.transpose(flat(4)[0:TP, 128 * j:128 * j + TP], E[:, n % 3, TP * j:TP * (j + 1)],
                                              ident[0:TP, 0:TP])
                ins.then_inc(ET_ps, 1)

            def ffn_AV(n):
                i, h = n // 4, n % 4
                pe.wait_ge(ET_done, n + 1)
                if h == 0 and i:
                    pe.wait_ge(O2_used, i)
                for j in range(i + 1):
                    ins = nc.tensor.matmul(ps[0:TP, 6, C * h:C * (h + 1)], AT[:, n % 2, j, :],
                                           Vc[:, j, C * (h // 2):C * (h // 2) + C], start=(j == 0), stop=(j == i))
                ins.then_inc(AV2_done, 1)

            def ffn_yT(i):
                pe.wait_ge(y_done, i + 1)
                if i:
                    pe.wait_ge(x2_done, i)
                if i == 3:
                    pe.wait_ge(flatT_done, 3)
                two_transposes(7, yat[:, i % 2, :]).then_inc(yT_ps, 1)

            def ffn_wo(i):
                pe.wait_ge(yT_done, i + 1)
                if i:
                    pe.wait_ge(x2_done, i)
                for k in range(KC):
                    ins = nc.tensor.matmul(ps[0:TP, 7, 256:512], yT[:, i % 2, k, :], wo[:, k, :],
                                           start=(k == 0), stop=(k == KC - 1))
                ins.then_inc(wo_ps, 1)

            def flatT(i):
                pe.wait_ge(flat_done, i + 1)
                two_transposes(FT_BANK[i], rowbuf[:, i % 2, 0, :]).then_inc(flatT_ps, 1)

            def logits(i):
                pe.wait_ge(flatT_done, i + 1)
                if i:
                    pe.wait_ge(rank_used, i)
                for k in range(KC):
                    ins = nc.tensor.matmul(ps[0:TP, LG_BANK[i], 256:256 + NE], xnT[:, k, i * TP:(i + 1) * TP],
                                           wr[:, k, :], start=(k == 0), stop=(k == KC - 1))
                ins.then_inc(logit_ps, 1)

            def rank(i):
                pe.wait_ge(sel_done, i + 1)
                for j in range(i + 1):
                    ins = nc.tensor.matmul(ps[0:TP, LG_BANK[i], 272:272 + NE], tri if j == i else ones, sel_of(j),
                                           start=(j == 0), stop=(j == i))
                if i == NT - 1:
                    for j in range(NT):
                        ins = nc.tensor.matmul(ps[0:TP, LG_BANK[i], 288:288 + NE], ones, sel_of(j), start=(j == 0),
                                               stop=(j == NT - 1))
                ins.then_inc(rank_ps, 1)

            for n in range(20):
                i, h = n // 4, n % 4
                if n >= 2:
                    pe.wait_ge(exp2_done, n - 1)
                w = TP * (i + 1)
                r = 64 * (h // 2)
                S = flat(2 * (n % 2))[0:TP, :]
                q = QKT[r:r + 64, h % 2, i * TP:(i + 1) * TP]
                edges = [0, w - TP, w] if w > 512 else [0, w]
                for a, b in zip(edges, edges[1:]):
                    b1 = min(b, 512)
                    last = b == w
                    if a < b1:
                        nc.tensor.matmul(S[:, a:b1], q, QKT[r:r + 64, 2, a:b1], start=True,
                                         stop=not (last and b1 <= 512), skip_group_check=True)
                    if b > 512:
                        nc.tensor.matmul(S[:, 512:b], q, QKT[r:r + 64, 2, 512:b], start=True, stop=False,
                                         skip_group_check=True)
                for a, b in ((w - TP, min(w, 512)), (512, w)):
                    if a < b:
                        ins = nc.tensor.matmul(S[:, a:b], identb, causal[:, a - (w - TP):b - (w - TP)], start=False,
                                               stop=True, skip_group_check=True)
                ins.then_inc(S2_ps, 1)
                if n >= 2:
                    ffn_T(n - 2)
                if n >= 3:
                    ffn_AV(n - 3)
                if n >= 12 and h == 0:
                    rank(i - 3)
                if h == 3 and 11 <= n < 19:
                    logits(i - 2)
                if n >= 10 and h == 2:
                    flatT(i - 2)
                if n >= 7 and h == 3:
                    ffn_yT(i - 1)
                if n >= 8 and h == 0:
                    ffn_wo(i - 2)
            ffn_T(18)
            ffn_AV(17)
            logits(2)
            ffn_wo(3)
            ffn_T(19)
            ffn_AV(18)
            rank(2)
            ffn_AV(19)
            flatT(3)
            ffn_yT(4)
            logits(3)
            ffn_wo(4)
            rank(3)
            flatT(4)
            logits(4)
            rank(4)

            def up_gate(s, u, j, e):
                if not isinstance(s, int):
                    pe.wait_ge(g_done, 2 * s + j - 1)
                for g in range(2):
                    for k in range(KC):
                        w = W13[:, bass.ds(e, 1), k, HID * g + HH * j:HID * g + HH * (j + 1)].rearrange("p a n -> p (a n)")
                        ins = nc.tensor.matmul(ps[:, 2 * j + g, 0:HH], xTb[:, u, k, :], w,
                                               start=(k == 0), stop=(k == KC - 1))
                ins.then_inc(ab_ps, 1)

            def gT(s, u):
                for j in range(2):
                    pe.wait_ge(g_done, 2 * s + j + 1)
                    for c in range(HC):
                        ins = nc.tensor.transpose(ps[0:HCW[c], 4 + j, 128 * c:128 * (c + 1)],
                                                  gb[:, u, j, 128 * c:128 * c + HCW[c]], ident)
                    ins.then_inc(gT_ps, 1)

            def down(s, e):
                pe.wait_ge(y_copied, s + 1)
                for j in range(2):
                    pe.wait_ge(gT_copied, 2 * s + j + 1)
                    for c in range(HC):
                        w = W2[0:HCW[c], bass.ds(e, 1), HC * j + c, :].rearrange("p a n -> p (a n)")
                        ins = nc.tensor.matmul(ps[:, 6, 0:D], hTb[0:HCW[c], j, c, :], w,
                                               start=(j == 0 and c == 0), stop=(j == 1 and c == HC - 1))
                ins.then_inc(y_ps, 1)

            def expert(s):
                return pe.value_load(blki[0:1, bass.ds(s, 1)], min_val=0, max_val=NE - 1)

            pe.wait_ge(blk_done, 1)
            pe.wait_ge(y_done, NT)
            pe.wait_ge(ET_done, 20)
            pe.wait_ge(x2_done, NT)
            pe.wait_ge(ld_w, 16 * (NE - NLATE))
            pe.wait_ge(ld_late, 16 * (4 * NE + NLATE))
            nc.tensor.matmul(ps[:, 4, :], zero16[:, 0:128], zero16, start=True, stop=True)
            nc.tensor.matmul(ps[:, 5, :], zero16[:, 0:128], zero16, start=True, stop=True)
            iters = pe.value_load(blki[0:1, 2 * NB:2 * NB + 1], min_val=1, max_val=(MAXB - 1) // 2)
            pe.wait_ge(xblk_ld[0], 16)
            two_transposes(7, xblk[:, 0, 0:D], 128).then_inc(mxT_ps, 1)
            e0 = expert(0)
            pe.wait_ge(mxT_done, 1)
            up_gate(0, 0, 0, e0)
            pe.wait_ge(xblk_ld[1], 16)
            two_transposes(7, xblk[:, 1, 0:D], 128).then_inc(mxT_ps, 1)
            up_gate(0, 0, 1, e0)
            with pe.Fori(0, iters) as m:
                for u, s in ((1, 2 * m + 1), (0, 2 * m + 2)):
                    e = expert(s)
                    pe.wait_ge(mxT_done, s + 1)
                    up_gate(s, u, 0, e)
                    pe.wait_ge(xblk_ld[1 - u], 16 * m + 32)
                    two_transposes(7, xblk[:, 1 - u, 0:D], 128).then_inc(mxT_ps, 1)
                    gT(s - 1, 1 - u)
                    up_gate(s, u, 1, e)
                    e_last = expert(s - 1)
                    down(s - 1, e_last)
            gT(2 * iters, 0)
            down(2 * iters, expert(2 * iters))

        @block.vector
        def _(dve):
            steps = [0]

            def link(ins):
                steps[0] += 1
                ins.then_inc(link_dve, 1)
                dve.wait_ge(link_dve, steps[0])

            def stats(src):
                for i in range(NT):
                    ins = nc.vector.bn_stats(st[:, i, :], src[:, i, :])
                link(ins)
                for i in range(NT):
                    ins = nc.vector.bn_aggr(mv[:, i, :], st[:, i, :])
                link(ins)
                return nc.vector.tensor_scalar(v_eps[:, 0:NT], mv[:, :, 1], EPS, None, ALU.add)

            dve.wait_ge(ld_x, 16)
            stats(X).then_inc(var1, 1)
            dve.wait_ge(ld_groups, 32)
            nc.vector.tensor_reduce(gmm[:, 0:1], edgesg, AX.X, ALU.min)
            nc.vector.tensor_reduce(gmm[:, 1:2], edgesg, AX.X, ALU.max).then_inc(gmm_done, 1)
            dve.wait_ge(rstd1, 1)
            for i in range(NT):
                nc.vector.tensor_scalar(xn[:, i, :], X[:, i, :], mv[:, i, 0:1], rstd[:, i:i + 1],
                                        ALU.subtract, ALU.mult).then_inc(xn_done, 1)
            dve.wait_ge(gmm_ps, 1)
            g = rr[:, 0:2 * NG].rearrange("p (k g) -> p k g", k=2)
            link(nc.vector.tensor_copy(rr[:, 0:2 * NG], ps[0:1, 7, 0:2 * NG]))
            bg = NT * NG
            r1 = rr[:, 80:80 + bg].rearrange("p (b g) -> p b g", b=NT)
            r2_ = rr[:, 280:280 + bg].rearrange("p (b g) -> p b g", b=NT)
            lo = crow[:, 0:bg].rearrange("p (b g) -> p b g", b=NT)
            hi = crow[:, 200:200 + bg].rearrange("p (b g) -> p b g", b=NT)
            up = crow[:, 400:400 + NG].unsqueeze(1).to_broadcast([1, NT, NG])
            down_ = crow[:, 440:440 + NG].unsqueeze(1).to_broadcast([1, NT, NG])
            nc.vector.tensor_tensor(r1, hi, g[:, 0:1, :].to_broadcast([1, NT, NG]), ALU.is_ge)
            link(nc.vector.tensor_tensor(r2_, lo, g[:, 1:2, :].to_broadcast([1, NT, NG]), ALU.is_le))
            link(nc.vector.tensor_tensor(r1, r1, r2_, ALU.mult))
            r3_ = rr[:, 480:480 + bg].rearrange("p (b g) -> p b g", b=NT)
            nc.vector.tensor_tensor(r2_, r1, down_, ALU.mult)
            link(nc.vector.tensor_tensor(r3_, r1, up, ALU.mult))
            nc.vector.tensor_reduce(rr[:, 700:705], r2_, AX.X, ALU.max)
            link(nc.vector.tensor_reduce(rr[:, 705:710], r3_, AX.X, ALU.max))
            link(nc.vector.tensor_scalar(rr[:, 710:715], rr[:, 700:705], -1.0, float(NG), ALU.mult, ALU.add))
            link(nc.vector.tensor_scalar(rr[:, 710:715], rr[:, 710:715], float(NG - 1), None, ALU.min))
            link(nc.vector.tensor_scalar(rr[:, 715:720], rr[:, 710:715], 1.0, None, ALU.add))
            link(nc.vector.tensor_tensor(rr[:, 715:720], rr[:, 715:720], rr[:, 705:710], ALU.max))
            nc.vector.tensor_copy(rangei[:, :, :].rearrange("p k b -> p (k b)"), rr[:, 710:720]).then_inc(range_done, 1)
            dve.wait_ge(range_done, 1)
            dve.wait_ge(ld_edges, 48)
            nc.vector.tensor_copy(srcf, srci)
            link(nc.vector.tensor_copy(dstf, dsti))
            for b in range(NT):
                ins = nc.vector.tensor_scalar(dstrel[:, b, :], dstf, float(TP * b), None, ALU.subtract)
            link(ins)
            seq = dve.alloc_register("dve_groups")
            slot = dve.alloc_register("dve_slot")
            dve.reg_mov(seq, 0)
            dve.reg_mov(slot, 0)
            dve.sem_inc(oh_used, SLOTS)
            for b in range(NT):
                first = dve.value_load(rangei[0:1, 0, b:b + 1], min_val=0, max_val=NG - 1)
                last = dve.value_load(rangei[0:1, 1, b:b + 1], min_val=1, max_val=NG)
                with dve.Fori(first, last) as gi:
                    done = dve.snap(seq, min_val=0, max_val=NT * NG)
                    r = ring[:, bass.ds(dve.snap(slot, min_val=0, max_val=SLOTS - 1), 1), :, :].rearrange("p a k n -> p (a k) n")
                    dve.wait_ge(oh_used, done + 1)
                    nc.vector.tensor_tensor(r[:, :, 640:768], iota16[:, 0:128].unsqueeze(1).to_broadcast([TP, EG, 128]),
                                            dstrel[:, b, bass.ds(EG * gi, EG)].unsqueeze(2).to_broadcast([TP, EG, 128]),
                                            ALU.is_equal)
                    for k in range(EG):
                        ins = nc.vector.tensor_scalar(r[:, k, 0:N], iota16, srcf[:, bass.ds(EG * gi + k, 1)], None,
                                                      ALU.is_equal)
                    ins.then_inc(oh_built, 1)
                    dve.reg_add(seq, seq, 1)
                    dve.reg_add(slot, slot, 1)
                    dve.reg_mod(slot, slot, SLOTS)
                if b == 0:
                    dve.wait_ge(ld_mix, 48)
                    link(nc.vector.tensor_reduce(wmean[:, :], wkv.rearrange("p k (h c) -> p (k h) c", c=C), AX.X, ALU.add))
                    nc.vector.tensor_scalar(wmean[:, :], wmean[:, :], 1.0 / C, None, ALU.mult).then_inc(wmean_done, 1)
            dve.wait_ge(cnt_done, 2 * NT)

            def mix_dbd():
                dve.wait_ge(dots_ps, 1)
                dve.wait_ge(consts_set, 3)
                for r in (0, 64):
                    ins = nc.vector.tensor_scalar(dbd[r:r + 64, :, r:r + 64],
                                                  ps[r:r + 64, 7, :].rearrange("p (e n) -> p e n", e=4)[:, :, r:r + 64],
                                                  1.0 / N, None, ALU.mult)
                ins.then_inc(dbd_done, 1)

            def mix_add(i):
                dve.wait_ge(mix_ps, i + 1)
                dve.wait_ge(xb_done, i + 1)
                nc.vector.tensor_tensor(x1[:, i, :], ps[0:TP, 7, 0:256], x1[:, i, :], ALU.add).then_inc(mix_used, 1)

            def gnn_weigh(n):
                dve.wait_ge(exp_done, n + 1)
                nc.vector.tensor_tensor_reduce(out=E[:, n % 3, :], in0=E[:, n % 3, :], in1=cnt[:, n // 4, :], scale=1.0,
                                               scalar=0.0, op0=ALU.mult, op1=ALU.add,
                                               accum_out=den[:, n:n + 1]).then_inc(A_done, 1)

            def gnn_out(i):
                dve.wait_ge(A_done, 4 * i + 4)
                link(nc.vector.tensor_scalar(rd[:, :], den[:, 4 * i:4 * i + 4], 1e-16, None, ALU.add))
                link(nc.vector.reciprocal(rd[:, :], rd[:, :]))
                dve.wait_ge(AV_done, 4 * i + 4)
                nc.vector.tensor_tensor(hrow[:, i, :].rearrange("p (h c) -> p h c", c=C),
                                        ps[0:TP, 6, 0:256].rearrange("p (h c) -> p h c", c=C),
                                        rd[:, :].unsqueeze(2).to_broadcast([TP, H, C]), ALU.mult).then_inc(O_used, 1)
                dve.wait_ge(O_used, i + 1)
                nc.vector.tensor_tensor(VS[:, i, D:512], VS[:, i, D:512], hrow[:, i, :], ALU.add).then_inc(agg_done, 1)

            for n in range(20):
                i = n // 4
                dve.wait_ge(S_ps, n + 1)
                dve.wait_ge(mask_done, i + 1)
                if n >= 3:
                    dve.wait_ge(AT_ps, n - 2)
                nc.vector.tensor_tensor_reduce(out=E[:, n % 3, :], in0=flat(2 * (n % 2))[0:TP, 0:N],
                                               in1=edge_mask[:, i, :], scale=1.0, scalar=3e38, op0=ALU.add, op1=ALU.min,
                                               accum_out=mn[:, n:n + 1]).then_inc(S_used, 1)
                if n:
                    gnn_weigh(n - 1)
                if n == 3:
                    mix_dbd()
                if n in MIX_OUT:
                    mix_add(MIX_OUT.index(n))
                if n % 4 == 2 and n > 4:
                    gnn_out(i - 1)
            gnn_weigh(19)
            gnn_out(NT - 1)
            dve.wait_ge(gelu_done, 1)
            dve.wait_ge(mix_used, NT)
            stats(VS[:, :, D:512]).then_inc(varg, 1)
            dve.wait_ge(rstdg, 1)
            for i in range(NT):
                ins = nc.vector.scalar_tensor_tensor(out=hrow[:, i, :], in0=VS[:, i, D:512], scalar=mv[:, i, 0:1],
                                                     in1=gamma, op0=ALU.subtract, op1=ALU.mult)
            link(ins)
            for i in range(NT):
                ins = nc.vector.scalar_tensor_tensor(out=x1[:, i, :], in0=hrow[:, i, :], scalar=rstd[:, i:i + 1],
                                                     in1=x1[:, i, :], op0=ALU.mult, op1=ALU.add)
            link(ins)
            stats(x1)
            nc.vector.tensor_scalar(v_eps[:, NT:2 * NT], mv[:, :, 1], 1.0 + EPS_RMS, EPS * EPS_RMS, ALU.mult,
                                    ALU.add).then_inc(var2, 1)
            dve.wait_ge(r2, 1)
            for i in range(NT):
                nc.vector.tensor_scalar(hrow[:, i, :], x1[:, i, :], mv[:, i, 0:1], rstd[:, NT + i:NT + i + 1],
                                        ALU.subtract, ALU.mult).then_inc(h_done, 1)
            for i in range(NT):
                nc.vector.tensor_scalar(xn[:, i, :], x1[:, i, :], mv[:, i, 0:1], rstd[:, i:i + 1], ALU.subtract, ALU.mult)
            dve.wait_ge(ld_const, 32)
            rot = rt[:, 64:64 + 768].rearrange("p (k n) -> p k n", k=2)
            for i in range(NT):
                dve.wait_ge(qkv_ps, i + 1)
                qk = ps[0:TP, 2 + i % 2, 0:384].rearrange("p (h s c) -> p h s c", h=6, s=2)
                ra = rot[:, 0, :].rearrange("p (h s c) -> p h s c", h=6, s=2)
                rb = rot[:, 1, :].rearrange("p (h s c) -> p h s c", h=6, s=2)
                cos = rope[:, 0, i, :].unsqueeze(1).to_broadcast([TP, 6, C])
                sin = rope[:, 1, i, :].rearrange("p (s c) -> p s c", s=2)
                nc.vector.tensor_tensor(rot[:, 0, :].rearrange("p (h c) -> p h c", h=6),
                                        ps[0:TP, 2 + i % 2, 0:384].rearrange("p (h c) -> p h c", h=6), cos, ALU.mult)
                for a in range(2):
                    ins = nc.vector.tensor_tensor(rb[:, :, a, :], qk[:, :, 1 - a, :],
                                                  sin[:, a:a + 1, :].to_broadcast([TP, 6, 32]), ALU.mult)
                ins.then_inc(qkv_used, 1)
                dve.wait_ge(qkv_used, i + 1)
                if i:
                    dve.wait_ge(qkT_ps, i)
                nc.vector.tensor_tensor(qkr, rot[:, 0, :], rot[:, 1, :], ALU.add).then_inc(qkr_done, 1)
                dve.wait_ge(qkr_done, i + 1)

            def ffn_y(i):
                dve.wait_ge(exp2_done, 4 * i + 4)
                link(nc.vector.reciprocal(rd[:, :], den2[:, 4 * i:4 * i + 4]))
                dve.wait_ge(AV2_done, 4 * i + 4)
                nc.vector.tensor_tensor(yat[:, i % 2, :].rearrange("p (h c) -> p h c", c=C),
                                        ps[0:TP, 6, 0:256].rearrange("p (h c) -> p h c", c=C),
                                        rd[:, :].unsqueeze(2).to_broadcast([TP, H, C]), ALU.mult).then_inc(y_done, 1)
                dve.wait_ge(y_done, i + 1)
                dve.sem_inc(O2_used, 1)

            def ffn_x2(i):
                dve.wait_ge(wo_ps, i + 1)
                nc.vector.tensor_tensor(xn[:, i, :], ps[0:TP, 7, 256:512], xn[:, i, :], ALU.add).then_inc(x2_done, 1)
                dve.wait_ge(x2_done, i + 1)
                link(nc.vector.tensor_tensor_reduce(out=rt[:, 400:656], in0=xn[:, i, :], in1=xn[:, i, :], scale=1.0 / D,
                                                    scalar=0.0, op0=ALU.mult, op1=ALU.add, accum_out=rt[:, 30 + i:31 + i]))
                nc.vector.tensor_scalar(v_eps[:, i:i + 1], rt[:, 30 + i:31 + i], EPS_RMS, None, ALU.add).then_inc(ms3, 1)

            def flat_rows(i):
                if i >= 2:
                    dve.wait_ge(scattered[i % 2], 32 * (i // 2))
                dve.wait_ge(r3, i + 1)
                for k in range(2):
                    ins = nc.vector.scalar_tensor_tensor(out=rowbuf[:, i % 2, k, 0:D], in0=xn[:, i, :],
                                                         scalar=rstd[:, i:i + 1], in1=ln2, op0=ALU.mult, op1=ALU.mult)
                    if k == 0:
                        ins.then_inc(flat_done, 1)
                nc.vector.tensor_copy(rowbuf[:, i % 2, :, D + 1:D + 2],
                                      ids[:, i:i + 1].unsqueeze(1).to_broadcast([TP, 2, 1]))

            def top2(i):
                dve.wait_ge(logit_ps, i + 1)
                link(nc.vector.tensor_copy(R(i, 0, 8), ps[0:TP, LG_BANK[i], 256:256 + NE]))
                link(nc.vector.max(out=R(i, 8, 8), in_=R(i, 0, 8)))
                nc.vector.tensor_scalar(R(i, 52, 1), R(i, 8, 1), -1.0, None, ALU.mult).then_inc(rmax_done, 1)
                link(nc.vector.max_index(out=rti[:, 8 * i:8 * i + 8], in_max=R(i, 8, 8), in_values=R(i, 0, 8)))
                link(nc.vector.tensor_copy(R(i, 24, 2), rti[:, 8 * i:8 * i + 2]))
                oh = R(i, 32, 16).rearrange("p (k e) -> p k e", k=2)
                link(nc.vector.tensor_tensor(oh, iota8.unsqueeze(1).to_broadcast([TP, 2, NE]),
                                             R(i, 24, 2).unsqueeze(2).to_broadcast([TP, 2, NE]), ALU.is_equal))
                nc.vector.tensor_tensor(sel_of(i), oh[:, 0, :], oh[:, 1, :], ALU.add).then_inc(sel_done, 1)

            def slots(i):
                dve.wait_ge(rexp_done, i + 1)
                link(nc.vector.tensor_scalar(R(i, 26, 1), R(i, 53, 1), 1e-9, 1.0, ALU.mult, ALU.add))
                link(nc.vector.tensor_tensor(R(i, 26, 1), R(i, 26, 1), R(i, 17, 1), ALU.add))
                link(nc.vector.reciprocal(R(i, 27, 1), R(i, 26, 1)))
                nc.vector.tensor_copy(rowbuf[:, i % 2, 0, D:D + 1], R(i, 27, 1))
                nc.vector.tensor_tensor(rowbuf[:, i % 2, 1, D:D + 1], R(i, 27, 1), R(i, 17, 1), ALU.mult)
                dve.wait_ge(rank_ps, i + 1)
                oh = R(i, 32, 16).rearrange("p (k e) -> p k e", k=2)
                nc.vector.tensor_tensor(R(i, 54, 8), ps[0:TP, LG_BANK[i], 272:272 + NE], region, ALU.add).then_inc(rank_used, 1)
                dve.wait_ge(rank_used, i + 1)
                link(nc.vector.tensor_tensor(oh, oh, R(i, 54, 8).unsqueeze(1).to_broadcast([TP, 2, NE]), ALU.mult))
                link(nc.vector.tensor_reduce(R(i, 28, 2), oh, AX.X, ALU.add))
                nc.vector.tensor_copy(rti[:, 40 + 2 * i:42 + 2 * i], R(i, 28, 2)).then_inc(slot_done, 1)

            for n in range(20):
                i = n // 4
                dve.wait_ge(S2_ps, n + 1)
                nc.vector.tensor_reduce(mn2[:, n:n + 1], flat(2 * (n % 2))[0:TP, 0:TP * (i + 1)], AX.X, ALU.max,
                                        negate=True).then_inc(max2_done, 1)
                if n % 4 == 2 and n >= 6:
                    ffn_y(i - 1)
                if n % 4 == 0 and n >= 8:
                    ffn_x2(i - 2)
                if n % 4 == 1 and n >= 9:
                    flat_rows(i - 2)
                if n % 4 == 3 and n >= 11 and n < 19:
                    top2(i - 2)
                if n % 4 == 0 and n >= 12:
                    slots(i - 3)
            top2(2)
            ffn_x2(3)
            slots(2)
            flat_rows(3)
            ffn_y(4)
            top2(3)
            ffn_x2(4)
            slots(3)
            flat_rows(4)
            top2(4)
            slots(4)
            tot = ps[0:1, LG_BANK[NT - 1], 288:288 + NE]
            blks, upto = rr[:, 700:708], rr[:, 708:716]
            link(nc.vector.tensor_tensor(rr[:, 640:680].rearrange("p (e k) -> p e k", e=NE),
                                         tot.unsqueeze(2).to_broadcast([1, NE, 5]),
                                         thr[0:1, :].unsqueeze(1).to_broadcast([1, NE, 5]), ALU.is_gt))
            link(nc.vector.tensor_reduce(blks, rr[:, 640:680].rearrange("p (e k) -> p e k", e=NE), AX.X, ALU.add))
            link(nc.vector.tensor_tensor_scan(upto, cf[0:1, 160:168], blks, 0.0, ALU.mult, ALU.add))
            e_of = rr[:, 720:720 + NB * NE].rearrange("p (g e) -> p g e", g=NB)
            e_blk = rr[:, 0:NB * NE].rearrange("p (g e) -> p g e", g=NB)
            link(nc.vector.tensor_tensor(e_of, upto.unsqueeze(1).to_broadcast([1, NB, NE]),
                                         crow[:, 480:480 + NB].unsqueeze(2).to_broadcast([1, NB, NE]), ALU.is_le))
            nc.vector.tensor_tensor(rr[:, 600:608], upto[:, 7:8].to_broadcast([1, 8]), crow[:, 500:508], ALU.is_gt)
            link(nc.vector.tensor_tensor(e_blk, e_of, blks.unsqueeze(1).to_broadcast([1, NB, NE]), ALU.mult))
            nc.vector.tensor_reduce(rr[:, 200:200 + NB], e_of, AX.X, ALU.add)
            nc.vector.tensor_reduce(rr[:, 236:237], rr[:, 600:608], AX.X, ALU.add)
            link(nc.vector.tensor_reduce(rr[:, 240:240 + NB], e_blk, AX.X, ALU.add))
            link(nc.vector.tensor_tensor(rr[:, 240:240 + NB], crow[:, 480:480 + NB], rr[:, 240:240 + NB], ALU.subtract))
            link(nc.vector.tensor_scalar(rr[:, 240:240 + NB], rr[:, 240:240 + NB], 128.0, None, ALU.mult))
            link(nc.vector.scalar_tensor_tensor(out=rr[:, 218:218 + NB], in0=rr[:, 200:200 + NB], scalar=float(CAP),
                                                in1=rr[:, 240:240 + NB], op0=ALU.mult, op1=ALU.add))
            nc.vector.tensor_scalar(rr[:, 200:200 + NB], rr[:, 200:200 + NB], float(NE - 1), None, ALU.min)
            link(nc.vector.tensor_scalar(rr[:, 218:218 + NB], rr[:, 218:218 + NB], float(NE * CAP), None, ALU.min))
            nc.vector.tensor_copy(blki[:, 0:2 * NB + 1], rr[:, 200:201 + 2 * NB]).then_inc(blk_done, 1)
            dve.wait_ge(blk_done, 1)

            def gate(s, u, j):
                dve.wait_ge(silu_done, 2 * s + j + 1)
                nc.vector.tensor_tensor(gb[:, u, j, :], ps[:, 2 * j + 1, 0:HH], sl[:, j, :], ALU.mult).then_inc(g_done, 1)

            iters = dve.value_load(blki[0:1, 2 * NB:2 * NB + 1], min_val=1, max_val=(MAXB - 1) // 2)
            dve.sem_inc(y_copied, 1)
            dve.sem_inc(y_free, 2)

            def y_copy(s, u):
                dve.wait_ge(y_ps, s + 1)
                dve.wait_ge(y_free, s + 1)
                nc.vector.tensor_scalar(yb[:, u, :], ps[:, 6, 0:D], slot_w[:, u:u + 1], None,
                                        ALU.mult).then_inc(y_copied, 1)

            def meta(u, s):
                dve.wait_ge(y_free, s + 1)
                dve.wait_ge(xblk_ld[u], s // 2 * 16 + 16 if isinstance(s, int) else 16 * m + 16 + 16 * (1 - u))
                nc.vector.tensor_copy(slot_w[:, u:u + 1], xblk[:, u, D:D + 1])
                nc.vector.tensor_copy(slot_id[:, u:u + 1], xblk[:, u, D + 1:D + 2]).then_inc(meta_done, 1)

            gate(0, 0, 0)
            gate(0, 0, 1)
            meta(0, 0)
            with dve.Fori(0, iters) as m:
                for u, s in ((1, 2 * m + 1), (0, 2 * m + 2)):
                    gate(s, u, 0)
                    gate(s, u, 1)
                    meta(u, s)
                    y_copy(s - 1, 1 - u)
            y_copy(2 * iters, 0)


def laid_out(a):
    def cols(w):
        n, k = w.shape
        return w.T.reshape(k // 128, 128, n).transpose(1, 0, 2)

    def krows(w):
        k, n = w.shape
        return w.reshape(k // 128, 128, n).transpose(1, 0, 2)

    g = "L0_gnn_"
    f = "L0_ffn_"
    src, dst = a["src"], a["dst"]
    wq = a[f + "wq"].reshape(H, C, D)[[0, 2, 1, 3]].reshape(D, D)
    mix = a["L0_mix_w_qkv"]
    w13 = np.concatenate([a[f + "w1"], a[f + "w3"]], axis=1)
    ident = np.eye(128, dtype=np.float32)
    c_f32 = np.zeros((128, 288), np.float32)
    c_f32[:, 0:128] = ident
    c_f32[:, 128:136] = np.arange(8)
    c_f32[:, 136:141] = np.arange(5) * 128
    c_f32[:, 141:146] = np.arange(128)[:, None] + TP * np.arange(NT)
    c_f32[:, 146:154] = CAP * np.arange(NE)
    c_f32[:, 160:168] = 1.0
    c_pad = np.zeros((128, RW), np.float32)
    c_pad[:, D + 1] = N + np.arange(128)
    bf = mybir.dt.np(bf16)
    r = np.arange(128)
    c_bf = np.zeros((128, 512), np.float32)
    c_bf[:, 0:128] = r[:, None] < r[None, :]
    c_bf[:, 128:256] = 1.0
    c_bf[:, 256:384] = ident
    c_bf[:, 384:512] = np.where(r[None, :] > r[:, None], -BIG, 0.0)
    inv_freq = 1.0 / 10000.0 ** (np.arange(0, C, 2, dtype=np.float32) / C)
    freqs = np.outer(np.arange(N, dtype=np.float32), inv_freq)
    cos, sin = np.cos(freqs), np.sin(freqs)
    c_rope = np.stack([np.concatenate([cos, cos], 1), np.concatenate([-sin, sin], 1)])
    c_row = np.zeros((1, 512), np.float32)
    b = np.arange(NT)
    c_row[0, 0:NT * NG] = np.repeat(TP * b, NG)
    c_row[0, 200:200 + NT * NG] = np.repeat(TP * b + TP - 1, NG)
    c_row[0, 400:400 + NG] = np.arange(NG) + 1
    c_row[0, 440:440 + NG] = NG - np.arange(NG)
    c_row[0, 480:480 + NB] = np.arange(NB)
    c_row[0, 500:508] = 2 * np.arange(8) + 1
    return dict(
        x_in=a["x"],
        edge_groups=dst.reshape(NG, EG * TP),
        edge_src=src.reshape(ET, TP).T,
        edge_dst=dst.reshape(ET, TP).T,
        w_gnn=krows(np.concatenate([a[g + "Wq"], a[g + "Wk"], a[g + "Wv"], a[g + "Wskip"]], axis=1)),
        b_gnn_qk=np.concatenate([a[g + "bq"], a[g + "bk"]]).reshape(4, 128).T,
        b_gnn_vs=np.concatenate([a[g + "bv"], a[g + "bskip"]]),
        w_mix_kv=cols(mix[MI:3 * MI]),
        w_mix_q=mix[0:MI].reshape(4, 128, D).transpose(1, 0, 2),
        w_mix_out=cols(a["L0_mix_w_out"]),
        rows=np.stack([a[g + "gamma"], a[g + "beta_ln"], a["L0_mix_b_out"], a[f + "ln2_w"]]),
        w_ffn_qkv=cols(np.concatenate([wq, a[f + "wk"], a[f + "wv"]])),
        w_ffn_o=cols(a[f + "wo"]),
        ln1_col=a[f + "ln1_w"].reshape(KC, 128).T,
        w_router=cols(a[f + "router_w"]),
        w13=w13.transpose(0, 2, 1).reshape(NE, KC, 128, 2 * HID).transpose(2, 0, 1, 3),
        w2=a[f + "w2"].transpose(0, 2, 1),
        c_f32=c_f32,
        c_bf16=c_bf.astype(bf),
        c_iota=np.arange(N).astype(np.float16),
        c_rope=c_rope.reshape(2, NT, TP, C).transpose(2, 0, 1, 3).astype(np.float32),
        c_row=c_row,
        c_pad=c_pad,
    )


def kernel(**inputs):
    import concourse.bacc as _bacc
    from concourse.bass_utils import run_bass_kernel_spmd as _run

    nc = _bacc.Bacc("TRN2", target_bir_lowering=False, num_devices=1)
    arrays = {k: np.ascontiguousarray(v) for k, v in laid_out({k: np.asarray(v) for k, v in inputs.items()}).items()}
    args = [nc.dram_tensor(k, v.shape, mybir.dt.from_np(v.dtype), kind="ExternalInput").ap() for k, v in arrays.items()]
    args.append(nc.dram_tensor("out", (N, D), fp32, kind="ExternalOutput").ap())
    build(nc, *args)
    r = _run(nc, [arrays], core_ids=[0])
    return r.results[0]["out"]
```

```python
import numpy as np
import concourse.bass as bass
from concourse import mybir
from contextlib import ExitStack

fp32 = mybir.dt.float32
bf16 = mybir.dt.bfloat16
fp16 = mybir.dt.float16
i32 = mybir.dt.int32
u32 = mybir.dt.uint32
ALU = mybir.AluOpType
ACT = mybir.ActivationFunctionType
AX = mybir.AxisListType

N, D = 625, 256
NT, TP = 5, 125
KC = D // 128
H, C = 4, 64
EDGES = 20000
ET = EDGES // TP
EG = 5
NG = ET // EG
SLOTS = 5
MH = 8
MI = MH * C
NE, HID = 8, 682
HH = HID // 2
HC = 3
HCW = (128, 128, HH - 256)
MAXB = 17
NB = MAXB + 1
CAP = 640
RW = D + 2
XROWS = NE * CAP + 128
EPS = 1e-5
EPS_RMS = 1e-6
BIG = 1e30


def build(nc, x, edge_groups, edge_src, edge_dst, w_gnn, b_gnn_qk, b_gnn_vs, w_mix_kv, w_mix_q,
          w_mix_out, rows, w_ffn_qkv, w_ffn_o, ln1_col, w_router, w13, w2, c_f32, c_bf16, c_iota,
          c_rope, c_row, c_pad, out):
    xg = nc.dram_tensor("xg_scratch", (XROWS, RW), fp32, kind="Internal").ap()
    acc = nc.dram_tensor("acc_scratch", (N + 128, D), fp32, kind="Internal").ap()
    ctx = ExitStack()
    with ctx:
        def sb(name, shape, dt=fp32):
            return ctx.enter_context(nc.sbuf_tensor(name, shape, dt))

        def sem(name):
            return ctx.enter_context(nc.semaphore(name))

        ATT = 3140
        attn_w13 = sb("attn_w13", [128, ATT + NE * KC * 2 * HID])
        W13 = attn_w13[:, ATT:].rearrange("p (e k n) -> p e k n", e=NE, k=KC)
        W2 = sb("W2", [128, NE, 2 * HC, D])
        w2_flat = W2[:, :, :, :].rearrange("p e k d -> p (e k d)")
        kvc = w2_flat[:, 0:5120].rearrange("p (i n) -> p i n", i=NT)
        wgnn = w2_flat[:, 5120:7168].rearrange("p (k n) -> p k n", k=KC)
        wkv = w2_flat[:, 7168:9216].rearrange("p (k n) -> p k n", k=KC)
        wmq = w2_flat[:, 9216:10240].rearrange("p (e n) -> p e n", e=4)
        wmo = w2_flat[:, 10240:11264].rearrange("p (e n) -> p e n", e=4)
        M1 = w2_flat[:, 11264:12288].rearrange("p (e n) -> p e n", e=4)
        NLATE = 5
        late_flat = W13[:, NE - NLATE:NE, :, :].rearrange("p e k n -> p (e k n)")
        VS = late_flat[0:TP, 0:2560].rearrange("p (i n) -> p i n", i=NT)
        gqkT = late_flat[:, 2560:5060].rearrange("p (m n) -> p m n", m=4)
        edge_mask = late_flat[:, 5060:6624].bitcast(bf16)[0:TP, 0:3125].rearrange("p (i n) -> p i n", i=NT)
        X = late_flat[0:TP, 6624:7904].rearrange("p (i n) -> p i n", i=NT)

        cnt = late_flat[0:TP, 7904:11029].rearrange("p (i n) -> p i n", i=NT)
        edgesg = late_flat[0:NG, 7904:7904 + EG * TP].bitcast(i32)
        dbd = late_flat[:, 11029:11541].rearrange("p (e n) -> p e n", e=4)
        bvs = late_flat[0:TP, 11541:12053]
        M2 = late_flat[:, 12053:12565].rearrange("p (k n) -> p k n", k=KC)
        pad = late_flat[:, 12565:12565 + RW]
        rowv = late_flat[0:TP, 12823:13591].rearrange("p (k n) -> p k n", k=3)
        gamma, beta, bout = (rowv[:, k, :] for k in range(3))

        CM = sb("CM", [128, 4352])
        AT = CM[0:TP, 0:1250].rearrange("p (u j n) -> p u j n", u=2, j=NT)
        rope = CM[0:TP, 1250:1890].rearrange("p (k i c) -> p k i c", k=2, i=NT)
        yat = CM[0:TP, 1890:2402].rearrange("p (u n) -> p u n", u=2)
        yT = CM[:, 2402:2902].rearrange("p (u k n) -> p u k n", u=2, k=KC)
        wqkv = CM[:, 2902:3926].rearrange("p (k n) -> p k n", k=KC)
        zero16 = CM[:, 3926:4182].bitcast(fp16)
        xblk = CM[:, 0:2 * RW].rearrange("p (u n) -> p u n", u=2)
        xTb = CM[:, 516:1028].rearrange("p (u k n) -> p u k n", u=2, k=KC)
        gb = CM[:, 1028:1028 + 4 * HH].rearrange("p (u j n) -> p u j n", u=2, j=2)
        hTb = CM[:, 2392:2392 + 768].rearrange("p (j k n) -> p j k n", j=2, k=HC)
        sl = CM[:, 3160:3160 + 2 * HH].rearrange("p (j n) -> p j n", j=2)

        NEARLY = 3
        ring = attn_w13[0:TP, 0:SLOTS * EG * 384].bitcast(fp16)
        ring = ring.rearrange("p (s k n) -> p s k n", s=SLOTS, k=EG)

        QKV_MEM = attn_w13[:, 0:ATT]
        QKT = QKV_MEM[:, 0:1875].rearrange("p (m n) -> p m n", m=3)
        Vc = QKV_MEM[0:TP, 1875:1875 + 640].rearrange("p (i n) -> p i n", i=NT)
        qkr = QKV_MEM[0:TP, 2515:2515 + 384]
        yb = QKV_MEM[:, 0:512].rearrange("p (u n) -> p u n", u=2)

        ER = sb("ER", [128, 1888])
        E = ER[0:TP, 0:1875].rearrange("p (s n) -> p s n", s=3)
        dstf = ER[0:TP, 0:160]
        srcf = ER[0:TP, 160:320]
        dstrel = ER[0:TP, 320:1120].rearrange("p (b t) -> p b t", b=NT)
        dsti = ER[0:TP, 1120:1280].bitcast(i32)
        srci = ER[0:TP, 1280:1440].bitcast(i32)
        iota16 = ER[0:TP, 1440:1756].bitcast(fp16)[:, 0:N]

        xnT = sb("xnT", [128, KC, N])
        xn = sb("xn", [TP, NT, D])
        x1 = sb("x1", [TP, NT, D])
        hrow = sb("hrow", [TP, NT, D])
        rowbuf = hrow[:, :, :].rearrange("p i n -> p (i n)")[:, 0:4 * RW].rearrange("p (u k n) -> p u k n", u=2, k=2)
        wo = sb("wo", [128, KC, D])
        wr = sb("wr", [128, KC, NE])
        ln1c = sb("ln1c", [128, KC])
        bqk = sb("bqk", [128, 4])
        ln2r = sb("ln2r", [TP, D])
        ln2 = ln2r[:, :]
        cf = sb("cf", [128, 128 + 160])
        ident = cf[:, 0:128]
        iota8 = cf[0:TP, 128:136]
        thr = cf[0:TP, 136:141]
        ids = cf[0:TP, 141:146]
        region = cf[0:TP, 146:154]
        cbf = sb("cbf", [128, 4 * 128], bf16)
        tri = cbf[0:TP, 0:TP]
        ones = cbf[0:TP, 128:128 + TP]
        identb = cbf[0:TP, 256:256 + TP]
        causal = cbf[0:TP, 384:384 + TP]
        powm = sb("powm", [TP, 80])
        st = sb("st", [TP, NT, 6])
        mv = sb("mv", [TP, NT, 2])
        v_eps = sb("v_eps", [TP, 2 * NT])
        rstd = sb("rstd", [TP, 2 * NT])
        wmean = sb("wmean", [128, 32])
        ss = sb("ss", [TP, NT, 16])
        ssp = sb("ssp", [TP, NT, 8])
        rkv = sb("rkv", [TP, NT, 8])
        gmm = sb("gmm", [NG, 2])
        crow = sb("crow", [1, 512])
        rr = sb("rr", [1, 920])
        rangei = sb("rangei", [1, 2, NT], i32)
        mn = sb("mn", [TP, 20])
        den = sb("den", [TP, 20])
        rd = sb("rd", [TP, 4])
        mn2 = sb("mn2", [TP, 20])
        den2 = sb("den2", [TP, 20])
        rt = sb("rt", [TP, 864])
        rti = sb("rti", [TP, 64], u32)
        blki = sb("blki", [1, 2 * NB + 4], i32)
        slot_w = sb("slot_w", [128, 2])
        slot_id = sb("slot_id", [128, 2], i32)
        warm = sb("warm", [1, 8])
        ps = ctx.enter_context(nc.psum_tensor("ps", [128, 8, 512], fp32))

        def flat(b, n=1024):
            return ps[:, b:b + (n + 511) // 512, :].rearrange("p b n -> p (b n)")[:, 0:n]

        ld_x, ld_ident, ld_groups, ld_const, ld_edges, ld_gnn, ld_mix, ld_ffn, ld_rows = (
            sem(n) for n in ("ld_x", "ld_ident", "ld_groups", "ld_const", "ld_edges", "ld_gnn", "ld_mix", "ld_ffn", "ld_rows"))
        ld_w, ld_late, xg_emptied = sem("ld_w"), sem("ld_late"), sem("xg_emptied")
        ld_pad, acc_emptied, acc_stored = sem("ld_pad"), sem("acc_emptied"), sem("acc_stored")
        link_dve, link_pool = sem("link_dve"), sem("link_pool")
        consts_set = sem("consts_set")
        var1, rstd1, xn_done, xnT_ps, xnT_done = (
            sem(n) for n in ("var1", "rstd1", "xn_done", "xnT_ps", "xnT_done"))
        bq_scaled, qk_ps, qk_done, vs_ps, vs_copied, vs_done = (
            sem(n) for n in ("bq_scaled", "qk_ps", "qk_done", "vs_ps", "vs_copied", "vs_done"))
        gmm_done, gmm_ps, range_done = sem("gmm_done"), sem("gmm_ps"), sem("range_done")
        oh_built, oh_used, cnt_ps, cnt_done, mask_done = (
            sem(n) for n in ("oh_built", "oh_used", "cnt_ps", "cnt_done", "mask_done"))
        wmean_done, wkv_centred, kv_ps, kv_copied, sq_done, kv_normed, mix_ps, mix_used = (
            sem(n) for n in ("wmean_done", "wkv_centred", "kv_ps", "kv_copied", "sq_done", "kv_normed", "mix_ps",
                             "mix_used"))
        dots_ps, dbd_done, M1_ps, M1_done, M2_ps, M2_done = (
            sem(n) for n in ("dots_ps", "dbd_done", "M1_ps", "M1_done", "M2_ps", "M2_done"))
        xb_done, S_ps, S_used, exp_done, A_done, AT_ps, AT_done, AV_done, O_used, gelu_done = (
            sem(n) for n in ("xb_done", "S_ps", "S_used", "exp_done", "A_done", "AT_ps", "AT_done",
                             "AV_done", "O_used", "gelu_done"))
        agg_done, varg, rstdg, var2, r2 = (sem(n) for n in ("agg_done", "varg", "rstdg", "var2", "r2"))
        h_done, hT_ps, hT_done, qkv_ps, qkr_done, vc_done, qkT_ps, qkT_done = (
            sem(n) for n in ("h_done", "hT_ps", "hT_done", "qkv_ps", "qkr_done", "vc_done", "qkT_ps",
                             "qkT_done"))
        qkv_used = sem("qkv_used")
        S2_ps, max2_done, exp2_done, ET_ps, ET_done, AV2_done, y_done, O2_used = (
            sem(n) for n in ("S2_ps", "max2_done", "exp2_done", "ET_ps", "ET_done", "AV2_done",
                             "y_done", "O2_used"))
        yT_ps, yT_done, wo_ps, x2_done = (sem(n) for n in ("yT_ps", "yT_done", "wo_ps", "x2_done"))
        ms3, r3, flat_done, flatT_ps, flatT_done, logit_ps = (
            sem(n) for n in ("ms3", "r3", "flat_done", "flatT_ps", "flatT_done", "logit_ps"))
        rmax_done, rexp_done, sel_done, rank_ps, rank_used, blk_done, slot_done, weights_done = (
            sem(n) for n in ("rmax_done", "rexp_done", "sel_done", "rank_ps", "rank_used", "blk_done",
                             "slot_done", "weights_done"))
        logits_read, total_ps = sem("logits_read"), sem("total_ps")
        scattered = [sem("scattered0"), sem("scattered1")]
        xblk_ld = [sem("xblk_ld0"), sem("xblk_ld1")]
        y_added, last_y_added, y_free = sem("y_added"), sem("last_y_added"), sem("y_free")
        y_seen = sem("y_seen")
        mxT_ps, mxT_done, ab_ps, silu_done, g_done, gT_ps, gT_copied, y_ps, y_copied = (
            sem(n) for n in ("mxT_ps", "mxT_done", "ab_ps", "silu_done", "g_done", "gT_ps",
                             "gT_copied", "y_ps", "y_copied"))
        res_done, meta_done, out_stored = sem("res_done"), sem("meta_done"), sem("out_stored")

        block = ctx.enter_context(nc.Block())

        MIX_OUT = (9, 10, 13, 14, 17)

        QKV_BANK = (2, 3, 6, 2, 3)

        FT_BANK = (5, 5, 7, 0, 2)
        LG_BANK = (5, 5, 1, 1, 3)

        def R(i, a, n):
            return rt[:, 64 * (i + 1) + a:64 * (i + 1) + a + n]

        def sel_of(i):
            return rt[:, 840 + 4 * i:844 + 4 * i].bitcast(bf16)

        VS_TILES = ((0, 3), (3, NT), (NT, NT), (NT, NT), (NT, NT))
        KV_TILES = ((0, 0), (0, 1), (1, 3), (3, 4), (4, NT))

        PARTS = ((0, 3), (3, NT))

        HALVES = ((0, 313), (313, 625))

        @block.sync
        def _(sp):
            sp.dma_start(X, x.rearrange("(i p) c -> p i c", p=TP)).then_inc(ld_x, 16)
            sp.dma_start(cf[:, :], c_f32).then_inc(ld_ident, 16)
            sp.dma_start(edgesg, edge_groups).then_inc(ld_groups, 16)
            sp.dma_start(crow[:, :], c_row).then_inc(ld_groups, 16)
            sp.dma_start(dsti, edge_dst).then_inc(ld_edges, 16)
            sp.dma_start(srci, edge_src).then_inc(ld_edges, 16)
            sp.dma_start(iota16, c_iota.partition_broadcast(TP)).then_inc(ld_edges, 16)
            sp.dma_start(wgnn, w_gnn).then_inc(ld_gnn, 16)
            sp.dma_start(bqk[:, :], b_gnn_qk).then_inc(ld_gnn, 16)
            sp.dma_start(bvs, b_gnn_vs.partition_broadcast(TP)).then_inc(ld_gnn, 16)
            sp.dma_start(wkv, w_mix_kv).then_inc(ld_mix, 16)
            sp.dma_start(wmq, w_mix_q).then_inc(ld_mix, 16)
            sp.dma_start(wmo, w_mix_out).then_inc(ld_mix, 16)
            sp.dma_start(rowv, rows[0:3, :].partition_broadcast(TP)).then_inc(ld_rows, 16)
            sp.dma_start(ln2, rows[3, :].partition_broadcast(TP)).then_inc(ld_rows, 16)
            sp.dma_start(cbf[:, :], c_bf16).then_inc(ld_const, 16)
            sp.dma_start(rope, c_rope).then_inc(ld_const, 16)
            sp.dma_start(wqkv, w_ffn_qkv).then_inc(ld_ffn, 16)
            sp.dma_start(wo[:, :, :], w_ffn_o).then_inc(ld_ffn, 16)
            sp.dma_start(wr[:, :, :], w_router).then_inc(ld_ffn, 16)
            sp.dma_start(ln1c[:, :], ln1_col).then_inc(ld_ffn, 16)
            for e in range(NEARLY, NE - NLATE):
                sp.dma_start(W13[:, e, :, :], w13[:, e, :, :]).then_inc(ld_w, 16)
            sp.dma_start(pad, c_pad).then_inc(ld_pad, 16)
            sp.wait_ge(ld_pad, 16)
            sp.dma_start(xg.rearrange("(j p) c -> p j c", p=128),
                         pad.unsqueeze(1).to_broadcast([128, XROWS // 128, RW])).then_inc(xg_emptied, 16)
            sp.dma_start(acc[N:N + 128, :], pad[:, 0:D]).then_inc(acc_emptied, 16)
            sp.wait_ge(cnt_ps, NT)
            for e in range(NEARLY):
                sp.dma_start(W13[:, e, :, :], w13[:, e, :, :]).then_inc(ld_w, 16)
            sp.wait_ge(M2_done, 1)
            for e in range(NE):
                for j in range(2):
                    sp.dma_start(W2[:, e, HC * j:HC * j + 2, :],
                                 w2[e, HH * j:HH * j + 256, :].rearrange("(k p) d -> p k d", p=128)
                                 ).then_inc(ld_late, 16)
                    sp.dma_start(W2[0:HCW[2], e, HC * j + 2, :],
                                 w2[e, HH * j + 256:HH * (j + 1), :]).then_inc(ld_late, 16)
            sp.wait_ge(xg_emptied, 16)
            sp.wait_ge(acc_emptied, 16)
            sp.wait_ge(var2, 2)
            for e in range(NE - NLATE, NE):
                sp.dma_start(W13[:, e, :, :], w13[:, e, :, :]).then_inc(ld_late, 16)
            for i in range(NT):
                sp.wait_ge(res_done, i + 1)
                sp.dma_start(acc[i * TP:(i + 1) * TP, :], x1[:, i, :]).then_inc(acc_stored, 16)
            def rows_of(s):
                return sp.value_load(blki[0:1, bass.ds(s + NB, 1)], min_val=0, max_val=NE * CAP)

            sp.wait_ge(blk_done, 1)
            first = rows_of(0)
            sp.wait_ge(scattered[0], 32 * 3)
            sp.wait_ge(scattered[1], 32 * 2)
            sp.dma_start(xblk[:, 0, :], xg[bass.ds(first, 128), :]).then_inc(xblk_ld[0], 16)
            second = rows_of(1)
            sp.dma_start(xblk[:, 1, :], xg[bass.ds(second, 128), :]).then_inc(xblk_ld[1], 16)
            iters = sp.value_load(blki[0:1, 2 * NB:2 * NB + 1], min_val=1, max_val=(MAXB - 1) // 2)
            with sp.Fori(0, iters) as m:
                for u, s in ((0, 2 * m + 1), (1, 2 * m + 2)):
                    row = rows_of(s + 1)
                    sp.wait_ge(mxT_ps, s)
                    sp.wait_ge(meta_done, s)
                    sp.dma_start(xblk[:, u, :], xg[bass.ds(row, 128), :]).then_inc(xblk_ld[u], 16)
            sp.wait_ge(last_y_added, 16)
            sp.dma_start(out, acc[0:N, :]).then_inc(out_stored, 16)
            sp.wait_ge(out_stored, 16)

        @block.gpsimd
        def _(pool):
            steps = [0]

            def link(ins):
                steps[0] += 1
                ins.then_inc(link_pool, 1)
                pool.wait_ge(link_pool, steps[0])

            nc.gpsimd.memset(powm[:, :], -0.5).then_inc(consts_set, 1)
            nc.gpsimd.memset(zero16, 0.0).then_inc(consts_set, 1)
            nc.gpsimd.memset(dbd, 0.0).then_inc(consts_set, 1)
            nc.gpsimd.memset(warm[:, 0:1], 0.0).then_inc(consts_set, 1)
            pool.wait_ge(consts_set, 4)
            pool.wait_ge(var1, 1)
            nc.gpsimd.tensor_tensor(rstd[:, 0:NT], v_eps[:, 0:NT], powm[:, 0:NT], ALU.pow).then_inc(rstd1, 1)
            pool.wait_ge(ld_gnn, 48)
            nc.gpsimd.tensor_scalar(bqk[:, 0:2], bqk[:, 0:2], -1.0 / 8.0, 0.0, ALU.mult, ALU.add).then_inc(bq_scaled, 1)
            pool.wait_ge(wmean_done, 1)
            link(nc.gpsimd.tensor_scalar(wmean[:, :], wmean[:, :], 1.0 / C, 0.0, ALU.mult, ALU.add))
            wk3 = wkv.rearrange("p k (h c) -> p (k h) c", c=C)
            nc.gpsimd.tensor_tensor(wk3, wk3, wmean[:, :].unsqueeze(2).to_broadcast([128, 32, C]),
                                    ALU.subtract).then_inc(wkv_centred, 1)
            for i in range(NT):
                pool.wait_ge(vs_copied, i + 1)
                nc.gpsimd.tensor_tensor(VS[:, i, :], VS[:, i, :], bvs, ALU.add).then_inc(vs_done, 1)
            pool.wait_ge(ld_rows, 32)
            pool.wait_ge(ld_x, 16)
            link(nc.gpsimd.tensor_tensor(beta, beta, bout, ALU.add))
            for i in range(NT):
                nc.gpsimd.tensor_tensor(x1[:, i, :], X[:, i, :], beta, ALU.add).then_inc(xb_done, 1)

            def mask(i):
                pool.wait_ge(cnt_done, 2 * i + 2)
                nc.gpsimd.tensor_scalar(edge_mask[:, i, :], cnt[:, i, :], 0.0, BIG, ALU.is_equal,
                                        ALU.mult).then_inc(mask_done, 1)

            for i in range(NT - 1):
                mask(i)
            pool.wait_ge(sq_done, NT)
            link(nc.gpsimd.tensor_scalar(ss[:, :, :], ss[:, :, :], 1.0 / C, EPS, ALU.mult, ALU.add))
            link(nc.gpsimd.tensor_tensor(ssp[:, :, :], ss[:, :, 0:8], ss[:, :, 8:16], ALU.mult))
            link(nc.gpsimd.tensor_tensor(rkv[:, :, :].rearrange("p i h -> p (i h)"),
                                         ssp[:, :, :].rearrange("p i h -> p (i h)"), powm[:, 0:40], ALU.pow))
            for i in range(NT):
                kk = kvc[0:TP, i, 0:512].rearrange("p (h c) -> p h c", c=C)
                nc.gpsimd.tensor_tensor(kk, kk, rkv[:, i, :].unsqueeze(2).to_broadcast([TP, MH, C]),
                                        ALU.mult).then_inc(kv_normed, 1)
            mask(NT - 1)
            both = [t[:, :].rearrange("p (k i) -> p k i", k=2) for t in (rstd, v_eps, powm[:, 0:2 * NT])]
            for g, (a, b) in enumerate(PARTS):
                pool.wait_ge(varg, g + 1)
                nc.gpsimd.tensor_tensor(rstd[:, a:b], v_eps[:, a:b], powm[:, a:b], ALU.pow).then_inc(rstdg, 1)
                pool.wait_ge(var2, g + 1)
                r, v, m = (t[:, :, a:b] for t in both)
                nc.gpsimd.tensor_tensor(r, v, m, ALU.pow).then_inc(r2, 1)

            def scatter(i):
                pool.wait_ge(slot_done, i + 1)
                pool.wait_ge(weights_done, i + 1)
                pool.wait_ge(xg_emptied, 16)
                for k in range(2):
                    nc.gpsimd.indirect_dma_start(
                        xg, bass.IndirectOffsetOnAxis(rti[:, 40 + 2 * i + k:41 + 2 * i + k], 0),
                        rowbuf[:, i % 2, k, :], None).then_inc(scattered[i % 2], 16)

            for i in range(NT):
                pool.wait_ge(ms3, i + 1)
                nc.gpsimd.tensor_tensor(rstd[:, i:i + 1], v_eps[:, i:i + 1], powm[:, i:i + 1], ALU.pow).then_inc(r3, 1)
                if i:
                    scatter(i - 1)
                if i < NT - 1:
                    nc.gpsimd.tensor_tensor(x1[:, i, :], x1[:, i, :], xn[:, i, :], ALU.add).then_inc(res_done, 1)
            scatter(NT - 1)
            nc.gpsimd.tensor_tensor(x1[:, NT - 1, :], x1[:, NT - 1, :], xn[:, NT - 1, :], ALU.add).then_inc(res_done, 1)
            pool.wait_ge(blk_done, 1)
            iters = pool.value_load(blki[0:1, 2 * NB:2 * NB + 1], min_val=1, max_val=(MAXB - 1) // 2)

            pool.wait_ge(acc_stored, 16 * NT)
            pool.wait_ge(acc_emptied, 16)

            def add_rows(u):
                pool.sem_inc(y_seen, 1)
                return nc.gpsimd.indirect_dma_start(
                    acc, bass.IndirectOffsetOnAxis(slot_id[:, u:u + 1], 0), yb[:, u, :], None,
                    compute_op=ALU.add)

            with pool.Fori(0, iters) as m:
                for u, s in ((0, 2 * m), (1, 2 * m + 1)):
                    pool.wait_ge(y_copied, s + 2)
                    add_rows(u).then_inc(y_added, 16)
                    pool.wait_ge(y_added, 16 * s + 16)
                    pool.sem_inc(y_free, 1)
            pool.wait_ge(y_copied, 2 * iters + 2)
            add_rows(0).then_inc(last_y_added, 16)

        @block.scalar
        def _(act):
            for i in range(NT):
                act.wait_ge(xnT_ps, i + 1)
                nc.scalar.copy(xnT[:, :, i * TP:(i + 1) * TP],
                               ps[:, i % 2, 0:256].rearrange("p (k n) -> p k n", k=KC)[:, :, 0:TP]).then_inc(xnT_done, 1)
            act.wait_ge(bq_scaled, 1)
            for j in range(8):
                m, (a, b) = j // 2, HALVES[j % 2]
                act.wait_ge(qk_ps, j + 1)
                nc.scalar.activation(gqkT[:, m, a:b], ps[:, 2 + j % 4, 0:b - a], ACT.Identity,
                                     bias=bqk[:, m:m + 1], scale=-0.125 if m < 2 else 1.0).then_inc(qk_done, 1)

            def cnt_copy(b):
                act.wait_ge(cnt_ps, b + 1)
                if b == 0:
                    act.wait_ge(range_done, 1)
                nc.scalar.copy(cnt[:, b, 0:512], ps[0:TP, 0, :]).then_inc(cnt_done, 1)
                nc.scalar.copy(cnt[:, b, 512:N], ps[0:TP, 1, 0:N - 512]).then_inc(cnt_done, 1)

            def kv_copy(i):
                kv = flat(4 - 2 * (i % 2))[0:TP, :]
                act.wait_ge(kv_ps, i + 1)
                nc.scalar.copy(kvc[0:TP, i, :], kv).then_inc(kv_copied, 1)
                act.wait_ge(kv_copied, i + 1)
                for g in range(2 * MH):
                    ins = nc.scalar.activation(kv[:, C * g:C * (g + 1)], kv[:, C * g:C * (g + 1)], ACT.Square,
                                               accum_out=ss[:, i, g:g + 1])
                ins.then_inc(sq_done, 1)

            def vs_copy(i):
                act.wait_ge(vs_ps, i + 1)
                nc.scalar.copy(VS[:, i, :], ps[0:TP, 6 + i % 2, :]).then_inc(vs_copied, 1)

            def head_sums():
                act.wait_ge(ld_mix, 48)
                wk3 = wkv.rearrange("p k (h c) -> p (k h) c", c=C)
                for g in range(KC * 2 * MH):
                    ins = nc.scalar.activation(wk3[:, g, :], wk3[:, g, :], ACT.Copy, accum_out=wmean[:, g:g + 1])
                ins.then_inc(wmean_done, 1)

            for b in range(NT):
                for i in range(*VS_TILES[b]):
                    vs_copy(i)
                if b == 0:
                    head_sums()
                for i in range(*KV_TILES[b]):
                    kv_copy(i)
                cnt_copy(b)

            def gnn_AT(n):
                act.wait_ge(AT_ps, n + 1)
                if n >= 2:
                    act.wait_ge(AV_done, n - 1)
                nc.scalar.copy(AT[:, n % 2, :, :],
                               flat(4)[0:TP, 0:640].rearrange("p (j n) -> p j n", j=NT)[:, :, 0:TP]).then_inc(AT_done, 1)

            def gelu(a, b):
                act.wait_ge(agg_done, b)
                nc.scalar.activation(VS[:, a:b, D:512], VS[:, a:b, D:512], ACT.Gelu).then_inc(gelu_done, 1)

            for n in range(20):
                act.wait_ge(S_used, n + 1)
                nc.scalar.activation(E[:, n % 3, :], E[:, n % 3, :], ACT.Exp,
                                     bias=mn[:, n:n + 1], scale=-1.0).then_inc(exp_done, 1)
                if n >= 2:
                    gnn_AT(n - 2)
                if n in (4, 5):
                    act.wait_ge(M1_ps, n - 3)
                    nc.scalar.copy(M1[:, 2 * (n - 4):2 * (n - 3), :],
                                   ps[:, 7, :].rearrange("p (e n) -> p e n", e=2)).then_inc(M1_done, 1)
                if n == 7:
                    act.wait_ge(M2_ps, 1)
                    nc.scalar.copy(M2.rearrange("p k n -> p (k n)"), ps[:, 7, :]).then_inc(M2_done, 1)
                if n == 15:
                    gelu(*PARTS[0])
            gnn_AT(18)
            gnn_AT(19)
            gelu(*PARTS[1])
            act.wait_ge(ld_ffn, 64)
            def hT_rows(i):
                act.wait_ge(hT_ps, i + 1)
                for k in range(KC):
                    ins = nc.scalar.activation(xnT[:, k, i * TP:(i + 1) * TP],
                                               ps[:, i % 2, 128 * k:128 * k + TP], ACT.Copy, scale=ln1c[:, k:k + 1])
                ins.then_inc(hT_done, 1)

            def qkT_copy(i):
                act.wait_ge(qkT_ps, i + 1)
                t = ps[:, 4 + i % 2, 0:384].rearrange("p (m n) -> p m n", m=3)[:, :, 0:TP]
                nc.scalar.mul(QKT[:, 0:2, i * TP:(i + 1) * TP], t[:, 0:2, :], 0.125)
                nc.scalar.copy(QKT[:, 2, i * TP:(i + 1) * TP], t[:, 2, :]).then_inc(qkT_done, 1)

            for i in range(*PARTS[0]):
                hT_rows(i)
            act.wait_ge(consts_set, 4)
            nc.scalar.activation(warm[:, 1:2], warm[:, 0:1], ACT.Exp)
            for i in range(NT):
                act.wait_ge(qkv_used, i + 1)
                nc.scalar.copy(Vc[:, i, :], ps[0:TP, QKV_BANK[i], 384:512]).then_inc(vc_done, 1)
                if i == 0:
                    for j in range(*PARTS[1]):
                        hT_rows(j)
                else:
                    qkT_copy(i - 1)
            qkT_copy(NT - 1)

            def ffn_ET(n):
                i = n // 4
                act.wait_ge(ET_ps, n + 1)
                if n >= 2:
                    act.wait_ge(AV2_done, n - 1)
                nc.scalar.copy(AT[:, n % 2, 0:i + 1, :],
                               flat(4)[0:TP, 0:640].rearrange("p (j n) -> p j n", j=NT)[:, 0:i + 1, 0:TP]).then_inc(ET_done, 1)

            def ffn_yT(i):
                act.wait_ge(yT_ps, i + 1)
                nc.scalar.copy(yT[:, i % 2, :, :],
                               ps[:, 7, 0:256].rearrange("p (k n) -> p k n", k=KC)[:, :, 0:TP]).then_inc(yT_done, 1)

            def flatT_copy(i):
                act.wait_ge(flatT_ps, i + 1)
                nc.scalar.copy(xnT[:, :, i * TP:(i + 1) * TP],
                               ps[:, FT_BANK[i], 0:256].rearrange("p (k n) -> p k n", k=KC)[:, :, 0:TP]).then_inc(flatT_done, 1)

            def router_exp(i):
                act.wait_ge(rmax_done, i + 1)
                nc.scalar.activation(R(i, 16, 8), R(i, 8, 8), ACT.Exp, bias=R(i, 52, 1),
                                     accum_out=R(i, 53, 1)).then_inc(rexp_done, 1)

            for n in range(20):
                i = n // 4
                act.wait_ge(max2_done, n + 1)
                if n >= 3:
                    act.wait_ge(ET_ps, n - 2)
                w = TP * (i + 1)
                nc.scalar.activation(E[:, n % 3, 0:w], flat(2 * (n % 2))[0:TP, 0:w], ACT.Exp,
                                     bias=mn2[:, n:n + 1], scale=1.0,
                                     accum_out=den2[:, n:n + 1]).then_inc(exp2_done, 1)
                if n >= 2:
                    ffn_ET(n - 2)
                if n % 4 == 3 and n >= 7:
                    ffn_yT(i - 1)
                if n % 4 == 2 and n >= 10:
                    flatT_copy(i - 2)
                if n % 4 == 0 and n >= 12:
                    router_exp(i - 3)
            ffn_ET(18)
            ffn_ET(19)
            ffn_yT(4)
            router_exp(2)
            flatT_copy(3)
            router_exp(3)
            flatT_copy(4)
            router_exp(4)
            nc.scalar.activation(warm[:, 2:3], warm[:, 0:1], ACT.Silu)

            def xT_copy(s, u):
                act.wait_ge(mxT_ps, s + 1)
                nc.scalar.copy(xTb[:, u, :, :], ps[:, 7, 0:256].rearrange("p (k n) -> p k n", k=KC)).then_inc(mxT_done, 1)

            def silu(s, j):
                act.wait_ge(ab_ps, 2 * s + j + 1)
                if not isinstance(s, int):
                    act.wait_ge(g_done, 2 * s + j - 1)
                nc.scalar.activation(sl[:, j, :], ps[:, 2 * j, 0:HH], ACT.Silu).then_inc(silu_done, 1)

            def hT_copy(s, j):
                act.wait_ge(gT_ps, 2 * s + j + 1)
                nc.scalar.copy(hTb[:, j, :, :], ps[:, 4 + j, 0:384].rearrange("p (k n) -> p k n", k=HC)).then_inc(gT_copied, 1)

            act.wait_ge(blk_done, 1)
            iters = act.value_load(blki[0:1, 2 * NB:2 * NB + 1], min_val=1, max_val=(MAXB - 1) // 2)
            xT_copy(0, 0)
            silu(0, 0)
            xT_copy(1, 1)
            silu(0, 1)
            with act.Fori(0, iters) as m:
                for u, s in ((1, 2 * m + 1), (0, 2 * m + 2)):
                    silu(s, 0)
                    xT_copy(s + 1, 1 - u)
                    hT_copy(s - 1, 0)
                    hT_copy(s - 1, 1)
                    silu(s, 1)
            for j in range(2):
                hT_copy(2 * iters, j)

        @block.tensor
        def _(pe):
            def two_transposes(bank, rows, src_parts=TP):
                for k in range(KC):
                    ins = nc.tensor.transpose(ps[:, bank, 128 * k:128 * k + src_parts],
                                              rows[:, 128 * k:128 * (k + 1)], ident[0:src_parts, 0:src_parts])
                return ins

            def stay_awake(times, bank):
                for _ in range(times):
                    nc.tensor.matmul(ps[:, bank, :], zero16[:, 0:128], zero16, start=True, stop=True)

            pe.wait_ge(consts_set, 4)
            pe.wait_ge(ld_ident, 16)
            pe.wait_ge(gmm_done, 1)
            for k in range(2):
                ins = nc.tensor.matmul(ps[0:1, 7, NG * k:NG * (k + 1)], gmm[:, k:k + 1], ident[0:NG, 0:NG],
                                       start=True, stop=True)
            ins.then_inc(gmm_ps, 1)
            for i in range(NT):
                pe.wait_ge(xn_done, i + 1)
                if i >= 2:
                    pe.wait_ge(xnT_done, i - 1)
                two_transposes(i % 2, xn[:, i, :]).then_inc(xnT_ps, 1)
            pe.wait_ge(ld_gnn, 48)
            pe.wait_ge(xnT_done, NT)
            for j in range(8):
                m, (a, b) = j // 2, HALVES[j % 2]
                if j >= 4:
                    pe.wait_ge(qk_done, j - 3)
                for k in range(KC):
                    ins = nc.tensor.matmul(ps[:, 2 + j % 4, 0:b - a], wgnn[:, k, 128 * m:128 * (m + 1)],
                                           xnT[:, k, a:b], start=(k == 0), stop=(k == KC - 1))
                ins.then_inc(qk_ps, 1)
            seq = pe.alloc_register("pe_groups")
            slot = pe.alloc_register("pe_slot")
            pe.reg_mov(seq, 0)
            pe.reg_mov(slot, 0)
            big, small = ps[:, 0, :], ps[:, 1, 0:N - 512]

            def zeros(start):
                nc.tensor.matmul(big, zero16[:, 0:128], zero16, start=start, stop=not start)
                return nc.tensor.matmul(small, zero16[:, 0:128], zero16[:, 0:N - 512], start=start, stop=not start)

            def count(b):
                first = pe.value_load(rangei[0:1, 0, b:b + 1], min_val=0, max_val=NG - 1)
                last = pe.value_load(rangei[0:1, 1, b:b + 1], min_val=1, max_val=NG)
                if b:
                    pe.wait_ge(cnt_done, 2 * b)
                zeros(True)
                with pe.Fori(first, last):
                    done = pe.snap(seq, min_val=0, max_val=NT * NG)
                    r = ring[:, bass.ds(pe.snap(slot, min_val=0, max_val=SLOTS - 1), 1), :, :].rearrange("p a k n -> p (a k) n")
                    pe.wait_ge(oh_built, done + 1)
                    for k in range(EG):
                        nc.tensor.matmul(big, r[:, k, 640:768], r[:, k, 0:512], start=False, stop=False)
                        ins = nc.tensor.matmul(small, r[:, k, 640:768], r[:, k, 512:N], start=False, stop=False)
                    ins.then_inc(oh_used, 1)
                    pe.reg_add(seq, seq, 1)
                    pe.reg_add(slot, slot, 1)
                    pe.reg_mod(slot, slot, SLOTS)
                zeros(False).then_inc(cnt_ps, 1)

            def mix_kv(i):
                if i >= 2:
                    pe.wait_ge(sq_done, i - 1)
                for j in range(2):
                    for k in range(KC):
                        ins = nc.tensor.matmul(ps[0:TP, 4 - 2 * (i % 2) + j, :], xnT[:, k, i * TP:(i + 1) * TP],
                                               wkv[:, k, 512 * j:512 * (j + 1)], start=(k == 0), stop=(k == KC - 1))
                ins.then_inc(kv_ps, 1)

            def vs_rows(i):
                if i >= 2:
                    pe.wait_ge(vs_copied, i - 1)
                for k in range(KC):
                    ins = nc.tensor.matmul(ps[0:TP, 6 + i % 2, :], xnT[:, k, i * TP:(i + 1) * TP],
                                           wgnn[:, k, 512:1024], start=(k == 0), stop=(k == KC - 1))
                ins.then_inc(vs_ps, 1)

            pe.wait_ge(range_done, 1)
            pe.wait_ge(consts_set, 4)
            def gnn_S(n):
                i, h = n // 4, n % 4
                r = 64 * (h % 2)
                for a, b in ((0, 512), (512, N)):
                    ins = nc.tensor.matmul(flat(2 - 2 * (n % 2))[0:TP, a:b], gqkT[r:r + 64, h // 2, i * TP:(i + 1) * TP],
                                           gqkT[r:r + 64, 2 + h // 2, a:b], start=True, stop=True)
                ins.then_inc(S_ps, 1)

            for b in range(NT):
                for i in range(*VS_TILES[b]):
                    vs_rows(i)
                for i in range(*KV_TILES[b]):
                    if i == 0:
                        pe.wait_ge(wkv_centred, 1)
                        pe.wait_ge(qk_done, 8)
                    mix_kv(i)
                if b == NT - 1:
                    pe.wait_ge(sq_done, NT - 1)
                    gnn_S(0)
                count(b)
            pe.wait_ge(ld_mix, 48)
            pe.wait_ge(cnt_done, 2 * NT)
            pe.wait_ge(sq_done, NT)
            pe.wait_ge(vs_done, NT)

            def mix_dots():
                pe.wait_ge(kv_normed, NT)
                for p in range(4):
                    for i in range(NT):
                        ins = nc.tensor.matmul(ps[:, 7, 128 * p:128 * (p + 1)],
                                               kvc[0:TP, i, 512 + 128 * p:512 + 128 * (p + 1)],
                                               kvc[0:TP, i, 128 * p:128 * (p + 1)], start=(i == 0), stop=(i == NT - 1))
                ins.then_inc(dots_ps, 1)

            def mix_M1(half):
                if half:
                    pe.wait_ge(M1_done, 1)
                else:
                    pe.wait_ge(dbd_done, 1)
                for p in (2 * half, 2 * half + 1):
                    ins = nc.tensor.matmul(ps[:, 7, 256 * (p % 2):256 * (p % 2) + 256], dbd[:, p, :],
                                           wmo[:, p, :], start=True, stop=True)
                ins.then_inc(M1_ps, 1)

            def mix_M2():
                pe.wait_ge(M1_done, 2)
                for m in range(KC):
                    for p in range(4):
                        ins = nc.tensor.matmul(ps[:, 7, 256 * m:256 * (m + 1)], wmq[:, p, 128 * m:128 * (m + 1)],
                                               M1[:, p, :], start=(p == 0), stop=(p == 3))
                ins.then_inc(M2_ps, 1)

            def mix_out(i):
                if i:
                    pe.wait_ge(mix_used, i)
                else:
                    pe.wait_ge(M2_done, 1)
                for k in range(KC):
                    ins = nc.tensor.matmul(ps[0:TP, 7, 0:256], xnT[:, k, i * TP:(i + 1) * TP], M2[:, k, :],
                                           start=(k == 0), stop=(k == KC - 1))
                ins.then_inc(mix_ps, 1)

            def gnn_AV(n):
                i, h = n // 4, n % 4
                pe.wait_ge(AT_done, n + 1)
                if h == 0 and i:
                    pe.wait_ge(O_used, i)
                for j in range(NT):
                    ins = nc.tensor.matmul(ps[0:TP, 6, C * h:C * (h + 1)], AT[:, n % 2, j, :],
                                           VS[:, j, C * h:C * (h + 1)], start=(j == 0), stop=(j == NT - 1))
                ins.then_inc(AV_done, 1)

            def gnn_T(n):
                pe.wait_ge(A_done, n + 1)
                if n >= 1:
                    pe.wait_ge(AT_done, n)
                for j in range(NT):
                    ins = nc.tensor.transpose(flat(4)[0:TP, 128 * j:128 * j + TP], E[:, n % 3, TP * j:TP * (j + 1)],
                                              ident[0:TP, 0:TP])
                ins.then_inc(AT_ps, 1)

            for n in range(20):
                i, h = n // 4, n % 4
                if n >= 2:
                    pe.wait_ge(S_used, n - 1)
                if n >= 1:
                    gnn_S(n)
                if n >= 2:
                    gnn_T(n - 2)
                if n == 2:
                    mix_dots()
                if n in (4, 5):
                    mix_M1(n - 4)
                if n == 7:
                    mix_M2()
                if n in MIX_OUT:
                    mix_out(MIX_OUT.index(n))
                if n >= 3:
                    gnn_AV(n - 3)
            gnn_T(18)
            gnn_AV(17)
            gnn_T(19)
            gnn_AV(18)
            gnn_AV(19)
            pe.wait_ge(ld_ffn, 64)
            pe.wait_ge(ld_const, 32)
            pe.wait_ge(S_used, 20)
            pe.wait_ge(mix_used, NT)
            def hT(i):
                pe.wait_ge(h_done, i + 1)
                if i >= 2:
                    pe.wait_ge(hT_done, i - 1)
                two_transposes(i % 2, hrow[:, i, :]).then_inc(hT_ps, 1)

            def qkv(i):
                pe.wait_ge(hT_done, i + 1)
                if i == 2:
                    pe.wait_ge(O_used, NT)
                if i >= 3:
                    pe.wait_ge(qkv_used, i - 2)
                    pe.wait_ge(vc_done, i - 2)
                for k in range(KC):
                    ins = nc.tensor.matmul(ps[0:TP, QKV_BANK[i], :], xnT[:, k, i * TP:(i + 1) * TP], wqkv[:, k, :],
                                           start=(k == 0), stop=(k == KC - 1))
                ins.then_inc(qkv_ps, 1)

            def qkT(i):
                pe.wait_ge(qkr_done, i + 1)
                if i >= 2:
                    pe.wait_ge(qkT_done, i - 1)
                for m in range(3):
                    ins = nc.tensor.transpose(ps[:, 4 + i % 2, 128 * m:128 * m + TP], qkr[:, 128 * m:128 * (m + 1)],
                                              ident[0:TP, 0:TP])
                ins.then_inc(qkT_ps, 1)

            stay_awake(8, 7)
            for i in range(*PARTS[0]):
                hT(i)
            for i in range(3):
                qkv(i)
            for i in range(*PARTS[1]):
                hT(i)
            for i in range(3, NT):
                qkT(i - 3)
                qkv(i)
            for i in range(NT - 3, NT):
                qkT(i)
            pe.wait_ge(qkT_done, NT)
            pe.wait_ge(vc_done, NT)
            pe.wait_ge(qkv_used, NT)

            def ffn_T(n):
                pe.wait_ge(exp2_done, n + 1)
                if n >= 1:
                    pe.wait_ge(ET_done, n)
                if n == 16:
                    pe.wait_ge(rank_used, 2)
                for j in range(n // 4 + 1):
                    ins = nc.tensor.transpose(flat(4)[0:TP, 128 * j:128 * j + TP], E[:, n % 3, TP * j:TP * (j + 1)],
                                              ident[0:TP, 0:TP])
                ins.then_inc(ET_ps, 1)

            def ffn_AV(n):
                i, h = n // 4, n % 4
                pe.wait_ge(ET_done, n + 1)
                if h == 0 and i:
                    pe.wait_ge(O2_used, i)
                for j in range(i + 1):
                    ins = nc.tensor.matmul(ps[0:TP, 6, C * h:C * (h + 1)], AT[:, n % 2, j, :],
                                           Vc[:, j, C * (h // 2):C * (h // 2) + C], start=(j == 0), stop=(j == i))
                ins.then_inc(AV2_done, 1)

            def ffn_yT(i):
                pe.wait_ge(y_done, i + 1)
                if i:
                    pe.wait_ge(x2_done, i)
                if i == 3:
                    pe.wait_ge(flatT_done, 3)
                two_transposes(7, yat[:, i % 2, :]).then_inc(yT_ps, 1)

            def ffn_wo(i):
                pe.wait_ge(yT_done, i + 1)
                if i:
                    pe.wait_ge(x2_done, i)
                for k in range(KC):
                    ins = nc.tensor.matmul(ps[0:TP, 7, 256:512], yT[:, i % 2, k, :], wo[:, k, :],
                                           start=(k == 0), stop=(k == KC - 1))
                ins.then_inc(wo_ps, 1)

            def flatT(i):
                pe.wait_ge(flat_done, i + 1)
                if i and FT_BANK[i] == LG_BANK[i - 1]:
                    pe.wait_ge(rank_used, i)
                two_transposes(FT_BANK[i], rowbuf[:, i % 2, 0, :]).then_inc(flatT_ps, 1)

            def logits(i):
                pe.wait_ge(flatT_done, i + 1)
                if i and LG_BANK[i] == LG_BANK[i - 1]:
                    pe.wait_ge(rank_used, i)
                for k in range(KC):
                    ins = nc.tensor.matmul(ps[0:TP, LG_BANK[i], 256:256 + NE], xnT[:, k, i * TP:(i + 1) * TP],
                                           wr[:, k, :], start=(k == 0), stop=(k == KC - 1))
                ins.then_inc(logit_ps, 1)

            def rank(i):
                pe.wait_ge(logits_read, i + 1)
                for j in range(i + 1):
                    pe.wait_ge(sel_done, j + 1)
                    ins = nc.tensor.matmul(ps[0:TP, LG_BANK[i], 272:272 + NE], tri if j == i else ones, sel_of(j),
                                           start=(j == 0), stop=(j == i))
                ins.then_inc(rank_ps, 1)

            def totals():
                pe.wait_ge(rank_used, NT - 1)
                for j in range(NT):
                    ins = nc.tensor.matmul(ps[0:TP, LG_BANK[NT - 2], 288:288 + NE], ones, sel_of(j), start=(j == 0),
                                           stop=(j == NT - 1))
                ins.then_inc(total_ps, 1)

            for n in range(20):
                i, h = n // 4, n % 4
                if n >= 2:
                    pe.wait_ge(exp2_done, n - 1)
                w = TP * (i + 1)
                r = 64 * (h // 2)
                S = flat(2 * (n % 2))[0:TP, :]
                q = QKT[r:r + 64, h % 2, i * TP:(i + 1) * TP]
                edges = [0, w - TP, w] if w > 512 else [0, w]
                for a, b in zip(edges, edges[1:]):
                    b1 = min(b, 512)
                    last = b == w
                    if a < b1:
                        nc.tensor.matmul(S[:, a:b1], q, QKT[r:r + 64, 2, a:b1], start=True,
                                         stop=not (last and b1 <= 512), skip_group_check=True)
                    if b > 512:
                        nc.tensor.matmul(S[:, 512:b], q, QKT[r:r + 64, 2, 512:b], start=True, stop=False,
                                         skip_group_check=True)
                for a, b in ((w - TP, min(w, 512)), (512, w)):
                    if a < b:
                        ins = nc.tensor.matmul(S[:, a:b], identb, causal[:, a - (w - TP):b - (w - TP)], start=False,
                                               stop=True, skip_group_check=True)
                ins.then_inc(S2_ps, 1)
                if n < 7:
                    stay_awake(2, 7)
                if n >= 2:
                    ffn_T(n - 2)
                if n >= 3:
                    ffn_AV(n - 3)
                if n >= 12 and h == 0:
                    rank(i - 3)
                if h == 3 and 11 <= n < 19:
                    logits(i - 2)
                if n >= 10 and h == 2:
                    flatT(i - 2)
                if n >= 7 and h == 3:
                    ffn_yT(i - 1)
                if n >= 8 and h == 0:
                    ffn_wo(i - 2)
            ffn_T(18)
            ffn_AV(17)
            logits(2)
            ffn_wo(3)
            ffn_T(19)
            ffn_AV(18)
            rank(2)
            ffn_AV(19)
            ffn_yT(4)
            flatT(3)
            ffn_wo(4)
            logits(3)
            rank(3)
            flatT(4)
            logits(4)
            rank(4)
            totals()
            stay_awake(20, 6)

            def up_gate(s, u, j, e):
                if not isinstance(s, int):
                    pe.wait_ge(g_done, 2 * s + j - 1)
                for g in range(2):
                    for k in range(KC):
                        w = W13[:, bass.ds(e, 1), k, HID * g + HH * j:HID * g + HH * (j + 1)].rearrange("p a n -> p (a n)")
                        ins = nc.tensor.matmul(ps[:, 2 * j + g, 0:HH], xTb[:, u, k, :], w,
                                               start=(k == 0), stop=(k == KC - 1))
                ins.then_inc(ab_ps, 1)

            def gT(s, u):
                for j in range(2):
                    pe.wait_ge(g_done, 2 * s + j + 1)
                    for c in range(HC):
                        ins = nc.tensor.transpose(ps[0:HCW[c], 4 + j, 128 * c:128 * (c + 1)],
                                                  gb[:, u, j, 128 * c:128 * c + HCW[c]], ident)
                    ins.then_inc(gT_ps, 1)

            def down(s, e):
                pe.wait_ge(y_copied, s + 1)
                for j in range(2):
                    pe.wait_ge(gT_copied, 2 * s + j + 1)
                    for c in range(HC):
                        w = W2[0:HCW[c], bass.ds(e, 1), HC * j + c, :].rearrange("p a n -> p (a n)")
                        ins = nc.tensor.matmul(ps[:, 6, 0:D], hTb[0:HCW[c], j, c, :], w,
                                               start=(j == 0 and c == 0), stop=(j == 1 and c == HC - 1))
                ins.then_inc(y_ps, 1)

            def expert(s):
                return pe.value_load(blki[0:1, bass.ds(s, 1)], min_val=0, max_val=NE - 1)

            pe.wait_ge(blk_done, 1)
            pe.wait_ge(y_done, NT)
            pe.wait_ge(ET_done, 20)
            pe.wait_ge(x2_done, NT)
            pe.wait_ge(ld_w, 16 * (NE - NLATE))
            pe.wait_ge(ld_late, 16 * (4 * NE + NLATE))
            nc.tensor.matmul(ps[:, 4, :], zero16[:, 0:128], zero16, start=True, stop=True)
            nc.tensor.matmul(ps[:, 5, :], zero16[:, 0:128], zero16, start=True, stop=True)
            iters = pe.value_load(blki[0:1, 2 * NB:2 * NB + 1], min_val=1, max_val=(MAXB - 1) // 2)
            e0 = expert(0)
            pe.wait_ge(xblk_ld[0], 16)
            two_transposes(7, xblk[:, 0, 0:D], 128).then_inc(mxT_ps, 1)
            pe.wait_ge(mxT_done, 1)
            up_gate(0, 0, 0, e0)
            pe.wait_ge(xblk_ld[1], 16)
            two_transposes(7, xblk[:, 1, 0:D], 128).then_inc(mxT_ps, 1)
            up_gate(0, 0, 1, e0)
            with pe.Fori(0, iters) as m:
                for u, s in ((1, 2 * m + 1), (0, 2 * m + 2)):
                    e = expert(s)
                    pe.wait_ge(mxT_done, s + 1)
                    up_gate(s, u, 0, e)
                    pe.wait_ge(xblk_ld[1 - u], 16 * m + 32)
                    two_transposes(7, xblk[:, 1 - u, 0:D], 128).then_inc(mxT_ps, 1)
                    gT(s - 1, 1 - u)
                    up_gate(s, u, 1, e)
                    e_last = expert(s - 1)
                    down(s - 1, e_last)
            gT(2 * iters, 0)
            down(2 * iters, expert(2 * iters))

        @block.vector
        def _(dve):
            steps = [0]

            def link(ins):
                steps[0] += 1
                ins.then_inc(link_dve, 1)
                dve.wait_ge(link_dve, steps[0])

            def stats(src):
                for i in range(NT):
                    ins = nc.vector.bn_stats(st[:, i, :], src[:, i, :])
                link(ins)
                for i in range(NT):
                    ins = nc.vector.bn_aggr(mv[:, i, :], st[:, i, :])
                link(ins)
                return nc.vector.tensor_scalar(v_eps[:, 0:NT], mv[:, :, 1], EPS, None, ALU.add)

            dve.wait_ge(ld_x, 16)
            stats(X).then_inc(var1, 1)
            dve.wait_ge(ld_groups, 32)
            nc.vector.tensor_reduce(gmm[:, 0:1], edgesg, AX.X, ALU.min)
            nc.vector.tensor_reduce(gmm[:, 1:2], edgesg, AX.X, ALU.max).then_inc(gmm_done, 1)
            dve.wait_ge(rstd1, 1)
            for i in range(NT):
                nc.vector.tensor_scalar(xn[:, i, :], X[:, i, :], mv[:, i, 0:1], rstd[:, i:i + 1],
                                        ALU.subtract, ALU.mult).then_inc(xn_done, 1)
            dve.wait_ge(ld_edges, 48)
            nc.vector.tensor_copy(srcf, srci)
            link(nc.vector.tensor_copy(dstf, dsti))
            for b in range(NT):
                ins = nc.vector.tensor_scalar(dstrel[:, b, :], dstf, float(TP * b), None, ALU.subtract)
            link(ins)
            dve.wait_ge(gmm_ps, 1)
            g = rr[:, 0:2 * NG].rearrange("p (k g) -> p k g", k=2)
            link(nc.vector.tensor_copy(rr[:, 0:2 * NG], ps[0:1, 7, 0:2 * NG]))
            bg = NT * NG
            r1 = rr[:, 80:80 + bg].rearrange("p (b g) -> p b g", b=NT)
            r2_ = rr[:, 280:280 + bg].rearrange("p (b g) -> p b g", b=NT)
            lo = crow[:, 0:bg].rearrange("p (b g) -> p b g", b=NT)
            hi = crow[:, 200:200 + bg].rearrange("p (b g) -> p b g", b=NT)
            up = crow[:, 400:400 + NG].unsqueeze(1).to_broadcast([1, NT, NG])
            down_ = crow[:, 440:440 + NG].unsqueeze(1).to_broadcast([1, NT, NG])
            nc.vector.tensor_tensor(r1, hi, g[:, 0:1, :].to_broadcast([1, NT, NG]), ALU.is_ge)
            link(nc.vector.tensor_tensor(r2_, lo, g[:, 1:2, :].to_broadcast([1, NT, NG]), ALU.is_le))
            link(nc.vector.tensor_tensor(r1, r1, r2_, ALU.mult))
            r3_ = rr[:, 480:480 + bg].rearrange("p (b g) -> p b g", b=NT)
            nc.vector.tensor_tensor(r2_, r1, down_, ALU.mult)
            link(nc.vector.tensor_tensor(r3_, r1, up, ALU.mult))
            nc.vector.tensor_reduce(rr[:, 700:705], r2_, AX.X, ALU.max)
            link(nc.vector.tensor_reduce(rr[:, 705:710], r3_, AX.X, ALU.max))
            link(nc.vector.tensor_scalar(rr[:, 710:715], rr[:, 700:705], -1.0, float(NG), ALU.mult, ALU.add))
            link(nc.vector.tensor_scalar(rr[:, 710:715], rr[:, 710:715], float(NG - 1), None, ALU.min))
            link(nc.vector.tensor_scalar(rr[:, 715:720], rr[:, 710:715], 1.0, None, ALU.add))
            link(nc.vector.tensor_tensor(rr[:, 715:720], rr[:, 715:720], rr[:, 705:710], ALU.max))
            nc.vector.tensor_copy(rangei[:, :, :].rearrange("p k b -> p (k b)"), rr[:, 710:720]).then_inc(range_done, 1)
            dve.wait_ge(range_done, 1)
            seq = dve.alloc_register("dve_groups")
            slot = dve.alloc_register("dve_slot")
            dve.reg_mov(seq, 0)
            dve.reg_mov(slot, 0)
            dve.sem_inc(oh_used, SLOTS)
            for b in range(NT):
                first = dve.value_load(rangei[0:1, 0, b:b + 1], min_val=0, max_val=NG - 1)
                last = dve.value_load(rangei[0:1, 1, b:b + 1], min_val=1, max_val=NG)
                with dve.Fori(first, last) as gi:
                    done = dve.snap(seq, min_val=0, max_val=NT * NG)
                    r = ring[:, bass.ds(dve.snap(slot, min_val=0, max_val=SLOTS - 1), 1), :, :].rearrange("p a k n -> p (a k) n")
                    dve.wait_ge(oh_used, done + 1)
                    nc.vector.tensor_tensor(r[:, :, 640:768], iota16[:, 0:128].unsqueeze(1).to_broadcast([TP, EG, 128]),
                                            dstrel[:, b, bass.ds(EG * gi, EG)].unsqueeze(2).to_broadcast([TP, EG, 128]),
                                            ALU.is_equal)
                    for k in range(EG):
                        ins = nc.vector.tensor_scalar(r[:, k, 0:N], iota16, srcf[:, bass.ds(EG * gi + k, 1)], None,
                                                      ALU.is_equal)
                    ins.then_inc(oh_built, 1)
                    dve.reg_add(seq, seq, 1)
                    dve.reg_add(slot, slot, 1)
                    dve.reg_mod(slot, slot, SLOTS)
            link(nc.vector.tensor_copy(rr[:, 0:1], rr[:, 1:2]))

            def mix_dbd():
                dve.wait_ge(dots_ps, 1)
                dve.wait_ge(consts_set, 4)
                for r in (0, 64):
                    ins = nc.vector.tensor_scalar(dbd[r:r + 64, :, r:r + 64],
                                                  ps[r:r + 64, 7, :].rearrange("p (e n) -> p e n", e=4)[:, :, r:r + 64],
                                                  1.0 / N, None, ALU.mult)
                ins.then_inc(dbd_done, 1)

            def mix_add(i):
                dve.wait_ge(mix_ps, i + 1)
                dve.wait_ge(xb_done, i + 1)
                nc.vector.tensor_tensor(x1[:, i, :], ps[0:TP, 7, 0:256], x1[:, i, :], ALU.add).then_inc(mix_used, 1)

            def gnn_weigh(n):
                dve.wait_ge(exp_done, n + 1)
                dve.wait_ge(cnt_done, 2 * (n // 4) + 2)
                nc.vector.tensor_tensor_reduce(out=E[:, n % 3, :], in0=E[:, n % 3, :], in1=cnt[:, n // 4, :], scale=1.0,
                                               scalar=0.0, op0=ALU.mult, op1=ALU.add,
                                               accum_out=den[:, n:n + 1]).then_inc(A_done, 1)

            def gnn_out(i):
                dve.wait_ge(A_done, 4 * i + 4)
                link(nc.vector.tensor_scalar(rd[:, :], den[:, 4 * i:4 * i + 4], 1e-16, None, ALU.add))
                link(nc.vector.reciprocal(rd[:, :], rd[:, :]))
                dve.wait_ge(AV_done, 4 * i + 4)
                nc.vector.tensor_tensor(hrow[:, i, :].rearrange("p (h c) -> p h c", c=C),
                                        ps[0:TP, 6, 0:256].rearrange("p (h c) -> p h c", c=C),
                                        rd[:, :].unsqueeze(2).to_broadcast([TP, H, C]), ALU.mult).then_inc(O_used, 1)
                dve.wait_ge(O_used, i + 1)
                nc.vector.tensor_tensor(VS[:, i, D:512], VS[:, i, D:512], hrow[:, i, :], ALU.add).then_inc(agg_done, 1)

            def row_stats(a, b, src):
                for i in range(a, b):
                    ins = nc.vector.bn_stats(st[:, i, :], src[:, i, :])
                link(ins)
                for i in range(a, b):
                    ins = nc.vector.bn_aggr(mv[:, i, :], st[:, i, :])
                link(ins)

            def post_stats(g):
                a, b = PARTS[g]
                dve.wait_ge(gelu_done, g + 1)
                row_stats(a, b, VS[:, :, D:512])
                nc.vector.tensor_scalar(v_eps[:, a:b], mv[:, a:b, 1], EPS, None, ALU.add).then_inc(varg, 1)

            def post_norm(a, b):
                dve.wait_ge(mix_used, b)
                dve.wait_ge(rstdg, 1 if b <= PARTS[0][1] else 2)
                for i in range(a, b):
                    ins = nc.vector.scalar_tensor_tensor(out=hrow[:, i, :], in0=VS[:, i, D:512], scalar=mv[:, i, 0:1],
                                                         in1=gamma, op0=ALU.subtract, op1=ALU.mult)
                link(ins)
                for i in range(a, b):
                    ins = nc.vector.scalar_tensor_tensor(out=x1[:, i, :], in0=hrow[:, i, :], scalar=rstd[:, i:i + 1],
                                                         in1=x1[:, i, :], op0=ALU.mult, op1=ALU.add)
                link(ins)
                row_stats(a, b, x1)
                nc.vector.tensor_scalar(v_eps[:, a:b], mv[:, a:b, 1], EPS, None, ALU.add)
                ins = nc.vector.tensor_scalar(v_eps[:, NT + a:NT + b], mv[:, a:b, 1], 1.0 + EPS_RMS, EPS * EPS_RMS,
                                              ALU.mult, ALU.add)
                if b in (PARTS[0][1], PARTS[1][1]):
                    ins.then_inc(var2, 1)

            def post_rows(g):
                dve.wait_ge(r2, g + 1)
                for i in range(*PARTS[g]):
                    nc.vector.tensor_scalar(hrow[:, i, :], x1[:, i, :], mv[:, i, 0:1], rstd[:, NT + i:NT + i + 1],
                                            ALU.subtract, ALU.mult).then_inc(h_done, 1)

            def post_residual(g):
                for i in range(*PARTS[g]):
                    nc.vector.tensor_scalar(xn[:, i, :], x1[:, i, :], mv[:, i, 0:1], rstd[:, i:i + 1], ALU.subtract,
                                            ALU.mult)

            for n in range(20):
                i = n // 4
                dve.wait_ge(S_ps, n + 1)
                dve.wait_ge(mask_done, i + 1)
                if n >= 3:
                    dve.wait_ge(AT_ps, n - 2)
                nc.vector.tensor_tensor_reduce(out=E[:, n % 3, :], in0=flat(2 - 2 * (n % 2))[0:TP, 0:N],
                                               in1=edge_mask[:, i, :], scale=1.0, scalar=3e38, op0=ALU.add, op1=ALU.min,
                                               accum_out=mn[:, n:n + 1]).then_inc(S_used, 1)
                if n:
                    gnn_weigh(n - 1)
                if n == 3:
                    mix_dbd()
                if n in MIX_OUT:
                    mix_add(MIX_OUT.index(n))
                if n % 4 == 2 and n > 4:
                    gnn_out(i - 1)
                if n == 16:
                    post_stats(0)
                if n == 17:
                    post_norm(0, 1)
            gnn_weigh(19)
            post_norm(1, PARTS[0][1])
            gnn_out(NT - 1)
            post_rows(0)
            post_stats(1)
            post_residual(0)
            post_norm(*PARTS[1])
            dve.wait_ge(ld_const, 32)
            rot = rt[:, 64:64 + 768].rearrange("p (k n) -> p k n", k=2)

            def rotate(i):
                dve.wait_ge(qkv_ps, i + 1)
                qk = ps[0:TP, QKV_BANK[i], 0:384].rearrange("p (h s c) -> p h s c", h=6, s=2)
                rb = rot[:, 1, :].rearrange("p (h s c) -> p h s c", h=6, s=2)
                cos = rope[:, 0, i, :].unsqueeze(1).to_broadcast([TP, 6, C])
                sin = rope[:, 1, i, :].rearrange("p (s c) -> p s c", s=2)
                nc.vector.tensor_tensor(rot[:, 0, :].rearrange("p (h c) -> p h c", h=6),
                                        ps[0:TP, QKV_BANK[i], 0:384].rearrange("p (h c) -> p h c", h=6), cos, ALU.mult)
                for a in range(2):
                    ins = nc.vector.tensor_tensor(rb[:, :, a, :], qk[:, :, 1 - a, :],
                                                  sin[:, a:a + 1, :].to_broadcast([TP, 6, 32]), ALU.mult)
                ins.then_inc(qkv_used, 1)
                dve.wait_ge(qkv_used, i + 1)
                if i:
                    dve.wait_ge(qkT_ps, i)
                nc.vector.tensor_tensor(qkr, rot[:, 0, :], rot[:, 1, :], ALU.add).then_inc(qkr_done, 1)
                dve.wait_ge(qkr_done, i + 1)

            rotate(0)
            post_rows(1)
            for i in range(1, NT):
                rotate(i)
            post_residual(1)

            def ffn_y(i):
                dve.wait_ge(exp2_done, 4 * i + 4)
                link(nc.vector.reciprocal(rd[:, :], den2[:, 4 * i:4 * i + 4]))
                dve.wait_ge(AV2_done, 4 * i + 4)
                nc.vector.tensor_tensor(yat[:, i % 2, :].rearrange("p (h c) -> p h c", c=C),
                                        ps[0:TP, 6, 0:256].rearrange("p (h c) -> p h c", c=C),
                                        rd[:, :].unsqueeze(2).to_broadcast([TP, H, C]), ALU.mult).then_inc(y_done, 1)
                dve.wait_ge(y_done, i + 1)
                dve.sem_inc(O2_used, 1)

            def ffn_x2(i):
                dve.wait_ge(wo_ps, i + 1)
                nc.vector.tensor_tensor(xn[:, i, :], ps[0:TP, 7, 256:512], xn[:, i, :], ALU.add).then_inc(x2_done, 1)
                dve.wait_ge(x2_done, i + 1)
                link(nc.vector.tensor_tensor_reduce(out=rt[:, 400:656], in0=xn[:, i, :], in1=xn[:, i, :], scale=1.0 / D,
                                                    scalar=0.0, op0=ALU.mult, op1=ALU.add, accum_out=rt[:, 30 + i:31 + i]))
                nc.vector.tensor_scalar(v_eps[:, i:i + 1], rt[:, 30 + i:31 + i], EPS_RMS, None, ALU.add).then_inc(ms3, 1)

            def flat_rows(i):
                if i >= 2:
                    dve.wait_ge(scattered[i % 2], 32 * (i // 2))
                dve.wait_ge(r3, i + 1)
                for k in range(2):
                    ins = nc.vector.scalar_tensor_tensor(out=rowbuf[:, i % 2, k, 0:D], in0=xn[:, i, :],
                                                         scalar=rstd[:, i:i + 1], in1=ln2, op0=ALU.mult, op1=ALU.mult)
                    if k == 0:
                        ins.then_inc(flat_done, 1)
                nc.vector.tensor_copy(rowbuf[:, i % 2, :, D + 1:D + 2],
                                      ids[:, i:i + 1].unsqueeze(1).to_broadcast([TP, 2, 1]))

            def top2(i):
                dve.wait_ge(logit_ps, i + 1)
                nc.vector.tensor_copy(R(i, 0, 8), ps[0:TP, LG_BANK[i], 256:256 + NE]).then_inc(logits_read, 1)
                dve.wait_ge(logits_read, i + 1)
                link(nc.vector.max(out=R(i, 8, 8), in_=R(i, 0, 8)))
                nc.vector.tensor_scalar(R(i, 52, 1), R(i, 8, 1), -1.0, None, ALU.mult).then_inc(rmax_done, 1)
                link(nc.vector.max_index(out=rti[:, 8 * i:8 * i + 8], in_max=R(i, 8, 8), in_values=R(i, 0, 8)))
                link(nc.vector.tensor_copy(R(i, 24, 2), rti[:, 8 * i:8 * i + 2]))
                oh = R(i, 32, 16).rearrange("p (k e) -> p k e", k=2)
                link(nc.vector.tensor_tensor(oh, iota8.unsqueeze(1).to_broadcast([TP, 2, NE]),
                                             R(i, 24, 2).unsqueeze(2).to_broadcast([TP, 2, NE]), ALU.is_equal))
                nc.vector.tensor_tensor(sel_of(i), oh[:, 0, :], oh[:, 1, :], ALU.add).then_inc(sel_done, 1)

            def weights(i):
                dve.wait_ge(rexp_done, i + 1)
                link(nc.vector.scalar_tensor_tensor(out=R(i, 26, 1), in0=R(i, 53, 1), scalar=1e-9, in1=R(i, 17, 1),
                                                    op0=ALU.mult, op1=ALU.add))
                link(nc.vector.tensor_scalar(R(i, 26, 1), R(i, 26, 1), 1.0, None, ALU.add))
                link(nc.vector.reciprocal(R(i, 27, 1), R(i, 26, 1)))
                nc.vector.tensor_copy(rowbuf[:, i % 2, 0, D:D + 1], R(i, 27, 1))
                nc.vector.tensor_tensor(rowbuf[:, i % 2, 1, D:D + 1], R(i, 27, 1), R(i, 17, 1),
                                        ALU.mult).then_inc(weights_done, 1)

            def slots(i):
                dve.wait_ge(rank_ps, i + 1)
                oh = R(i, 32, 16).rearrange("p (k e) -> p k e", k=2)
                nc.vector.tensor_tensor(R(i, 54, 8), ps[0:TP, LG_BANK[i], 272:272 + NE], region, ALU.add).then_inc(rank_used, 1)
                dve.wait_ge(rank_used, i + 1)
                link(nc.vector.tensor_tensor(oh, oh, R(i, 54, 8).unsqueeze(1).to_broadcast([TP, 2, NE]), ALU.mult))
                link(nc.vector.tensor_reduce(R(i, 28, 2), oh, AX.X, ALU.add))
                nc.vector.tensor_copy(rti[:, 40 + 2 * i:42 + 2 * i], R(i, 28, 2)).then_inc(slot_done, 1)

            for n in range(20):
                i = n // 4
                dve.wait_ge(S2_ps, n + 1)
                nc.vector.tensor_reduce(mn2[:, n:n + 1], flat(2 * (n % 2))[0:TP, 0:TP * (i + 1)], AX.X, ALU.max,
                                        negate=True).then_inc(max2_done, 1)
                if n % 4 == 2 and n >= 6:
                    ffn_y(i - 1)
                if n % 4 == 0 and n >= 8:
                    ffn_x2(i - 2)
                if n % 4 == 1 and n >= 9:
                    flat_rows(i - 2)
                if n % 4 == 3 and n >= 11 and n < 19:
                    top2(i - 2)
                if n % 4 == 1 and n >= 13:
                    slots(i - 3)
                if n % 4 == 2 and n >= 14:
                    weights(i - 3)
            top2(2)
            ffn_x2(3)
            slots(2)
            ffn_y(4)
            weights(2)
            flat_rows(3)
            ffn_x2(4)
            top2(3)
            flat_rows(4)
            slots(3)
            weights(3)
            top2(4)
            weights(4)
            slots(4)
            dve.wait_ge(total_ps, 1)
            tot = ps[0:1, LG_BANK[NT - 2], 288:288 + NE]
            blks, upto = rr[:, 700:708], rr[:, 708:716]
            link(nc.vector.tensor_tensor(rr[:, 640:680].rearrange("p (e k) -> p e k", e=NE),
                                         tot.unsqueeze(2).to_broadcast([1, NE, 5]),
                                         thr[0:1, :].unsqueeze(1).to_broadcast([1, NE, 5]), ALU.is_gt))
            link(nc.vector.tensor_reduce(blks, rr[:, 640:680].rearrange("p (e k) -> p e k", e=NE), AX.X, ALU.add))
            link(nc.vector.tensor_tensor_scan(upto, cf[0:1, 160:168], blks, 0.0, ALU.mult, ALU.add))
            e_of = rr[:, 720:720 + NB * NE].rearrange("p (g e) -> p g e", g=NB)
            e_blk = rr[:, 0:NB * NE].rearrange("p (g e) -> p g e", g=NB)
            link(nc.vector.tensor_tensor(e_of, upto.unsqueeze(1).to_broadcast([1, NB, NE]),
                                         crow[:, 480:480 + NB].unsqueeze(2).to_broadcast([1, NB, NE]), ALU.is_le))
            nc.vector.tensor_tensor(rr[:, 600:608], upto[:, 7:8].to_broadcast([1, 8]), crow[:, 500:508], ALU.is_gt)
            link(nc.vector.tensor_tensor(e_blk, e_of, blks.unsqueeze(1).to_broadcast([1, NB, NE]), ALU.mult))
            nc.vector.tensor_reduce(rr[:, 200:200 + NB], e_of, AX.X, ALU.add)
            nc.vector.tensor_reduce(rr[:, 236:237], rr[:, 600:608], AX.X, ALU.add)
            link(nc.vector.tensor_reduce(rr[:, 240:240 + NB], e_blk, AX.X, ALU.add))
            link(nc.vector.tensor_tensor(rr[:, 240:240 + NB], crow[:, 480:480 + NB], rr[:, 240:240 + NB], ALU.subtract))
            link(nc.vector.tensor_scalar(rr[:, 240:240 + NB], rr[:, 240:240 + NB], 128.0, None, ALU.mult))
            link(nc.vector.scalar_tensor_tensor(out=rr[:, 218:218 + NB], in0=rr[:, 200:200 + NB], scalar=float(CAP),
                                                in1=rr[:, 240:240 + NB], op0=ALU.mult, op1=ALU.add))
            nc.vector.tensor_scalar(rr[:, 200:200 + NB], rr[:, 200:200 + NB], float(NE - 1), None, ALU.min)
            link(nc.vector.tensor_scalar(rr[:, 218:218 + NB], rr[:, 218:218 + NB], float(NE * CAP), None, ALU.min))
            nc.vector.tensor_copy(blki[:, 0:2 * NB + 1], rr[:, 200:201 + 2 * NB]).then_inc(blk_done, 1)
            dve.wait_ge(blk_done, 1)

            def gate(s, u, j):
                dve.wait_ge(silu_done, 2 * s + j + 1)
                nc.vector.tensor_tensor(gb[:, u, j, :], ps[:, 2 * j + 1, 0:HH], sl[:, j, :], ALU.mult).then_inc(g_done, 1)

            iters = dve.value_load(blki[0:1, 2 * NB:2 * NB + 1], min_val=1, max_val=(MAXB - 1) // 2)
            dve.sem_inc(y_copied, 1)
            dve.sem_inc(y_free, 2)

            def y_copy(s, u):
                dve.wait_ge(y_ps, s + 1)
                dve.wait_ge(y_free, s + 1)
                nc.vector.tensor_scalar(yb[:, u, :], ps[:, 6, 0:D], slot_w[:, u:u + 1], None,
                                        ALU.mult).then_inc(y_copied, 1)

            def meta(u, s):
                dve.wait_ge(y_free, s + 1)
                dve.wait_ge(xblk_ld[u], s // 2 * 16 + 16 if isinstance(s, int) else 16 * m + 16 + 16 * (1 - u))
                nc.vector.tensor_copy(slot_w[:, u:u + 1], xblk[:, u, D:D + 1])
                nc.vector.tensor_copy(slot_id[:, u:u + 1], xblk[:, u, D + 1:D + 2]).then_inc(meta_done, 1)

            meta(0, 0)
            gate(0, 0, 0)
            gate(0, 0, 1)
            with dve.Fori(0, iters) as m:
                for u, s in ((1, 2 * m + 1), (0, 2 * m + 2)):
                    gate(s, u, 0)
                    gate(s, u, 1)
                    meta(u, s)
                    y_copy(s - 1, 1 - u)
            y_copy(2 * iters, 0)


def laid_out(a):
    def cols(w):
        n, k = w.shape
        return w.T.reshape(k // 128, 128, n).transpose(1, 0, 2)

    def krows(w):
        k, n = w.shape
        return w.reshape(k // 128, 128, n).transpose(1, 0, 2)

    g = "L0_gnn_"
    f = "L0_ffn_"
    src, dst = a["src"], a["dst"]
    wq = a[f + "wq"].reshape(H, C, D)[[0, 2, 1, 3]].reshape(D, D)
    mix = a["L0_mix_w_qkv"]
    w13 = np.concatenate([a[f + "w1"], a[f + "w3"]], axis=1)
    ident = np.eye(128, dtype=np.float32)
    c_f32 = np.zeros((128, 288), np.float32)
    c_f32[:, 0:128] = ident
    c_f32[:, 128:136] = np.arange(8)
    c_f32[:, 136:141] = np.arange(5) * 128
    c_f32[:, 141:146] = np.arange(128)[:, None] + TP * np.arange(NT)
    c_f32[:, 146:154] = CAP * np.arange(NE)
    c_f32[:, 160:168] = 1.0
    c_pad = np.zeros((128, RW), np.float32)
    c_pad[:, D + 1] = N + np.arange(128)
    bf = mybir.dt.np(bf16)
    r = np.arange(128)
    c_bf = np.zeros((128, 512), np.float32)
    c_bf[:, 0:128] = r[:, None] < r[None, :]
    c_bf[:, 128:256] = 1.0
    c_bf[:, 256:384] = ident
    c_bf[:, 384:512] = np.where(r[None, :] > r[:, None], -BIG, 0.0)
    inv_freq = 1.0 / 10000.0 ** (np.arange(0, C, 2, dtype=np.float32) / C)
    freqs = np.outer(np.arange(N, dtype=np.float32), inv_freq)
    cos, sin = np.cos(freqs), np.sin(freqs)
    c_rope = np.stack([np.concatenate([cos, cos], 1), np.concatenate([-sin, sin], 1)])
    c_row = np.zeros((1, 512), np.float32)
    b = np.arange(NT)
    c_row[0, 0:NT * NG] = np.repeat(TP * b, NG)
    c_row[0, 200:200 + NT * NG] = np.repeat(TP * b + TP - 1, NG)
    c_row[0, 400:400 + NG] = np.arange(NG) + 1
    c_row[0, 440:440 + NG] = NG - np.arange(NG)
    c_row[0, 480:480 + NB] = np.arange(NB)
    c_row[0, 500:508] = 2 * np.arange(8) + 1
    return dict(
        x_in=a["x"],
        edge_groups=dst.reshape(NG, EG * TP),
        edge_src=src.reshape(ET, TP).T,
        edge_dst=dst.reshape(ET, TP).T,
        w_gnn=krows(np.concatenate([a[g + "Wq"], a[g + "Wk"], a[g + "Wv"], a[g + "Wskip"]], axis=1)),
        b_gnn_qk=np.concatenate([a[g + "bq"], a[g + "bk"]]).reshape(4, 128).T,
        b_gnn_vs=np.concatenate([a[g + "bv"], a[g + "bskip"]]),
        w_mix_kv=cols(mix[MI:3 * MI]),
        w_mix_q=mix[0:MI].reshape(4, 128, D).transpose(1, 0, 2),
        w_mix_out=cols(a["L0_mix_w_out"]),
        rows=np.stack([a[g + "gamma"], a[g + "beta_ln"], a["L0_mix_b_out"], a[f + "ln2_w"]]),
        w_ffn_qkv=cols(np.concatenate([wq, a[f + "wk"], a[f + "wv"]])),
        w_ffn_o=cols(a[f + "wo"]),
        ln1_col=a[f + "ln1_w"].reshape(KC, 128).T,
        w_router=cols(a[f + "router_w"]),
        w13=w13.transpose(0, 2, 1).reshape(NE, KC, 128, 2 * HID).transpose(2, 0, 1, 3),
        w2=a[f + "w2"].transpose(0, 2, 1),
        c_f32=c_f32,
        c_bf16=c_bf.astype(bf),
        c_iota=np.arange(N).astype(np.float16),
        c_rope=c_rope.reshape(2, NT, TP, C).transpose(2, 0, 1, 3).astype(np.float32),
        c_row=c_row,
        c_pad=c_pad,
    )


def kernel(**inputs):
    import concourse.bacc as _bacc
    from concourse.bass_utils import run_bass_kernel_spmd as _run

    nc = _bacc.Bacc("TRN2", target_bir_lowering=False, num_devices=1)
    arrays = {k: np.ascontiguousarray(v) for k, v in laid_out({k: np.asarray(v) for k, v in inputs.items()}).items()}
    args = [nc.dram_tensor(k, v.shape, mybir.dt.from_np(v.dtype), kind="ExternalInput").ap() for k, v in arrays.items()]
    args.append(nc.dram_tensor("out", (N, D), fp32, kind="ExternalOutput").ap())
    build(nc, *args)
    r = _run(nc, [arrays], core_ids=[0])
    return r.results[0]["out"]
```
